# Optimizing a Trainium2 kernel written in Bass

```python
import numpy as np
import jax
import jax.numpy as jnp

def _softmax(x, axis=-1):
    return jax.nn.softmax(x, axis=axis)

def _gelu(x):
    return jax.nn.gelu(x, approximate=True)

def _silu(x):
    return jax.nn.silu(x)

def _sigmoid(x):
    return jax.nn.sigmoid(x)

def _layernorm(x, axis=-1, eps=1e-05):
    m = jnp.mean(x, axis=axis, keepdims=True)
    v = jnp.var(x, axis=axis, keepdims=True)
    return (x - m) / jnp.sqrt(v + eps)

def _scatter_add(tgt, idx, src, axis=0):
    return tgt.at[idx].add(src)

def _segment_sum(src, seg, n):
    return jax.ops.segment_sum(src, seg, n)
kernel_name = 'mk_decoder_preln_d1_seqx_r4_aaf2dd'

def setup_inputs(seed: int=0):
    np.random.seed(seed)
    _w = jnp.asarray

    def _rec_inputs():
        import jax
        import jax.numpy as jnp
        _rk = jax.random.key(seed)
        x = -0.0003929 + 0.9999 * jax.random.normal(jax.random.fold_in(_rk, 1), (4, 512, 512), jnp.float32)
        _lenS = 512 - jax.random.randint(jax.random.fold_in(_rk, 7), (4,), 0, max(1, 512 // 4) + 1, jnp.int32)
        _lenS2 = 512 - jax.random.randint(jax.random.fold_in(_rk, 8), (4,), 0, max(1, 512 // 4) + 1, jnp.int32)
        _ctx_2048P = jax.random.normal(jax.random.fold_in(_rk, 11), (4, 16, 512), jnp.float32)
        _ctx_2048c = jax.random.dirichlet(jax.random.fold_in(_rk, 511), 0.3 * jnp.ones((16,), jnp.float32), (4, 512))
        _ctx_2048t = jnp.einsum('bsk,bkd->bsd', _ctx_2048c, _ctx_2048P)
        _ctx_2048t = _ctx_2048t * jax.lax.rsqrt(jnp.mean(jnp.square(_ctx_2048t)) + 1e-12) * 0.953939
        ctx_2048 = -0.000514642 + 1.00011 * (_ctx_2048t + 0.3 * jax.random.normal(jax.random.fold_in(_rk, 611), (4, 512, 512), jnp.float32))
        return (x, ctx_2048)
    x, ctx_2048 = _rec_inputs()

    def _L0_attn_setup():
        import jax, jax.numpy as jnp
        import numpy as np
        EMBED_DIM = 512
        NUM_HEADS = 16
        HEAD_DIM = EMBED_DIM // NUM_HEADS
        WINDOW = 128
        THETA = 10000.0

        def _rope_cos_sin(seq_len, dim, dtype):
            inv_freq = 1.0 / THETA ** (jnp.arange(0, dim, 2, dtype=jnp.float32) / dim)
            t = jnp.arange(seq_len, dtype=jnp.float32)
            angles = t[:, None] * inv_freq[None, :]
            angles = jnp.repeat(angles, 2, axis=-1)
            return (jnp.cos(angles).astype(dtype), jnp.sin(angles).astype(dtype))

        def _rotate_half(x):
            x2 = x.reshape(*x.shape[:-1], x.shape[-1] // 2, 2)
            rot = jnp.stack([-x2[..., 1], x2[..., 0]], axis=-1)
            return rot.reshape(x.shape)
        key = jax.random.key(seed)
        k1, k2, k3, k4 = jax.random.split(key, 4)
        x = jax.random.normal(k1, (2, 512, EMBED_DIM), dtype=jnp.float32)
        scale = 1.0 / np.sqrt(EMBED_DIM)
        W_qkv = jax.random.normal(k2, (EMBED_DIM, 3 * EMBED_DIM), dtype=jnp.float32) * scale
        W_out = jax.random.normal(k3, (EMBED_DIM, EMBED_DIM), dtype=jnp.float32) * scale
        b_out = jax.random.normal(k4, (EMBED_DIM,), dtype=jnp.float32) * 0.01
        return {'x': x, 'W_qkv': W_qkv, 'W_out': W_out, 'b_out': b_out}
    _L0_attn_all = _L0_attn_setup()
    _L0_attn_in = {k: v for k, v in _L0_attn_all.items() if k in ('W_qkv', 'W_out', 'b_out')}
    del _L0_attn_all

    def _L0_xattn_setup():
        import jax, jax.numpy as jnp
        import numpy as np
        DIM = 512
        NHEADS = 32
        HEAD_DIM = DIM // NHEADS
        EPS = 1e-06

        def _rmsnorm(t):
            return t * jax.lax.rsqrt(jnp.mean(t * t, axis=-1, keepdims=True) + EPS)
        key = jax.random.key(seed)
        kx, kc, kq, kk, kv = jax.random.split(key, 5)
        x = jax.random.normal(kx, (2, 1024, DIM), dtype=jnp.float32)
        context = jax.random.normal(kc, (2, 128, DIM), dtype=jnp.float32)
        std = 0.02
        Wq = jax.random.normal(kq, (DIM, DIM), dtype=jnp.float32) * std
        Wk = jax.random.normal(kk, (DIM, DIM), dtype=jnp.float32) * std
        Wv = jax.random.normal(kv, (DIM, DIM), dtype=jnp.float32) * std
        return {'x': x, 'context': context, 'Wq': Wq, 'Wk': Wk, 'Wv': Wv}
    _L0_xattn_all = _L0_xattn_setup()
    _L0_xattn_in = {k: v for k, v in _L0_xattn_all.items() if k in ('Wq', 'Wk', 'Wv')}
    del _L0_xattn_all

    def _L0_ffn_setup():
        import jax, jax.numpy as jnp
        import numpy as np
        B, S, D = (2, 512, 512)
        E, I, TOPK = (64, 192, 8)
        M = B * S
        CAP = 2 * (M * TOPK) // E

        def _moe(x, router_weight, gate_proj, up_proj, down_proj):
            b, s, d = x.shape
            xf = x.reshape(-1, d)
            m = xf.shape[0]
            logits = xf @ router_weight
            probs = jax.nn.softmax(logits.astype(jnp.float32), axis=-1)
            topw, topi = jax.lax.top_k(probs, TOPK)
            topw = topw / topw.sum(axis=-1, keepdims=True)
            flat_e = topi.reshape(-1)
            flat_w = topw.reshape(-1).astype(x.dtype)
            order = jnp.argsort(flat_e)
            se = flat_e[order]
            tok = order // TOPK
            counts = jax.ops.segment_sum(jnp.ones_like(flat_e), flat_e, num_segments=E)
            starts = jnp.cumsum(counts) - counts
            pos = jnp.arange(m * TOPK) - starts[se]
            valid = pos < CAP
            posc = jnp.minimum(pos, CAP - 1)
            xe = jnp.zeros((E, CAP, d), x.dtype).at[se, pos].set(xf[tok], mode='drop')
            h = jax.nn.silu(jnp.einsum('ecd,edi->eci', xe, gate_proj)) * jnp.einsum('ecd,edi->eci', xe, up_proj)
            ye = jnp.einsum('eci,eid->ecd', h, down_proj)
            contrib = jnp.where(valid[:, None], ye[se, posc], 0.0) * flat_w[order][:, None]
            out = jnp.zeros((m, d), x.dtype).at[tok].add(contrib)
            return out.reshape(b, s, d)
        key = jax.random.key(seed)
        k0, k1, k2, k3, k4 = jax.random.split(key, 5)
        return {'x': jax.random.normal(k0, (B, S, D), jnp.float32), 'router_weight': jax.random.normal(k1, (D, E), jnp.float32) * 0.02, 'gate_proj': jax.random.normal(k2, (E, D, I), jnp.float32) * 0.02, 'up_proj': jax.random.normal(k3, (E, D, I), jnp.float32) * 0.02, 'down_proj': jax.random.normal(k4, (E, I, D), jnp.float32) * 0.02}
    _L0_ffn_all = _L0_ffn_setup()
    _L0_ffn_in = {k: v for k, v in _L0_ffn_all.items() if k in ('router_weight', 'gate_proj', 'up_proj', 'down_proj')}
    del _L0_ffn_all
    return {'x': x, 'ctx_2048': ctx_2048, 'L0_attn_W_qkv': _L0_attn_in['W_qkv'], 'L0_attn_W_out': _L0_attn_in['W_out'], 'L0_attn_b_out': _L0_attn_in['b_out'], 'L0_xattn_Wq': _L0_xattn_in['Wq'], 'L0_xattn_Wk': _L0_xattn_in['Wk'], 'L0_xattn_Wv': _L0_xattn_in['Wv'], 'L0_ffn_router_weight': _L0_ffn_in['router_weight'], 'L0_ffn_gate_proj': _L0_ffn_in['gate_proj'], 'L0_ffn_up_proj': _L0_ffn_in['up_proj'], 'L0_ffn_down_proj': _L0_ffn_in['down_proj']}

def reference(x, ctx_2048, L0_attn_W_qkv, L0_attn_W_out, L0_attn_b_out, L0_xattn_Wq, L0_xattn_Wk, L0_xattn_Wv, L0_ffn_router_weight, L0_ffn_gate_proj, L0_ffn_up_proj, L0_ffn_down_proj):
    import jax
    import jax.numpy as jnp

    def _L0_attn_ref(x, W_qkv, W_out, b_out):
        import jax, jax.numpy as jnp
        import numpy as np
        EMBED_DIM = 512
        NUM_HEADS = 16
        HEAD_DIM = EMBED_DIM // NUM_HEADS
        WINDOW = 128
        THETA = 10000.0

        def _rope_cos_sin(seq_len, dim, dtype):
            inv_freq = 1.0 / THETA ** (jnp.arange(0, dim, 2, dtype=jnp.float32) / dim)
            t = jnp.arange(seq_len, dtype=jnp.float32)
            angles = t[:, None] * inv_freq[None, :]
            angles = jnp.repeat(angles, 2, axis=-1)
            return (jnp.cos(angles).astype(dtype), jnp.sin(angles).astype(dtype))

        def _rotate_half(x):
            x2 = x.reshape(*x.shape[:-1], x.shape[-1] // 2, 2)
            rot = jnp.stack([-x2[..., 1], x2[..., 0]], axis=-1)
            return rot.reshape(x.shape)
        b, l, e = x.shape
        qkv = jnp.einsum('ble,ef->blf', x, W_qkv)
        qkv = qkv.reshape(b, l, NUM_HEADS, HEAD_DIM, 3)
        qkv = jnp.moveaxis(qkv, (4, 2), (0, 2))
        q, k, v = (qkv[0], qkv[1], qkv[2])
        cos, sin = _rope_cos_sin(l, HEAD_DIM, x.dtype)
        q = q * cos + _rotate_half(q) * sin
        k = k * cos + _rotate_half(k) * sin
        i = jnp.arange(l)[:, None]
        j = jnp.arange(l)[None, :]
        mask = (j <= i) & (j >= i - WINDOW)
        scale = 1.0 / np.sqrt(HEAD_DIM)
        scores = jnp.einsum('bhid,bhjd->bhij', q, k) * scale
        scores = jnp.where(mask, scores, jnp.finfo(scores.dtype).min)
        attn = jax.nn.softmax(scores, axis=-1)
        out = jnp.einsum('bhij,bhjd->bhid', attn, v)
        out = jnp.moveaxis(out, 1, 2).reshape(b, l, e)
        return jnp.einsum('ble,ef->blf', out, W_out) + b_out

    def _L0_xattn_ref(x, context, Wq, Wk, Wv):
        import jax, jax.numpy as jnp
        import numpy as np
        DIM = 512
        NHEADS = 32
        HEAD_DIM = DIM // NHEADS
        EPS = 1e-06

        def _rmsnorm(t):
            return t * jax.lax.rsqrt(jnp.mean(t * t, axis=-1, keepdims=True) + EPS)
        b, n, _ = x.shape
        m = context.shape[1]
        q = x @ Wq.T
        k_raw = context @ Wk.T
        v_raw = context @ Wv.T
        q = q.reshape(b, n, NHEADS, HEAD_DIM).transpose(0, 2, 1, 3)
        kv = jnp.concatenate([k_raw, v_raw], axis=-1)
        kv = kv.reshape(b, m, NHEADS, HEAD_DIM, 2)
        k = kv[..., 0].transpose(0, 2, 1, 3)
        v = kv[..., 1].transpose(0, 2, 1, 3)
        q = _rmsnorm(q)
        k = _rmsnorm(k)
        scale = HEAD_DIM ** (-0.5)
        scores = jnp.einsum('bhnd,bhmd->bhnm', q, k) * scale
        attn = jax.nn.softmax(scores, axis=-1)
        out = jnp.einsum('bhnm,bhmd->bhnd', attn, v)
        return out.transpose(0, 2, 1, 3).reshape(b, n, NHEADS * HEAD_DIM)

    def _L0_ffn_ref(x, router_weight, gate_proj, up_proj, down_proj):
        import jax, jax.numpy as jnp
        import numpy as np
        B, S, D = (2, 512, 512)
        E, I, TOPK = (64, 192, 8)
        M = B * S
        CAP = 2 * (M * TOPK) // E

        def _moe(x, router_weight, gate_proj, up_proj, down_proj):
            b, s, d = x.shape
            xf = x.reshape(-1, d)
            m = xf.shape[0]
            logits = xf @ router_weight
            probs = jax.nn.softmax(logits.astype(jnp.float32), axis=-1)
            topw, topi = jax.lax.top_k(probs, TOPK)
            topw = topw / topw.sum(axis=-1, keepdims=True)
            flat_e = topi.reshape(-1)
            flat_w = topw.reshape(-1).astype(x.dtype)
            order = jnp.argsort(flat_e)
            se = flat_e[order]
            tok = order // TOPK
            counts = jax.ops.segment_sum(jnp.ones_like(flat_e), flat_e, num_segments=E)
            starts = jnp.cumsum(counts) - counts
            pos = jnp.arange(m * TOPK) - starts[se]
            valid = pos < CAP
            posc = jnp.minimum(pos, CAP - 1)
            xe = jnp.zeros((E, CAP, d), x.dtype).at[se, pos].set(xf[tok], mode='drop')
            h = jax.nn.silu(jnp.einsum('ecd,edi->eci', xe, gate_proj)) * jnp.einsum('ecd,edi->eci', xe, up_proj)
            ye = jnp.einsum('eci,eid->ecd', h, down_proj)
            contrib = jnp.where(valid[:, None], ye[se, posc], 0.0) * flat_w[order][:, None]
            out = jnp.zeros((m, d), x.dtype).at[tok].add(contrib)
            return out.reshape(b, s, d)
        return _moe(x, router_weight, gate_proj, up_proj, down_proj)
    x = x + _L0_attn_ref(_layernorm(x, axis=-1), L0_attn_W_qkv, L0_attn_W_out, L0_attn_b_out)
    x = x + _L0_xattn_ref(_layernorm(x, axis=-1), ctx_2048, L0_xattn_Wq, L0_xattn_Wk, L0_xattn_Wv)
    x = x + _L0_ffn_ref(_layernorm(x, axis=-1), L0_ffn_router_weight, L0_ffn_gate_proj, L0_ffn_up_proj, L0_ffn_down_proj)
    return x

_drawn_inputs = setup_inputs


def setup_inputs(seed=0):
    import zlib

    import numpy as np

    out = dict(_drawn_inputs(seed))
    spreads = {}
    factors = {'L0_attn_b_out': 6.238,
     'L0_ffn_router_weight': 6.001,
     'L0_ffn_gate_proj': 5.774,
     'L0_ffn_up_proj': 5.661,
     'L0_ffn_down_proj': 5.655}
    for name, (base, spread) in spreads.items():
        noise = np.random.default_rng([zlib.crc32(name.encode()), seed]).standard_normal(out[name].shape)
        drawn = base * np.exp(spread * noise) if base else spread * noise
        out[name] = jnp.asarray(drawn.astype(out[name].dtype))
    for name, factor in factors.items():
        out[name] = (out[name] * factor).astype(out[name].dtype)
    return out
```

```python
from contextlib import ExitStack

import concourse.bass as bass
from concourse import mybir

F32 = mybir.dt.float32
F32R = mybir.dt.float32r
BF16 = mybir.dt.bfloat16
I32 = mybir.dt.int32
U32 = mybir.dt.uint32
ALU = mybir.AluOpType
ACT = mybir.ActivationFunctionType
AX = mybir.AxisListType

P = 128
B, S, D = 4, 512, 512
T = S // P
NT = B * T
C = D // P
H1, D1 = 16, 32
H2, D2 = 32, 16
E, I, TOPK = 64, 192, 8
CAP = 256
CT = CAP // P
LN_EPS, RMS_EPS = 1e-5, 1e-6
MASKED = -1e30

START = 1

K_IDENT, K_TRI, K_MASK, K_ROPE = 0, 128, 256, 256 + 3 * 256
K_IOTA = K_ROPE + 4 * T * D1
K_TOK = K_IOTA + E
K_COLS = K_TOK + NT


class Phase:

    def __init__(self, nc, ctx, tag):
        self.nc, self.ctx, self.tag, self.sems = nc, ctx, tag, []

    def sb(self, name, shape, dt=F32):
        return self.ctx.enter_context(self.nc.sbuf_tensor(f"{self.tag}_{name}", shape, dt))

    def ps(self, name, shape, dt=F32):
        return self.ctx.enter_context(self.nc.psum_tensor(f"{self.tag}_{name}", shape, dt))

    def sem(self, name):
        self.sems.append(self.ctx.enter_context(self.nc.semaphore(f"{self.tag}_{name}")))
        return self.sems[-1]

    def main_block(self):
        self.ctx.callback(self.clear)
        return self.ctx.enter_context(self.nc.Block())

    def clear(self):
        with self.nc.Block() as block:
            @block.sync
            def _(sp):
                for s in self.sems:
                    sp.sem_clear(s)


def product(pe, out, hi_l, lo_l, hi_r, lo_r, chunks, stop=True):
    for c in range(chunks):
        pe.matmul(out, hi_l(c), hi_r(c), start=(c == 0), stop=False)
        pe.matmul(out, hi_l(c), lo_r(c), start=False, stop=False)
        last = pe.matmul(out, lo_l(c), hi_r(c), start=False, stop=(stop and c == chunks - 1))
    return last


def self_attention(nc, consts, x, w_qkv, w_out, b_out, x1):
    with ExitStack() as ctx:
        m = Phase(nc, ctx, "sa")
        ident = m.sb("ident", [P, P])
        identb = m.sb("identb", [P, P], BF16)
        maskf = m.sb("maskf", [P, 3, 2 * P])
        mask = m.sb("mask", [P, 3, 2 * P], BF16)
        rope = m.sb("rope", [P, 4, T, D1])
        bias = m.sb("bias", [P, D])
        wh = m.sb("wh", [P, C, 3, D], F32R)
        wl = m.sb("wl", [P, C, 3, D], F32R)
        oh = m.sb("oh", [P, C, D], F32R)
        ol = m.sb("ol", [P, C, D], F32R)
        raw = m.sb("raw", [P, 2, 3 * D])

        ld_x = [m.sem(f"ld_x{t}") for t in range(T)]
        st_x = [m.sem(f"st_x{t}") for t in range(T)]
        (init, s_gate, s_bst, s_mv, s_ve, s_rs, s_xn, s_xT, s_xh, s_xl, s_q, s_k, s_v, s_t, s_r, s_hi, s_lo, s_vv, s_trA, s_trD,
         s_evA, s_evD, s_mx, s_ri, s_pn, s_oh, s_ol, s_op, s_x1, s_x1b) = [m.sem(n) for n in (
             "init gate bst mv ve rs xn xT xh xl q k v t r hi lo vv trA trD "
             "evA evD mx ri pn oh ol op x1 x1b").split()]
        s_sc = [m.sem(f"sc{i}") for i in range(2)]
        s_ex = [m.sem(f"ex{i}") for i in range(2)]
        s_pv = [m.sem(f"pv{i}") for i in range(2)]
        counters = [s_gate, s_bst, s_mv, s_ve, s_rs, s_xn, s_xT, s_xh, s_xl, s_q, s_k, s_v, s_t, s_r, s_hi, s_lo,
                    s_vv, s_trA, s_trD, s_evA, s_evD, s_mx, s_ri, s_pn, s_oh, s_ol, s_op, s_x1, s_x1b]
        counters += st_x + s_sc + s_ex + s_pv

        with ExitStack() as c2, nc.Block() as block:
            s = Phase(nc, c2, "sw")
            s_c, s_cb = s.sem("const"), s.sem("cast")
            s_w = [s.sem(f"raw{i}") for i in range(2)]
            w_hi, w_lo = s.sem("hi"), s.sem("lo")
            c2.callback(s.clear)

            @block.sync
            def _(sp):
                for counter in counters:
                    sp.sem_inc(counter, START)
                sp.dma_start(ident[:], consts[:, K_IDENT:K_IDENT + P]).then_inc(s_c, 16)
                sp.dma_start(maskf[:].rearrange("p a b -> p (a b)"), consts[:, K_MASK:K_MASK + 768]).then_inc(s_c, 16)
                sp.dma_start(rope[:].rearrange("p a b c -> p (a b c)"),
                             consts[:, K_ROPE:K_ROPE + 4 * T * D1]).then_inc(s_c, 16)
                sp.dma_start(bias[:], b_out.rearrange("(a n) -> a n", a=1).to_broadcast([P, D])).then_inc(s_c, 16)
                for c in range(2 * C):
                    if c >= 2:
                        sp.wait_ge(w_lo, c - 1)
                    if c < C:
                        sp.dma_start(raw[:, c % 2, :], w_qkv[c * P:(c + 1) * P, :]).then_inc(s_w[c % 2], 16)
                    else:
                        sp.dma_start(raw[:, c % 2, 0:D], w_out[(c - C) * P:(c - C + 1) * P, :]).then_inc(s_w[c % 2], 16)
                sp.wait_ge(s_c, 64)

            def parts(c):
                if c < C:
                    return raw[:, c % 2, :].rearrange("p (f t) -> p t f", t=3), wh[:, c], wl[:, c]
                return raw[:, c % 2, 0:D], oh[:, c - C], ol[:, c - C]

            @block.scalar
            def _(act):
                for c in range(2 * C):
                    src, hi, lo = parts(c)
                    act.wait_ge(s_w[c % 2], 16 * (c // 2 + 1))
                    act.activation(hi, src, ACT.Copy).then_inc(w_hi, 1)

            @block.vector
            def _(dve):
                dve.wait_ge(s_c, 64)
                dve.tensor_copy(identb[:], ident[:]).then_inc(s_cb, 1)
                dve.tensor_copy(mask[:], maskf[:]).then_inc(s_cb, 1)
                for c in range(2 * C):
                    src, hi, lo = parts(c)
                    dve.wait_ge(w_hi, c + 1)
                    dve.tensor_tensor(lo, src, hi.bitcast(F32), ALU.subtract).then_inc(w_lo, 1)

        xs = m.sb("x", [P, T, D])
        st6 = m.sb("st6", [P, T, 6])
        mv = m.sb("mv", [P, T, 2])
        ve = m.sb("ve", [P, T])
        half = m.sb("half", [P, 1])
        eps = m.sb("eps", [P, 1])
        gate = m.sb("gate", [P, 1])
        rstd = m.sb("rstd", [P, T])
        xn = m.sb("xn", [P, D])
        xh = m.sb("xh", [P, C, P], F32R)
        xl = m.sb("xl", [P, C, P], F32R)
        t1 = m.sb("t1", [P, 2, D])
        t2 = m.sb("t2", [P, 2, D])
        rot = m.sb("rot", [P, 2, D])
        stack = m.sb("stack", [P, 2, H1, 3 * D1], F32R)
        qT = m.sb("qT", [3 * D1, H1, P], F32R)
        kT = m.sb("kT", [3 * D1, H1, 2, P], F32R)
        v = m.sb("v", [P, T, H1, D1])
        prob = m.sb("prob", [P, H1, 2 * P])
        nmax = m.sb("nmax", [P, H1])
        rsum = m.sb("rsum", [P, H1])
        rinv = m.sb("rinv", [P, H1])
        pT = m.sb("pT", [P, 2, 2, 4, P])
        oTh = m.sb("oTh", [P, C, P], F32R)
        oTl = m.sb("oTl", [P, C, P], F32R)

        b0 = m.ps("b0", [P, C, P])
        bq = [m.ps(f"b{1 + i}", [P, D]) for i in range(3)]
        bt = [m.ps(f"b{4 + i}", [P, 4, P]) for i in range(2)]
        bs = [m.ps(f"b{6 + i}", [P, 2, 2 * P]) for i in range(2)]

        class Steps:

            def body(self, b):
                for step in (self.norm, self.q, self.k, self.v):
                    step(b, 0)
                for t in range(T):
                    ahead = t + 1 < T
                    if ahead:
                        self.norm(b, t + 1)
                    self.turn(b, t)
                    self.group(b, t, 0)
                    if ahead:
                        self.q(b, t + 1)
                    self.group(b, t, 1)
                    if ahead:
                        self.k(b, t + 1)
                    self.group(b, t, 2)
                    if ahead:
                        self.v(b, t + 1)
                    self.group(b, t, 3)
                    self.end(b, t)

            def norm(self, b, t): pass
            def q(self, b, t): pass
            def k(self, b, t): pass
            def v(self, b, t): pass
            def turn(self, b, t): pass
            def group(self, b, t, g): pass
            def end(self, b, t): pass

        def turned(gg, t):
            h = 4 * (gg % 4)
            return qT[:, h:h + 4, :] if gg < 4 else kT[:, h:h + 4, t % 2, :]

        block = m.main_block()

        @block.sync
        def _(sp):
            with sp.Fori(0, B) as b:
                for t in range(T):
                    sp.wait_ge(st_x[t], START + b * 16)
                    sp.dma_start(xs[:, t], x[bass.ds(b * T + t, 1), :, :].rearrange("a p d -> (a p) d")).then_inc(ld_x[t], 16)
                for t in range(T):
                    sp.wait_ge(s_x1b, START + b * T + t + 1)
                    sp.dma_start(x1[bass.ds(b * T + t, 1), :, :].rearrange("a p d -> (a p) d"), xs[:, t]).then_inc(st_x[t], 16)
            for t in range(T):
                sp.wait_ge(st_x[t], START + 16 * B)

        @block.gpsimd
        def _(pool):
            pool.memset(half[:], -0.5).then_inc(init, 1)
            pool.memset(eps[:], LN_EPS).then_inc(init, 1)
            pool.memset(kT[:].bitcast(F32), 0.0).then_inc(init, 1)
            pool.memset(v[:], 0.0).then_inc(init, 1)
            pool.wait_ge(init, 4)

            class Work(Steps):
                def norm(self, b, t):
                    n = b * T + t
                    pool.wait_ge(s_mv, START + n + 1)
                    pool.tensor_tensor(ve[:, t:t + 1], mv[:, t, 1:2], eps[:], ALU.add).then_inc(s_ve, 1)
                    pool.wait_ge(s_ve, START + n + 1)
                    pool.tensor_tensor(rstd[:, t:t + 1], ve[:, t:t + 1], half[:], ALU.pow).then_inc(s_rs, 1)

                def rotate(self, b, t, i):
                    n = b * T + t
                    pool.wait_ge(s_t, START + 4 * n + 2 * i + 2)
                    pool.wait_ge(s_lo, START + 2 * n)
                    pool.tensor_tensor(rot[:, i], t1[:, i], t2[:, i], ALU.add).then_inc(s_r, 1)

                def q(self, b, t):
                    self.rotate(b, t, 0)

                def k(self, b, t):
                    self.rotate(b, t, 1)

                def normalise(self, b, t, g):
                    pool.wait_ge(s_ri, START + (b * T + t) * 4 + g + 1)
                    pool.tensor_tensor(prob[:, 4 * g:4 * g + 4, :], prob[:, 4 * g:4 * g + 4, :],
                                       rinv[:, 4 * g:4 * g + 4].unsqueeze(2).to_broadcast([P, 4, 2 * P]),
                                       ALU.mult).then_inc(s_pn, 1)

                def group(self, b, t, g):
                    self.normalise(b, t, g)

                def end(self, b, t):
                    pool.wait_ge(s_x1, START + b * T + t + 1)
                    pool.tensor_tensor(xs[:, t], xs[:, t], bias[:], ALU.add).then_inc(s_x1b, 1)

            with pool.Fori(0, B) as b:
                Work().body(b)

        @block.scalar
        def _(act):
            class Work(Steps):
                def norm(self, b, t):
                    n = b * T + t
                    act.wait_ge(s_xT, START + n + 1)
                    act.wait_ge(s_v, START + n)
                    act.activation(xh[:], b0[:], ACT.Copy).then_inc(s_xh, 1)

                def q(self, b, t):
                    n = b * T + t
                    act.wait_ge(s_r, START + 2 * n + 1)
                    act.wait_ge(s_sc[0], START + (4 * n - 3 if t else 4 * n))
                    act.activation(stack[:, 0, :, 0:2 * D1].rearrange("p h (r d) -> p h r d", r=2),
                                   rot[:, 0].rearrange("p (h d) -> p h d", h=H1).unsqueeze(2).to_broadcast([P, H1, 2, D1]),
                                   ACT.Copy).then_inc(s_hi, 1)

                def k(self, b, t):
                    n = b * T + t
                    act.wait_ge(s_r, START + 2 * n + 2)
                    pair = stack[:, 1].rearrange("p h (r d) -> p h r d", r=3)[:, :, 0:3:2, :]
                    act.activation(pair, rot[:, 1].rearrange("p (h d) -> p h d", h=H1).unsqueeze(2).to_broadcast([P, H1, 2, D1]),
                                   ACT.Copy).then_inc(s_hi, 1)

                def v(self, b, t):
                    n = b * T + t
                    act.wait_ge(s_v, START + n + 1)
                    act.activation(v[:, t].rearrange("p h d -> p (h d)"), bq[2][:], ACT.Copy).then_inc(s_vv, 1)

                def turn(self, b, t):
                    n = b * T + t
                    for i in range(4):
                        act.wait_ge(s_trA, START + 8 * n + i + 1)
                        act.activation(turned(2 * i, t), bt[0][0:3 * D1], ACT.Copy).then_inc(s_evA, 1)

                def evac(self, b, t, g):
                    n = b * T + t
                    act.wait_ge(s_trA, START + 8 * n + 4 + g + 1)
                    act.wait_ge(s_pv[g % 2], START + 2 * n + g // 2)
                    act.activation(pT[:, g % 2, 0], bt[0][:], ACT.Copy).then_inc(s_evA, 1)

                def group(self, b, t, g):
                    n = b * T + t
                    for p in (2 * g, 2 * g + 1):
                        act.wait_ge(s_mx, START + 8 * n + p + 1)
                        for i in range(2):
                            h = 2 * p + i
                            act.activation(prob[:, h, :], bs[p % 2][:, i, :], ACT.Exp, bias=nmax[:, h:h + 1],
                                           accum_out=rsum[:, h:h + 1]).then_inc(s_ex[p % 2], 1)
                    if g >= 1:
                        self.evac(b, t, g - 1)

                def end(self, b, t):
                    self.evac(b, t, 3)
                    n = b * T + t
                    act.wait_ge(s_pv[1], START + 2 * n + 2)
                    act.wait_ge(s_op, START + n)
                    act.activation(oTh[:], b0[:], ACT.Copy).then_inc(s_oh, 1)

            with act.Fori(0, B) as b:
                Work().body(b)

        @block.vector
        def _(dve):
            def swapped(ps):
                return ps[:].rearrange("p (h i c) -> p h i c", h=H1, c=2)[:, :, :, ::-1]

            class Work(Steps):
                def norm(self, b, t):
                    n = b * T + t
                    dve.wait_ge(ld_x[t], b * 16 + 16)
                    dve.bn_stats(st6[:, t], xs[:, t]).then_inc(s_bst, 1)
                    dve.wait_ge(s_bst, START + n + 1)
                    dve.tensor_copy(gate[:], st6[:, t, 0:1]).then_inc(s_gate, 1)
                    dve.bn_aggr(mv[:, t], st6[:, t]).then_inc(s_mv, 1)
                    dve.wait_ge(s_rs, START + n + 1)
                    dve.wait_ge(s_xT, START + n)
                    dve.tensor_scalar(xn[:], xs[:, t], mv[:, t, 0:1], rstd[:, t:t + 1], ALU.subtract,
                                      ALU.mult).then_inc(s_xn, 1)
                    dve.wait_ge(s_xh, START + n + 1)
                    dve.tensor_tensor(xl[:], b0[:], xh[:].bitcast(F32), ALU.subtract).then_inc(s_xl, 1)

                def rotate(self, b, t, i, arrived):
                    n = b * T + t
                    dve.wait_ge(arrived, START + n + 1)
                    dve.wait_ge(s_r, START + 2 * n)
                    cos, sin = (rope[:, 2 * i + j, t] for j in range(2))
                    dve.tensor_tensor(t1[:, i].rearrange("p (h d) -> p h d", h=H1),
                                      bq[i][:].rearrange("p (h d) -> p h d", h=H1),
                                      cos.unsqueeze(1).to_broadcast([P, H1, D1]), ALU.mult).then_inc(s_t, 1)
                    dve.tensor_tensor(t2[:, i].rearrange("p (h i c) -> p h i c", h=H1, c=2), swapped(bq[i]),
                                      sin.rearrange("p (i c) -> p i c", c=2).unsqueeze(1).to_broadcast([P, H1, D1 // 2, 2]),
                                      ALU.mult).then_inc(s_t, 1)
                    dve.wait_ge(s_hi, START + 2 * n + i + 1)
                    dst = stack[:, i, :, (2 - i) * D1:(3 - i) * D1]
                    dve.tensor_tensor(dst, rot[:, i].rearrange("p (h d) -> p h d", h=H1),
                                      stack[:, i, :, 0:D1].bitcast(F32), ALU.subtract).then_inc(s_lo, 1)

                def q(self, b, t):
                    self.rotate(b, t, 0, s_q)

                def k(self, b, t):
                    self.rotate(b, t, 1, s_k)

                def turn(self, b, t):
                    n = b * T + t
                    for i in range(4):
                        dve.wait_ge(s_trD, START + 8 * n + i + 1)
                        dve.tensor_copy(turned(2 * i + 1, t), bt[1][0:3 * D1]).then_inc(s_evD, 1)

                def evac(self, b, t, g):
                    n = b * T + t
                    dve.wait_ge(s_trD, START + 8 * n + 4 + g + 1)
                    dve.wait_ge(s_pv[g % 2], START + 2 * n + g // 2)
                    dve.tensor_copy(pT[:, g % 2, 1], bt[1][:]).then_inc(s_evD, 1)

                def group(self, b, t, g):
                    n = b * T + t
                    for p in (2 * g, 2 * g + 1):
                        dve.wait_ge(s_sc[p % 2], START + 4 * n + g + 1)
                        dve.tensor_reduce(nmax[:, 2 * p:2 * p + 2], bs[p % 2][:], AX.X, ALU.max,
                                          negate=True).then_inc(s_mx, 1)
                    if g >= 1:
                        self.evac(b, t, g - 1)
                    for i in range(2):
                        dve.wait_ge(s_ex[i], START + 8 * n + 2 * g + 2)
                    dve.reciprocal(rinv[:, 4 * g:4 * g + 4], rsum[:, 4 * g:4 * g + 4]).then_inc(s_ri, 1)

                def end(self, b, t):
                    self.evac(b, t, 3)
                    n = b * T + t
                    dve.wait_ge(s_oh, START + n + 1)
                    dve.tensor_tensor(oTl[:], b0[:], oTh[:].bitcast(F32), ALU.subtract).then_inc(s_ol, 1)
                    dve.wait_ge(s_op, START + n + 1)
                    dve.tensor_tensor(xs[:, t], bq[0][:], xs[:, t], ALU.add).then_inc(s_x1, 1)

            with dve.Fori(0, B) as b:
                Work().body(b)

        @block.tensor
        def _(pe):
            pe.wait_ge(init, 4)

            class Work(Steps):
                def norm(self, b, t):
                    n = b * T + t
                    pe.wait_ge(s_xn, START + n + 1)
                    pe.wait_ge(s_ol, START + b * T + max(t - 1, 0))
                    for c in range(C):
                        last = pe.transpose(b0[:, c, :], xn[:, c * P:(c + 1) * P], ident[:])
                    last.then_inc(s_xT, 1)

                def project(self, i, done):
                    product(pe, bq[i][:], lambda c: xh[:, c], lambda c: xl[:, c], lambda c: wh[:, c, i],
                            lambda c: wl[:, c, i], C).then_inc(done, 1)

                def q(self, b, t):
                    n = b * T + t
                    pe.wait_ge(s_xh, START + n + 1)
                    pe.wait_ge(s_xl, START + n + 1)
                    pe.wait_ge(s_t, START + 4 * n)
                    pe.wait_ge(s_x1, START + b * T + max(t - 1, 0))
                    self.project(0, s_q)

                def k(self, b, t):
                    self.project(1, s_k)

                def v(self, b, t):
                    pe.wait_ge(s_vv, START + b * T + t)
                    self.project(2, s_v)

                def turn(self, b, t):
                    n = b * T + t
                    for gg in range(8):
                        i = gg // 4
                        if gg % 4 == 0:
                            pe.wait_ge(s_hi, START + 2 * n + i + 1)
                            pe.wait_ge(s_lo, START + 2 * n + i + 1)
                        pe.wait_ge((s_evA, s_evD)[gg % 2], START + 8 * n + gg // 2)
                        for j in range(4):
                            last = pe.transpose(bt[gg % 2][0:3 * D1, j, :], stack[:, i, 4 * (gg % 4) + j, :].bitcast(F32),
                                                ident[:])
                        last.then_inc((s_trA, s_trD)[gg % 2], 1)

                def values(self, b, t, g):
                    n = b * T + t
                    pe.wait_ge(s_pn, START + 4 * n + g + 1)
                    for i in range(2):
                        pe.wait_ge((s_evA, s_evD)[i], START + 8 * n + 4 + g)
                        for j in range(4):
                            last = pe.transpose(bt[i][:, j, :], prob[:, 4 * g + j, i * P:(i + 1) * P], ident[:])
                        last.then_inc((s_trA, s_trD)[i], 1)
                    for i in range(2):
                        pe.wait_ge((s_evA, s_evD)[i], START + 8 * n + 5 + g)
                        if g == 0 and i == 0:
                            pe.wait_ge(s_vv, START + n + 1)
                        keys = t if i == t % 2 else (t - 1) % T
                        for j in range(4):
                            last = pe.matmul(b0[32 * j:32 * j + 32, g, :], v[:, keys, 4 * g + j, :], pT[:, g % 2, i, j, :],
                                             start=(i == 0), stop=(i == 1))
                    last.then_inc(s_pv[g % 2], 1)

                def group(self, b, t, g):
                    n = b * T + t
                    if g == 0:
                        pe.wait_ge(s_evA, START + 8 * n + 4)
                        pe.wait_ge(s_evD, START + 8 * n + 4)
                    kind = 2 if t == 0 else t % 2
                    for p in (2 * g, 2 * g + 1):
                        pe.wait_ge(s_ex[p % 2], START + 8 * n + 2 * g)
                        out = bs[p % 2]
                        pe.matmul(out[:], identb[:], mask[:, kind].unsqueeze(1).to_broadcast([P, 2, 2 * P]), start=True,
                                  stop=False)
                        for i in range(2):
                            h = 2 * p + i
                            last = pe.matmul(out[:, i, :], qT[:, h, :], kT[:, h].rearrange("p a b -> p (a b)"),
                                             start=False, stop=(i == 1))
                        last.then_inc(s_sc[p % 2], 1)
                    if g >= 1:
                        self.values(b, t, g - 1)

                def end(self, b, t):
                    n = b * T + t
                    self.values(b, t, 3)
                    pe.wait_ge(s_oh, START + n + 1)
                    pe.wait_ge(s_ol, START + n + 1)
                    pe.wait_ge(s_t, START + 4 * (b * T + min(t + 2, T)))
                    product(pe, bq[0][:], lambda c: oTh[:, c], lambda c: oTl[:, c], lambda c: oh[:, c],
                            lambda c: ol[:, c], C).then_inc(s_op, 1)

            with pe.Fori(0, B) as b:
                Work().body(b)


def cross_attention(nc, consts, context, wq, wk, wv, w_router, x1, x2, xn3, logits):
    W2 = 4 * D2
    PAIRS = H2 // 2
    G = H2 // 4
    with ExitStack() as ctx:
        m = Phase(nc, ctx, "xa")
        ident = m.sb("ident", [P, P])
        wh = m.sb("wh", [P, 3, C, D], F32R)
        wl = m.sb("wl", [P, 3, C, D], F32R)
        rh = m.sb("rh", [P, C, E], F32R)
        rl = m.sb("rl", [P, C, E], F32R)
        kT = m.sb("kT", [P, PAIRS, 2, S], F32R)
        v = m.sb("v", [P, T, H2, D2 + 1])
        out_ps = m.ps("out", [P, S])
        b0 = m.ps("b0", [P, C, P])
        ring = [m.ps(f"ring{i}", [P, 2, D]) for i in range(3)]

        ld_x = [m.sem(f"ld_x{t}") for t in range(T)]
        ld_c = [m.sem(f"ld_c{t}") for t in range(T)]
        st_x = [m.sem(f"st_x{t}") for t in range(T)]
        st_n = [m.sem(f"st_n{i}") for i in range(2)]
        counters = []

        def counter(name):
            counters.append(m.sem(name))
            return counters[-1]

        s_gate, s_bst, s_mv, s_ve, s_rs, s_xn = [counter(n) for n in "gate bst mv ve rs xn".split()]
        s_xT, s_xh, s_xl, s_pr, s_sq, s_ss, s_ms, s_rr = [counter(n) for n in "xT xh xl pr sq ss ms rr".split()]
        s_kn, s_hi, s_lo, s_vv, s_tr, s_eA, s_eD, s_lg = [counter(n) for n in "kn hi lo vv tr eA eD lg".split()]
        s_sc = [counter(f"sc{i}") for i in range(3)]
        s_ex = [counter(f"ex{i}") for i in range(3)]
        s_pv, s_ot, s_tt, s_ri, s_sm, s_x2 = [counter(n) for n in "pv ot tt ri sm x2".split()]
        counters += st_x + st_n

        with ExitStack() as c2, nc.Block() as block:
            s = Phase(nc, c2, "xw")
            raw = s.sb("raw", [P, 3, C, D])
            rr = s.sb("router", [P, C, E])
            w_c, w_r = s.sem("const"), s.sem("router")
            w_w = [s.sem(f"raw{i}") for i in range(3)]
            w_t, w_hi, w_lo, w_z, w_zo = s.sem("turned"), s.sem("hi"), s.sem("lo"), s.sem("zero"), s.sem("zero_out")
            c2.callback(s.clear)

            @block.sync
            def _(sp):
                for c in counters:
                    sp.sem_inc(c, START)
                sp.dma_start(ident[:], consts[:, K_IDENT:K_IDENT + P]).then_inc(w_c, 16)
                for i, w in enumerate((wq, wk, wv)):
                    sp.dma_start(raw[:, i], w.rearrange("(c p) d -> p c d", p=P)).then_inc(w_w[i], 16)
                sp.dma_start(rr[:], w_router.rearrange("(c p) e -> p c e", p=P)).then_inc(w_r, 16)

            @block.gpsimd
            def _(pool):
                pool.memset(kT[:].bitcast(F32), 0.0).then_inc(w_z, 1)
                pool.memset(v[:], 1.0).then_inc(w_z, 1)
                pool.wait_ge(w_z, 2)

            @block.tensor
            def _(pe):
                pe.wait_ge(w_c, 16)
                for n in range(3 * C):
                    i, c = n // C, n % C
                    if c == 0:
                        pe.wait_ge(w_w[i], 16)
                    if n >= 2:
                        pe.wait_ge(w_lo, n - 1)
                    for f in range(C):
                        last = pe.transpose(ring[n % 2][:, 0, f * P:(f + 1) * P], raw[:, i, f, c * P:(c + 1) * P], ident[:])
                    last.then_inc(w_t, 1)

            @block.scalar
            def _(act):
                for n in range(3 * C):
                    act.wait_ge(w_t, n + 1)
                    act.activation(wh[:, n // C, n % C], ring[n % 2][:, 0], ACT.Copy).then_inc(w_hi, 1)
                act.wait_ge(w_r, 16)
                act.activation(rh[:], rr[:], ACT.Copy).then_inc(w_hi, 1)

            @block.vector
            def _(dve):
                dve.memset(out_ps[:], 0.0).then_inc(w_zo, 1)
                for n in range(3 * C):
                    dve.wait_ge(w_hi, n + 1)
                    dve.tensor_tensor(wl[:, n // C, n % C], ring[n % 2][:, 0], wh[:, n // C, n % C].bitcast(F32),
                                      ALU.subtract).then_inc(w_lo, 1)
                dve.wait_ge(w_hi, 3 * C + 1)
                dve.tensor_tensor(rl[:], rr[:], rh[:].bitcast(F32), ALU.subtract).then_inc(w_lo, 1)

        xs = m.sb("x", [P, T, D])
        prob = m.sb("prob", [P, 2, 4, S])
        cx = prob[:, 1]
        st6 = m.sb("st6", [P, T, 6])
        mv = m.sb("mv", [P, T, 2])
        ve = m.sb("ve", [P, T])
        rstd = m.sb("rstd", [P, T])
        half = m.sb("half", [P, H2])
        eps = m.sb("eps", [P, 1])
        gate = m.sb("gate", [P, 1])
        xn = m.sb("xn", [P, 2, D])
        xh = m.sb("xh", [P, 2, C, P], F32R)
        xl = m.sb("xl", [P, 2, C, P], F32R)
        sq = m.sb("sq", [P, H2, D2])
        ss = m.sb("ss", [P, H2])
        ms = m.sb("ms", [P, H2])
        rr = m.sb("rr", [P, H2])
        kn = sq
        stack = m.sb("stack", [P, H2, W2], F32R)
        qT = m.sb("qT", [P, PAIRS, S], F32R)
        oT = m.sb("oT", [P, S])
        rinv = m.sb("rinv", [P, T, 4])
        scaled = sq[:, 0:T * 4, :].rearrange("p (t h) d -> p t h d", t=T)
        init = m.sem("init")

        ITEMS, KQ = 3 * T, 2 * T
        xT_banks = [b0, ring[2][:, 0, :].rearrange("p (c q) -> p c q", c=C)]
        turn_banks = [ring[1][:, i, :].rearrange("p (a q) -> p a q", a=4) for i in range(2)]
        UNITS = G * T * 2
        PER_SLOT = [len(range(i, UNITS, 3)) for i in range(3)]

        def reads(engine, upto):
            return sum(1 if u < 4 * T or u % 2 == engine else 0 for u in range(upto))

        READS = reads(0, 4 * KQ)

        def product_bank(j):
            return [ring[0][:, 0], ring[0][:, 1]] if j < T else [ring[0][:, j % 2]]

        block = m.main_block()

        @block.sync
        def _(sp):
            with sp.Fori(0, B) as b:
                for t in range(T):
                    sp.wait_ge(s_pv, START + b * G * T)
                    sp.dma_start(cx[:, t], context[bass.ds(b * T + t, 1), :, :].rearrange("a p d -> (a p) d"))\
                      .then_inc(ld_c[t], 16)
                for t in range(T):
                    sp.wait_ge(st_x[t], START + b * 16)
                    sp.dma_start(xs[:, t], x1[bass.ds(b * T + t, 1), :, :].rearrange("a p d -> (a p) d"))\
                      .then_inc(ld_x[t], 16)
                for t in range(T):
                    sp.wait_ge(s_x2, START + (b + 1) * G)
                    sp.dma_start(x2[bass.ds(b * T + t, 1), :, :].rearrange("a p d -> (a p) d"), xs[:, t])\
                      .then_inc(st_x[t], 16)
                for t in range(T):
                    sp.wait_ge(s_xn, START + b * KQ + T + t + 1)
                    sp.dma_start(xn3[bass.ds(b * T + t, 1), :, :].rearrange("a p d -> (a p) d"), xn[:, t % 2])\
                      .then_inc(st_n[t % 2], 16)
            for t in range(T):
                sp.wait_ge(st_x[t], START + 16 * B)
            for i in range(2):
                sp.wait_ge(st_n[i], START + 16 * B * T // 2)

        @block.gpsimd
        def _(pool):
            pool.memset(half[:], -0.5).then_inc(init, 1)
            pool.memset(eps[:], LN_EPS).then_inc(init, 1)
            pool.memset(stack[:].bitcast(F32), 0.0).then_inc(init, 1)
            pool.wait_ge(init, 3)

            def deviation(b, k):
                pool.wait_ge(s_mv, START + 2 * b + k + 1)
                pool.tensor_tensor(ve[:], mv[:, :, 1], eps[:].to_broadcast([P, T]), ALU.add).then_inc(s_ve, 1)
                pool.wait_ge(s_ve, START + 2 * b + k + 1)
                pool.tensor_tensor(rstd[:], ve[:], half[:, 0:T], ALU.pow).then_inc(s_rs, 1)

            with pool.Fori(0, B) as b:
                deviation(b, 0)
                for j in range(KQ):
                    pool.wait_ge(s_ms, START + b * KQ + j + 1)
                    pool.tensor_tensor(rr[:], ms[:], half[:], ALU.pow).then_inc(s_rr, 1)
                deviation(b, 1)

        @block.scalar
        def _(act):
            act.wait_ge(init, 3)

            def high_x(b, j):
                n = b * ITEMS + j
                act.wait_ge(s_xT, START + n + 1)
                act.wait_ge(s_pr, START + (n - 1 if j else n))
                act.activation(xh[:, j % 2], xT_banks[j % 2][:, :, :] if j % 2 == 0 else xT_banks[1], ACT.Copy)\
                   .then_inc(s_xh, 1)

            def heads(b, j):
                n = b * KQ + j
                act.wait_ge(s_pr, START + b * ITEMS + j + 1)
                act.wait_ge(s_lo, START + n)
                banks = product_bank(j)
                if j < T:
                    for i, bank in enumerate(banks):
                        kv = bank.rearrange("p (h d c) -> p h d c", d=D2, c=2)
                        last = act.activation(sq[:, 16 * i:16 * i + 16], kv[:, :, :, 0], ACT.Square)
                        act.activation(v[:, j, 16 * i:16 * i + 16, 0:D2], kv[:, :, :, 1], ACT.Copy).then_inc(s_vv, 1)
                    last.then_inc(s_sq, 1)
                else:
                    act.activation(sq[:].rearrange("p h d -> p (h d)"), banks[0], ACT.Square).then_inc(s_sq, 1)
                act.wait_ge(s_kn, START + n + 1)
                act.wait_ge(s_tr, START + 4 * n)
                places = stack[:].rearrange("p h (r d) -> p h r d", r=4)
                places = places[:, :, 0:3:2, :] if j < T else places[:, :, 0:2, :]
                act.activation(places, kn[:].unsqueeze(2).to_broadcast([P, H2, 2, D2]), ACT.Copy).then_inc(s_hi, 1)

            def turned(b, j):
                n = b * KQ + j
                for q in range(4):
                    if j < T:
                        act.wait_ge(s_tr, START + 4 * n + q + 1)
                        act.activation(kT[0:64, 4 * q:4 * q + 4, 0, j * P:(j + 1) * P], turn_banks[q % 2][0:64],
                                       ACT.Copy).then_inc(s_eA, 1)
                    elif q % 2 == 0:
                        act.wait_ge(s_tr, START + 4 * n + q + 1)
                        act.activation(qT[:, 4 * q:4 * q + 4, (j - T) * P:(j - T + 1) * P], turn_banks[0],
                                       ACT.Copy).then_inc(s_eA, 1)

            with act.Fori(0, B) as b:
                high_x(b, 0)
                for j in range(KQ):
                    if j + 1 < KQ:
                        high_x(b, j + 1)
                    heads(b, j)
                    turned(b, j)
                for u in range(UNITS):
                    act.wait_ge(s_sc[u % 3], START + b * PER_SLOT[u % 3] + u // 3 + 1)
                    if u >= 4:
                        act.wait_ge(s_pv, START + b * G * T + u // 2 - 1)
                    act.activation(prob[:, u // 2 % 2, 2 * (u % 2):2 * (u % 2) + 2, :], ring[u % 3][:], ACT.Exp,
                                   scale=D2 ** -0.5).then_inc(s_ex[u % 3], 1)
                for j in range(KQ, ITEMS):
                    high_x(b, j)

        @block.vector
        def _(dve):
            dve.wait_ge(init, 3)

            def low_x(b, j):
                dve.wait_ge(s_xh, START + b * ITEMS + j + 1)
                dve.tensor_tensor(xl[:, j % 2], xT_banks[j % 2][:, :, :] if j % 2 == 0 else xT_banks[1],
                                  xh[:, j % 2].bitcast(F32), ALU.subtract).then_inc(s_xl, 1)

            def statistics(b, k):
                for t in range(T):
                    if k == 0:
                        dve.wait_ge(ld_x[t], b * 16 + 16)
                    last = dve.bn_stats(st6[:, t], xs[:, t])
                last.then_inc(s_bst, 1)
                dve.wait_ge(s_bst, START + 2 * b + k + 1)
                dve.tensor_copy(gate[:], st6[:, T - 1, 0:1]).then_inc(s_gate, 1)
                for t in range(T):
                    last = dve.bn_aggr(mv[:, t], st6[:, t])
                last.then_inc(s_mv, 1)

            def normalise(b, j):
                t, k = j % T, j // T - 1
                if t == 0:
                    dve.wait_ge(s_rs, START + 2 * b + k + 1)
                dve.wait_ge(s_xT, START + b * ITEMS + j - 1)
                dve.wait_ge(st_n[t % 2], START + 16 * (2 * b + (1 if k == 1 and t >= 2 else 0)))
                dve.tensor_scalar(xn[:, t % 2], xs[:, t], mv[:, t, 0:1], rstd[:, t:t + 1], ALU.subtract,
                                  ALU.mult).then_inc(s_xn, 1)

            def heads(b, j):
                n = b * KQ + j
                dve.wait_ge(s_sq, START + n + 1)
                dve.tensor_reduce(ss[:], sq[:], AX.X, ALU.add).then_inc(s_ss, 1)
                dve.wait_ge(s_ss, START + n + 1)
                dve.tensor_scalar(ms[:], ss[:], 1.0 / D2, RMS_EPS, ALU.mult, ALU.add).then_inc(s_ms, 1)
                dve.wait_ge(s_rr, START + n + 1)
                if j < T:
                    dve.wait_ge(s_vv, START + 2 * (b * T + j) + 2)
                for i, bank in enumerate(product_bank(j)):
                    if j < T:
                        src, hs = bank.rearrange("p (h d c) -> p h d c", d=D2, c=2)[:, :, :, 0], slice(16 * i, 16 * i + 16)
                    else:
                        src, hs = bank.rearrange("p (h d) -> p h d", d=D2), slice(0, H2)
                    nh = src.shape[1]
                    last = dve.tensor_tensor(kn[:, hs], src, rr[:, hs].unsqueeze(2).to_broadcast([P, nh, D2]), ALU.mult)
                last.then_inc(s_kn, 1)
                dve.wait_ge(s_hi, START + n + 1)
                at = 1 if j < T else 2
                dve.tensor_tensor(stack[:, :, at * D2:(at + 1) * D2], kn[:], stack[:, :, 0:D2].bitcast(F32),
                                  ALU.subtract).then_inc(s_lo, 1)

            def turned(b, j):
                n = b * KQ + j
                for q in range(4):
                    if j < T:
                        dve.wait_ge(s_tr, START + 4 * n + q + 1)
                        dve.tensor_copy(kT[64:128, 4 * q:4 * q + 4, 1, j * P:(j + 1) * P], turn_banks[q % 2][64:128])\
                           .then_inc(s_eD, 1)
                    elif q % 2 == 1:
                        dve.wait_ge(s_tr, START + 4 * n + q + 1)
                        dve.tensor_copy(qT[:, 4 * q:4 * q + 4, (j - T) * P:(j - T + 1) * P], turn_banks[1]).then_inc(s_eD, 1)

            with dve.Fori(0, B) as b:
                statistics(b, 0)
                low_x(b, 0)
                for j in range(KQ):
                    if j + 1 < KQ:
                        if j + 1 >= T:
                            normalise(b, j + 1)
                        low_x(b, j + 1)
                    heads(b, j)
                    turned(b, j)
                for g in range(G):
                    k = b * G + g
                    dve.wait_ge(s_pv, START + k * T + T)
                    dve.wait_ge(s_tt, START + k)
                    dve.tensor_copy(oT[:], out_ps[:]).then_inc(s_ot, 1)
                    dve.wait_ge(s_tt, START + k + 1)
                    o = b0[:].rearrange("p t (h d) -> p t h d", h=4)
                    dve.reciprocal(rinv[:], o[:, :, :, D2]).then_inc(s_ri, 1)
                    dve.wait_ge(s_ri, START + k + 1)
                    dve.tensor_tensor(scaled, o[:, :, :, 0:D2], rinv[:].unsqueeze(3).to_broadcast([P, T, 4, D2]),
                                      ALU.mult).then_inc(s_sm, 1)
                    dve.wait_ge(s_sm, START + k + 1)
                    part = xs[:, :, g * 4 * D2:(g + 1) * 4 * D2]
                    dve.tensor_tensor(part, part, scaled.rearrange("p t h d -> p t (h d)"), ALU.add).then_inc(s_x2, 1)
                dve.wait_ge(s_x2, START + b * G + G)
                statistics(b, 1)
                for j in range(KQ, ITEMS):
                    normalise(b, j)
                    low_x(b, j)
                    dve.wait_ge(s_pr, START + b * ITEMS + j + 1)
                    dve.tensor_copy(logits[:, bass.ds(b * T + (j - KQ), 1), :].rearrange("p a e -> p (a e)"),
                                    product_bank(j)[0][:, 0:E]).then_inc(s_lg, 1)

        @block.tensor
        def _(pe):
            def turn_x(b, j):
                n = b * ITEMS + j
                if j < T:
                    pe.wait_ge(ld_c[j], b * 16 + 16)
                else:
                    pe.wait_ge(s_xn, START + b * KQ + (j - T) + 1)
                if j == 0:
                    pe.wait_ge(s_x2, START + b * G)
                pe.wait_ge(s_xl, START + (n - 1 if j else n))
                src = cx[:, j] if j < T else xn[:, j % 2]
                for c in range(C):
                    last = pe.transpose(xT_banks[j % 2][:, c, :], src[:, c * P:(c + 1) * P], ident[:])
                last.then_inc(s_xT, 1)

            def project(b, j):
                n = b * ITEMS + j
                pe.wait_ge(s_xh, START + n + 1)
                pe.wait_ge(s_xl, START + n + 1)
                if j == 0:
                    pe.wait_ge(s_lg, START + b * T)
                elif j <= T:
                    pe.wait_ge(s_kn, START + b * KQ + j)
                    pe.wait_ge(s_vv, START + 2 * (b * T + j))
                elif j < KQ:
                    pe.wait_ge(s_kn, START + b * KQ + j - 1)
                elif j >= KQ + 2:
                    pe.wait_ge(s_lg, START + b * T + j - KQ - 1)
                i = j % 2
                for w, bank in zip((1, 2) if j < T else (0,), product_bank(j)):
                    if j < KQ:
                        last = product(pe, bank, lambda c: xh[:, i, c], lambda c: xl[:, i, c], lambda c: wh[:, w, c],
                                       lambda c: wl[:, w, c], C)
                    else:
                        last = product(pe, bank[:, 0:E], lambda c: xh[:, i, c], lambda c: xl[:, i, c], lambda c: rh[:, c],
                                       lambda c: rl[:, c], C)
                last.then_inc(s_pr, 1)

            def turn_heads(b, j):
                n = b * KQ + j
                pe.wait_ge(s_hi, START + n + 1)
                pe.wait_ge(s_lo, START + n + 1)
                for q in range(4):
                    use = max(4 * j + q - 1, 0)
                    pe.wait_ge(s_eA, START + b * READS + reads(0, use))
                    pe.wait_ge(s_eD, START + b * READS + reads(1, use))
                    for a in range(4):
                        last = pe.transpose(turn_banks[q % 2][:, a, :],
                                            stack[:, 2 * (4 * q + a):2 * (4 * q + a) + 2, :].bitcast(F32)
                                            .rearrange("p h w -> p (h w)"), ident[:])
                    last.then_inc(s_tr, 1)

            def scores(b, u):
                g, kt, pair = u // (2 * T), u // 2 % T, 2 * (u // (2 * T)) + u % 2
                if u >= 3:
                    pe.wait_ge(s_ex[u % 3], START + b * PER_SLOT[u % 3] + u // 3)
                for i in range(2):
                    last = pe.matmul(ring[u % 3][:, i, :], kT[:, pair, i, kt * P:(kt + 1) * P], qT[:, pair, :],
                                     start=True, stop=True)
                last.then_inc(s_sc[u % 3], 1)

            def values(b, w):
                g, kt = w // T, w % T
                for u in (2 * w, 2 * w + 1):
                    pe.wait_ge(s_ex[u % 3], START + b * PER_SLOT[u % 3] + u // 3 + 1)
                if kt == 0:
                    pe.wait_ge(s_ot, START + b * G + g)
                for i in range(4):
                    last = pe.matmul(out_ps[32 * i:32 * i + D2 + 1, :], v[:, kt, 4 * g + i, :], prob[:, w % 2, i, :],
                                     start=(kt == 0), stop=(kt == T - 1))
                last.then_inc(s_pv, 1)

            def turn_out(b, g):
                pe.wait_ge(s_ot, START + b * G + g + 1)
                pe.wait_ge(s_x2, START + b * G + g)
                for t in range(T):
                    last = pe.transpose(b0[:, t, :], oT[:, t * P:(t + 1) * P], ident[:])
                last.then_inc(s_tt, 1)

            with pe.Fori(0, B) as b:
                turn_x(b, 0)
                for j in range(KQ):
                    if j + 1 < KQ:
                        turn_x(b, j + 1)
                    project(b, j)
                    turn_heads(b, j)
                pe.wait_ge(s_eA, START + (b + 1) * READS)
                pe.wait_ge(s_eD, START + (b + 1) * READS)
                pe.wait_ge(s_vv, START + (b + 1) * 2 * T)
                WORK = G * T
                for w in range(WORK + 1):
                    if w < WORK:
                        scores(b, 2 * w)
                        scores(b, 2 * w + 1)
                    if w >= 1:
                        values(b, w - 1)
                    if w >= 3 and (w - 3) % T == 2:
                        turn_out(b, (w - 3) // T)
                turn_out(b, G - 1)
                for j in range(KQ, ITEMS):
                    turn_x(b, j)
                    project(b, j)


def route(nc, consts, logits, slot, weight, token, slots_dram, ybuf):
    NONE = E * CAP
    with ExitStack() as ctx:
        m = Phase(nc, ctx, "ro")
        k_sb = m.sb("consts", [P, K_COLS])
        tri = m.sb("tri", [P, P], BF16)
        ones = m.sb("ones", [P, P], BF16)
        ids = m.sb("ids", [P, NT], I32)
        zero_i = m.sb("zero_i", [P, P], I32)
        zero = m.sb("zero", [1, D])
        gate = m.sb("gate", [P, 5])
        now = m.sb("now", [P, 2, TOPK], I32)
        nowid = m.sb("nowid", [P, 2], I32)
        top = m.sb("top", [P, NT, TOPK])
        index = m.sb("index", [P, NT, TOPK], U32)
        indexf = m.sb("indexf", [P, NT, TOPK])
        onehot = m.sb("onehot", [P, NT, TOPK, E], BF16)
        picked = m.sb("picked", [P, NT, TOPK, E])
        mask = m.sb("mask", [P, NT, E], BF16)
        before = m.sb("before", [P, NT, E], BF16)
        base = m.sb("base", [P, E])
        over = m.sb("over", [P, NT, E])
        place = m.sb("place", [P, NT, E])
        slotf = m.sb("slotf", [P, NT, TOPK])
        diff = m.sb("diff", [P, NT, TOPK])
        total = m.sb("total", [P, NT])
        filled = m.sb("filled", [P, P], I32)
        filledf = m.sb("filledf", [P, P])
        pos = m.ps("pos", [P, 2, NT // 2, E])
        turned = m.ps("turned", [P, P])
        sc = [m.sem(f"scatter{i}") for i in range(2)]
        (s_g, ld, st_z, s_now, ld_f, s_c, s_d, s_top, s_pos, s_exp, s_slot, s_tt, s_before) = [m.sem(n) for n in (
            "g ld st_z now ld_f c d top pos exp slot tt before").split()]
        block = m.main_block()
        iota = k_sb[:, K_IOTA:K_IOTA + E]

        @block.sync
        def _(sp):
            sp.dma_start(k_sb[:], consts).then_inc(ld, 16)
            sp.wait_ge(s_c, 2)
            sp.dma_start(slots_dram.rearrange("(c p) a -> c (p a)", p=P), zero_i[:]).then_inc(st_z, 16)
            sp.dma_start(ybuf[NONE:NONE + 1, :], zero[:]).then_inc(st_z, 16)
            for c in sc:
                sp.wait_ge(c, 16 * TOPK * NT // 2)
            sp.dma_start(filled[:], slots_dram.rearrange("(c p) a -> c (p a)", p=P)).then_inc(ld_f, 16)
            sp.wait_ge(ld_f, 16)

        @block.gpsimd
        def _(pool):
            pool.memset(gate[:], 0.0).then_inc(s_g, 1)
            pool.memset(zero_i[:], 0).then_inc(s_c, 1)
            pool.memset(zero[:], 0.0).then_inc(s_c, 1)
            pool.wait_ge(st_z, 32)
            pool.wait_ge(s_slot, 1)
            pool.wait_ge(s_g, 1)
            with pool.Fori(0, NT // 2) as r:
                for i in range(2):
                    pool.tensor_copy(now[:, i], slot[:, bass.ds((2 * r + i) * TOPK, TOPK)]).then_inc(s_now, 1)
                    pool.tensor_copy(nowid[:, i:i + 1], ids[:, bass.ds(2 * r + i, 1)]).then_inc(s_now, 1)
                    pool.wait_ge(s_now, 4 * r + 2 * i + 2)
                    pool.tensor_tensor(gate[:, 1 + i:2 + i], gate[:, 0:1], gate[:, 0:1], ALU.add)
                    for k in range(TOPK):
                        pool.indirect_dma_start(
                            out=slots_dram, out_offset=bass.IndirectOffsetOnAxis(now[:, i, k:k + 1], 0),
                            in_=nowid[:, i:i + 1], in_offset=None, bounds_check=NONE - 1, oob_is_err=False).then_inc(sc[i], 16)
                for i in range(2):
                    pool.wait_ge(sc[i], 16 * TOPK * (r + 1))
                    pool.tensor_tensor(gate[:, 3 + i:4 + i], gate[:, 0:1], gate[:, 0:1], ALU.add)

        @block.scalar
        def _(act):
            act.wait_ge(s_top, 1)
            act.activation(diff[:], diff[:], ACT.Exp).then_inc(s_exp, 1)

        @block.tensor
        def _(pe):
            pe.wait_ge(s_before, 1)
            for i in range(2):
                half = slice(i * NT // 2, (i + 1) * NT // 2)
                pe.matmul(pos[:, i], tri[:], mask[:, half], start=True, stop=False)
                last = pe.matmul(pos[:, i], ones[:], before[:, half], start=False, stop=True)
            last.then_inc(s_pos, 1)
            pe.wait_ge(s_slot, 3)
            pe.transpose(turned[:], filledf[:], k_sb[:, K_IDENT:K_IDENT + P]).then_inc(s_tt, 1)

        @block.vector
        def _(dve):
            count = [0]

            def then(ins):
                count[0] += 1
                ins.then_inc(s_d, 1)
                dve.wait_ge(s_d, count[0])

            dve.wait_ge(ld, 16)
            dve.tensor_copy(tri[:], k_sb[:, K_TRI:K_TRI + P])
            dve.memset(ones[:], 1.0)
            dve.memset(before[:, 0], 0.0)
            dve.tensor_copy(ids[:], k_sb[:, K_TOK:K_TOK + NT])
            dve.tensor_scalar(base[:], iota, float(CAP), None, ALU.mult)
            for n in range(NT):
                last = dve.max(top[:, n], logits[:, n])
            then(last)
            for n in range(NT):
                last = dve.max_index(index[:, n], top[:, n], logits[:, n])
            then(last)
            dve.tensor_tensor(diff[:], top[:], top[:, :, 0:1].to_broadcast([P, NT, TOPK]), ALU.subtract).then_inc(s_top, 1)
            then(dve.tensor_copy(indexf[:], index[:]))
            then(dve.tensor_tensor(onehot[:].rearrange("p n k e -> p (n k) e"),
                                   indexf[:].rearrange("p n k -> p (n k)").unsqueeze(2).to_broadcast([P, NT * TOPK, E]),
                                   iota.unsqueeze(1).to_broadcast([P, NT * TOPK, E]), ALU.is_equal))
            with nc.allow_low_precision(reason="sums of at most 16 ones"):
                then(dve.tensor_reduce(mask[:], onehot[:].rearrange("p n k e -> p n e k"), AX.X, ALU.add))
            for n in range(1, NT):
                ins = dve.tensor_tensor(before[:, n], before[:, n - 1], mask[:, n - 1], ALU.add)
                then(ins) if n < NT - 1 else ins.then_inc(s_before, 1)
            dve.wait_ge(s_pos, 1)
            places = pos[:].rearrange("p a n e -> p (a n) e")
            dve.tensor_scalar(over[:], places, float(CAP), float(2 * NONE), ALU.is_ge, ALU.mult)
            then(dve.tensor_tensor(place[:], places, base[:].unsqueeze(1).to_broadcast([P, NT, E]), ALU.add))
            then(dve.tensor_tensor(place[:], place[:], over[:], ALU.add))
            for i in range(2):
                h = slice(i * NT // 2, (i + 1) * NT // 2)
                last = dve.tensor_tensor(picked[:, h], onehot[:, h],
                                         place[:, h].unsqueeze(2).to_broadcast([P, NT // 2, TOPK, E]), ALU.mult)
            then(last)
            then(dve.tensor_reduce(slotf[:], picked[:], AX.X, ALU.add))
            then(dve.tensor_scalar(slotf[:], slotf[:], float(NONE), None, ALU.min))
            dve.tensor_copy(slot[:], slotf[:].rearrange("p n k -> p (n k)")).then_inc(s_slot, 1)
            dve.wait_ge(s_exp, 1)
            then(dve.tensor_reduce(total[:], diff[:], AX.X, ALU.add))
            then(dve.reciprocal(total[:], total[:]))
            dve.tensor_tensor(weight[:].rearrange("p (n k) -> p n k", k=TOPK), diff[:],
                              total[:].unsqueeze(2).to_broadcast([P, NT, TOPK]), ALU.mult).then_inc(s_slot, 1)
            dve.wait_ge(ld_f, 16)
            dve.tensor_copy(filledf[:], filled[:]).then_inc(s_slot, 1)
            dve.wait_ge(s_tt, 1)
            dve.tensor_copy(token[:], turned[:]).then_inc(s_slot, 1)


def experts(nc, consts, token, xn3, w_gate, w_up, w_down, ybuf):
    R = I - P
    with ExitStack() as ctx:
        m = Phase(nc, ctx, "ex")
        ident = m.sb("ident", [P, P])
        raw = m.sb("raw", [P, 2, C, 2, I])
        rawd = m.sb("rawd", [P, 2, 2, D])
        wh = m.sb("wh", [P, 2, C, 3, P], F32R)
        wl = m.sb("wl", [P, 2, C, 3, P], F32R)
        dh = m.sb("dh", [P, 2, 2, D], F32R)
        dl = m.sb("dl", [P, 2, 2, D], F32R)
        gate = m.sb("gate", [P, 5])
        now = m.sb("now", [P, 2, CT], I32)
        xg = m.sb("xg", [P, 2, CT, D])
        xh = m.sb("xh", [P, 2, C, CAP], F32R)
        xl = m.sb("xl", [P, 2, C, CAP], F32R)
        sg = m.sb("sg", [P, 2, 2, CAP])
        h = m.sb("h", [P, 2, 2, CAP])
        hh = m.sb("hh", [P, 2, 2, CAP], F32R)
        hl = m.sb("hl", [P, 2, CAP], F32R)
        y = m.sb("y", [P, 2, CT, D])
        bx = [m.ps(f"bx{i}", [P, C, P]) for i in range(2)]
        ba = [m.ps(f"ba{i}", [P, 2, CAP]) for i in range(2)]
        bb = [m.ps(f"bb{i}", [P, CAP]) for i in range(2)]
        by = [m.ps(f"by{i}", [P, D]) for i in range(2)]

        ld_w = [m.sem(f"ld_w{i}") for i in range(2)]
        ld_d = [m.sem(f"ld_d{i}") for i in range(2)]
        ld_g = [m.sem(f"ld_g{i}") for i in range(2)]
        st_y = [[m.sem(f"st_y{i}{j}") for j in range(2)] for i in range(2)]
        w_c, w_g, s_now = m.sem("const"), m.sem("gate"), m.sem("now")
        counters = st_y[0] + st_y[1]

        def counter(name):
            counters.append(m.sem(name))
            return counters[-1]

        s_wh, s_wl, s_dh, s_dl, s_xT, s_xh, s_xl, s_gu = [counter(n) for n in "wh wl dh dl xT xh xl gu".split()]
        s_sg, s_h, s_hh, s_hl, s_dn, s_yA, s_yD = [counter(n) for n in "sg h hh hl dn yA yD".split()]

        with nc.Block() as block:
            @block.sync
            def _(sp):
                for c in counters:
                    sp.sem_inc(c, START)
                sp.dma_start(ident[:], consts[:, K_IDENT:K_IDENT + P]).then_inc(w_c, 16)
                sp.wait_ge(w_c, 16)

            @block.gpsimd
            def _(pool):
                pool.memset(gate[:], 0.0).then_inc(w_g, 1)
                pool.wait_ge(w_g, 1)

        def wait(eng, sem, count):
            if not isinstance(count, int) or count > 0:
                eng.wait_ge(sem, START + count)

        PAIRS = E // 2 - 2

        def loop(eng, first, step, last):
            first()
            step(0, 0, 0)
            with eng.Fori(0, PAIRS) as r:
                step(2 * r + 1, 1, r)
                step(2 * r + 2, 0, r + 1)
            for e in range(2 * PAIRS + 1, E):
                step(e, e % 2, e // 2)
            last()

        def nothing():
            pass

        def expert(a, e):
            return a[e:e + 1] if isinstance(e, int) else a[bass.ds(e, 1)]

        block = m.main_block()

        @block.sync
        def _(sp):
            def load(e, i, r):
                wait(sp, s_wl, 2 * e - 2)
                for n, w in enumerate((w_gate, w_up)):
                    sp.dma_start(raw[:, i, :, n, :], expert(w, e).rearrange("a (c p) f -> p (a c) f", p=P)).then_inc(ld_w[i], 16)
                wait(sp, s_dl, e - 1)
                w = expert(w_down, e)
                sp.dma_start(rawd[:, i, 0, :], w[:, 0:P, :].rearrange("a p d -> (a p) d")).then_inc(ld_d[i], 16)
                for rows in (slice(0, R), slice(R, P)):
                    sp.dma_start(rawd[rows, i, 1, :], w[:, P:I, :].rearrange("a p d -> (a p) d")).then_inc(ld_d[i], 16)

            def store(e, i):
                for j in range(CT):
                    sp.wait_ge((s_yA, s_yD)[j], START + e + 1)
                    at = CT * e + j
                    rows = ybuf[at * P:(at + 1) * P, :] if isinstance(e, int) else ybuf[bass.ds(at * P, P), :]
                    sp.dma_start(rows, y[:, i, j]).then_inc(st_y[i][j], 16)

            def step(e, i, r):
                if not isinstance(e, int) or e < E - 2:
                    load(e + 2, i, r + 1)
                if not isinstance(e, int) or e > 0:
                    store(e - 1, 1 - i)

            def last():
                store(E - 1, 1)
                for i in range(2):
                    for j in range(CT):
                        sp.wait_ge(st_y[i][j], START + 16 * E // 2)

            def first():
                load(0, 0, 0)
                load(1, 1, 0)

            loop(sp, first, step, last)

        @block.gpsimd
        def _(pool):
            def gather(e, i, r):
                wait(pool, s_xT, 2 * e - 2)
                pool.tensor_tensor(gate[:, 1 + i:2 + i], gate[:, 0:1], gate[:, 0:1], ALU.add)
                at = token[:, CT * e:CT * e + CT] if isinstance(e, int) else token[:, bass.ds(CT * e, CT)]
                pool.tensor_copy(now[:, i], at).then_inc(s_now, 1)
                pool.wait_ge(s_now, e + 1)
                pool.tensor_tensor(gate[:, 3 + i:4 + i], gate[:, 0:1], gate[:, 0:1], ALU.add)
                for j in range(CT):
                    pool.indirect_dma_start(out=xg[:, i, j, :], out_offset=None, in_=xn3,
                                            in_offset=bass.IndirectOffsetOnAxis(now[:, i, j:j + 1], 0)).then_inc(ld_g[i], 16)

            def low(e, i):
                pool.wait_ge(s_dh, START + e + 1)
                pool.tensor_tensor(dl[:, i], rawd[:, i], dh[:, i].bitcast(F32), ALU.subtract).then_inc(s_dl, 1)

            def step(e, i, r):
                if not isinstance(e, int) or e < E - 1:
                    gather(e + 1, 1 - i, r + i)
                low(e, i)

            loop(pool, lambda: gather(0, 0, 0), step, nothing)

        def weight_parts(i):
            yield raw[:, i, :, :, 0:P], wh[:, i, :, 0:2, :], wl[:, i, :, 0:2, :]
            yield raw[:, i, :, :, P:I], *(w[:, i, :, 2, :].rearrange("p c (n f) -> p c n f", n=2) for w in (wh, wl))

        @block.scalar
        def _(act):
            def weights(e, i, r):
                act.wait_ge(ld_w[i], 32 * (r + 1))
                wait(act, s_gu, e - 1)
                for src, hi, _ in weight_parts(i):
                    act.activation(hi, src, ACT.Copy).then_inc(s_wh, 1)

            def down_weights(e, i, r):
                act.wait_ge(ld_d[i], 48 * (r + 1))
                wait(act, s_dn, 2 * e - 2)
                act.activation(dh[:, i], rawd[:, i], ACT.Copy).then_inc(s_dh, 1)

            def tokens(e, i):
                for j in range(CT):
                    act.wait_ge(s_xT, START + CT * e + j + 1)
                    act.activation(xh[:, i, :, j * P:(j + 1) * P], bx[j][:], ACT.Copy).then_inc(s_xh, 1)

            def inner(e, i):
                act.wait_ge(s_gu, START + e + 1)
                act.activation(sg[:, i, 0], ba[i][:, 0], ACT.Silu).then_inc(s_sg, 1)
                act.activation(sg[0:R, i, 1], bb[i][0:R], ACT.Silu).then_inc(s_sg, 1)

            def inner_high(e, i):
                act.wait_ge(s_h, START + 2 * e + 2)
                act.activation(hh[:, i, 0], h[:, i, 0], ACT.Copy).then_inc(s_hh, 1)
                act.activation(hh[0:R, i, 1], h[0:R, i, 1], ACT.Copy).then_inc(s_hh, 1)

            def store(e, i, r):
                act.wait_ge(s_dn, START + 2 * e + 1)
                wait(act, st_y[i][0], 16 * r)
                act.activation(y[:, i, 0], by[0][:], ACT.Copy).then_inc(s_yA, 1)

            def first():
                weights(0, 0, 0)
                down_weights(0, 0, 0)
                tokens(0, 0)

            def step(e, i, r):
                ahead = not isinstance(e, int) or e < E - 1
                if ahead:
                    weights(e + 1, 1 - i, r + i)
                inner(e, i)
                if ahead:
                    tokens(e + 1, 1 - i)
                inner_high(e, i)
                if not isinstance(e, int) or e > 0:
                    store(e - 1, 1 - i, r - 1 + i)
                if ahead:
                    down_weights(e + 1, 1 - i, r + i)

            loop(act, first, step, lambda: store(E - 1, 1, E // 2 - 1))

        @block.vector
        def _(dve):
            def weights(e, i):
                dve.wait_ge(s_wh, START + 2 * e + 2)
                for src, hi, lo in weight_parts(i):
                    dve.tensor_tensor(lo, src, hi.bitcast(F32), ALU.subtract).then_inc(s_wl, 1)

            def tokens(e, i):
                for j in range(CT):
                    dve.wait_ge(s_xh, START + CT * e + j + 1)
                    at = slice(j * P, (j + 1) * P)
                    dve.tensor_tensor(xl[:, i, :, at], bx[j][:], xh[:, i, :, at].bitcast(F32), ALU.subtract).then_inc(s_xl, 1)

            def inner(e, i):
                dve.wait_ge(s_sg, START + 2 * e + 2)
                dve.tensor_tensor(h[:, i, 0], ba[i][:, 1], sg[:, i, 0], ALU.mult).then_inc(s_h, 1)
                dve.tensor_tensor(h[0:R, i, 1], bb[i][R:2 * R], sg[0:R, i, 1], ALU.mult).then_inc(s_h, 1)

            def inner_low(e, i):
                dve.wait_ge(s_hh, START + 2 * e + 2)
                dve.tensor_tensor(hl[:, i], h[:, i, 0], hh[:, i, 0].bitcast(F32), ALU.subtract).then_inc(s_hl, 1)
                dve.tensor_tensor(hh[R:2 * R, i, 1], h[0:R, i, 1], hh[0:R, i, 1].bitcast(F32), ALU.subtract).then_inc(s_hl, 1)

            def store(e, i, r):
                dve.wait_ge(s_dn, START + 2 * e + 2)
                wait(dve, st_y[i][1], 16 * r)
                dve.tensor_copy(y[:, i, 1], by[1][:]).then_inc(s_yD, 1)

            def first():
                weights(0, 0)
                tokens(0, 0)

            def step(e, i, r):
                ahead = not isinstance(e, int) or e < E - 1
                if ahead:
                    weights(e + 1, 1 - i)
                inner(e, i)
                if ahead:
                    tokens(e + 1, 1 - i)
                inner_low(e, i)
                if not isinstance(e, int) or e > 0:
                    store(e - 1, 1 - i, r - 1 + i)

            loop(dve, first, step, lambda: store(E - 1, 1, E // 2 - 1))

        @block.tensor
        def _(pe):
            def turn(e, i, r):
                pe.wait_ge(ld_g[i], 16 * CT * (r + 1))
                for j in range(CT):
                    wait(pe, s_xl, CT * e + j - 1)
                    for c in range(C):
                        last = pe.transpose(bx[j][:, c, :], xg[:, i, j, c * P:(c + 1) * P], ident[:])
                    last.then_inc(s_xT, 1)

            def up(e, i):
                pe.wait_ge(s_wl, START + 2 * e + 2)
                pe.wait_ge(s_xl, START + CT * e + CT)
                wait(pe, s_h, 2 * e - 2)
                for n, out in enumerate((ba[i][:, 0], ba[i][:, 1], bb[i][:])):
                    last = product(pe, out, lambda c: wh[:, i, c, n], lambda c: wl[:, i, c, n], lambda c: xh[:, i, c],
                                   lambda c: xl[:, i, c], C)
                last.then_inc(s_gu, 1)

            def down(e, i):
                pe.wait_ge(s_dl, START + e + 1)
                pe.wait_ge(s_hl, START + 2 * e + 2)
                for j in range(CT):
                    wait(pe, (s_yA, s_yD)[j], e)
                    at = slice(j * P, (j + 1) * P)
                    product(pe, by[j][:], lambda c: hh[:, i, 0, at], lambda c: hl[:, i, at], lambda c: dh[:, i, 0],
                            lambda c: dl[:, i, 0], 1, stop=False)
                    pe.matmul(by[j][:], hh[:, i, 1, at], dh[:, i, 1], start=False, stop=False)
                    pe.matmul(by[j][:], hh[:, i, 1, at], dl[:, i, 1], start=False, stop=True).then_inc(s_dn, 1)

            def first():
                turn(0, 0, 0)

            def step(e, i, r):
                up(e, i)
                if not isinstance(e, int) or e < E - 1:
                    turn(e + 1, 1 - i, r + i)
                if not isinstance(e, int) or e > 0:
                    down(e - 1, 1 - i)

            loop(pe, first, step, lambda: down(E - 1, 1))


def combine(nc, slot, weight, x2, ybuf, out):
    with ExitStack() as ctx:
        m = Phase(nc, ctx, "co")
        xs = m.sb("x", [P, 2, D])
        yg = m.sb("y", [P, 2, TOPK, D])
        gate = m.sb("gate", [P, 5])
        now = m.sb("now", [P, 2, TOPK], I32)
        s_g, s_now = m.sem("gate"), m.sem("now")
        ld_x = [m.sem(f"ld_x{i}") for i in range(2)]
        ld_y = [m.sem(f"ld_y{i}") for i in range(2)]
        st = [m.sem(f"st{i}") for i in range(2)]
        s_acc = [m.sem(f"acc{i}") for i in range(2)]
        counters = st + s_acc
        with nc.Block() as block:
            @block.sync
            def _(sp):
                for c in counters:
                    sp.sem_inc(c, START)

            @block.gpsimd
            def _(pool):
                pool.memset(gate[:], 0.0).then_inc(s_g, 1)
                pool.wait_ge(s_g, 1)

        block = m.main_block()

        @block.sync
        def _(sp):
            with sp.Fori(0, NT // 2) as r:
                for i in range(2):
                    sp.wait_ge(st[i], START + 16 * r)
                    sp.dma_start(xs[:, i], x2[bass.ds(2 * r + i, 1)].rearrange("a p d -> (a p) d")).then_inc(ld_x[i], 16)
                for i in range(2):
                    sp.wait_ge(s_acc[i], START + TOPK * (r + 1))
                    sp.dma_start(out[bass.ds(2 * r + i, 1)].rearrange("a p d -> (a p) d"), xs[:, i]).then_inc(st[i], 16)
            for i in range(2):
                sp.wait_ge(st[i], START + 16 * NT // 2)

        @block.gpsimd
        def _(pool):
            with pool.Fori(0, NT // 2) as r:
                for i in range(2):
                    pool.wait_ge(s_acc[i], START + TOPK * r)
                    pool.tensor_tensor(gate[:, 1 + i:2 + i], gate[:, 0:1], gate[:, 0:1], ALU.add)
                    pool.tensor_copy(now[:, i], slot[:, bass.ds((2 * r + i) * TOPK, TOPK)]).then_inc(s_now, 1)
                    pool.wait_ge(s_now, 2 * r + i + 1)
                    pool.tensor_tensor(gate[:, 3 + i:4 + i], gate[:, 0:1], gate[:, 0:1], ALU.add)
                    for k in range(TOPK):
                        pool.indirect_dma_start(
                            out=yg[:, i, k, :], out_offset=None, in_=ybuf,
                            in_offset=bass.IndirectOffsetOnAxis(now[:, i, k:k + 1], 0)).then_inc(ld_y[i], 16)

        @block.vector
        def _(dve):
            with dve.Fori(0, NT // 2) as r:
                for i in range(2):
                    dve.wait_ge(ld_x[i], 16 * (r + 1))
                    dve.wait_ge(ld_y[i], 16 * TOPK * (r + 1))
                    for k in range(TOPK):
                        if k:
                            dve.wait_ge(s_acc[i], START + TOPK * r + k)
                        dve.scalar_tensor_tensor(xs[:, i], yg[:, i, k], weight[:, bass.ds((2 * r + i) * TOPK + k, 1)],
                                                 xs[:, i], ALU.mult, ALU.add).then_inc(s_acc[i], 1)


def decoder_layer(nc, consts, x, context, w_qkv, w_out, b_out, wq, wk, wv, w_router, w_gate, w_up, w_down, out):
    def tiles(a):
        return a.rearrange("b (t p) d -> (b t) p d", p=P)

    x1 = nc.dram_tensor("x1", (NT, P, D), F32).ap()
    x2 = nc.dram_tensor("x2", (NT, P, D), F32).ap()
    xn3 = nc.dram_tensor("xn3", (NT, P, D), F32).ap()
    slots = nc.dram_tensor("slots", (E * CAP, 1), I32).ap()
    ybuf = nc.dram_tensor("ybuf", (E * CAP + 1, D), F32).ap()
    self_attention(nc, consts, tiles(x), w_qkv, w_out, b_out, x1)
    with nc.sbuf_tensor("logits", [P, NT, E], F32) as logits:
        cross_attention(nc, consts, tiles(context), wq, wk, wv, w_router, x1, x2, xn3, logits)
        with nc.sbuf_tensor("slot", [P, NT * TOPK], I32) as slot, nc.sbuf_tensor("weight", [P, NT * TOPK], F32) as weight, \
                nc.sbuf_tensor("token", [P, E * CT], I32) as token:
            route(nc, consts, logits, slot, weight, token, slots, ybuf)
            experts(nc, consts, token, xn3.rearrange("n p d -> (n p) d"), w_gate, w_up, w_down, ybuf)
            combine(nc, slot, weight, x2, ybuf, tiles(out))


def constants():
    import numpy as np

    i = np.arange(P)
    k = np.zeros((P, K_COLS), np.float32)
    k[:, K_IDENT:K_IDENT + P] = np.eye(P)
    k[:, K_TRI:K_TRI + P] = i[:, None] < i[None, :]
    own = np.where(i[None, :] <= i[:, None], 0.0, MASKED)
    past = np.where(i[None, :] >= i[:, None], 0.0, MASKED)
    none = np.full((P, P), MASKED)
    for n, pair in enumerate(((own, past), (past, own), (own, none))):
        k[:, K_MASK + n * 2 * P:K_MASK + (n + 1) * 2 * P] = np.concatenate(pair, 1)
    inv_freq = (1.0 / np.float32(10000.0) ** (np.arange(0, D1, 2, dtype=np.float32) / np.float32(D1))).astype(np.float32)
    angles = np.repeat(np.arange(S, dtype=np.float32)[:, None] * inv_freq[None, :], 2, axis=-1)
    sign = np.where(np.arange(D1) % 2 == 0, -1.0, 1.0)
    cos, sin = np.cos(angles), np.sin(angles) * sign
    scale = D1 ** -0.5
    for n, table in enumerate((cos * scale, sin * scale, cos, sin)):
        at = K_ROPE + n * T * D1
        k[:, at:at + T * D1] = table.reshape(T, P, D1).transpose(1, 0, 2).reshape(P, T * D1)
    k[:, K_IOTA:K_IOTA + E] = np.arange(E)
    k[:, K_TOK:K_TOK + NT] = i[:, None] + P * np.arange(NT)
    return k


_INS = ["x", "ctx_2048", "L0_attn_W_qkv", "L0_attn_W_out", "L0_attn_b_out", "L0_xattn_Wq", "L0_xattn_Wk", "L0_xattn_Wv",
        "L0_ffn_router_weight", "L0_ffn_gate_proj", "L0_ffn_up_proj", "L0_ffn_down_proj"]


def kernel(**inputs):
    import numpy as np
    import concourse.bacc as bacc
    from concourse.bass_utils import run_bass_kernel_spmd

    nc = bacc.Bacc("TRN2", target_bir_lowering=False, num_devices=1)
    arrays, args = {"consts_dram": constants()}, []
    for name in _INS:
        arrays[f"in_{name}_dram"] = np.ascontiguousarray(inputs[name])
    for name, a in arrays.items():
        args.append(nc.dram_tensor(name, a.shape, mybir.dt.from_np(a.dtype), kind="ExternalInput").ap())
    out = nc.dram_tensor("out_0_dram", (B, S, D), F32, kind="ExternalOutput").ap()
    decoder_layer(nc, *args, out)
    r = run_bass_kernel_spmd(nc, [arrays], core_ids=[0])
    return r.results[0]["out_0_dram"]
```

```python
from contextlib import ExitStack

import concourse.bass as bass
from concourse import mybir

F32 = mybir.dt.float32
F32R = mybir.dt.float32r
BF16 = mybir.dt.bfloat16
I32 = mybir.dt.int32
U32 = mybir.dt.uint32
ALU = mybir.AluOpType
ACT = mybir.ActivationFunctionType
AX = mybir.AxisListType

P = 128
B, S, D = 4, 512, 512
T = S // P
NT = B * T
C = D // P
H1, D1 = 16, 32
H2, D2 = 32, 16
E, I, TOPK = 64, 192, 8
CAP = 256
CT = CAP // P
LN_EPS, RMS_EPS = 1e-5, 1e-6
MASKED = -1e30

START = 2

K_IDENT, K_TRI, K_MASK, K_ROPE = 0, 128, 256, 256 + 3 * 256
K_IOTA = K_ROPE + 4 * T * D1
K_TOK = K_IOTA + E
K_COLS = K_TOK + NT


class Phase:

    def __init__(self, nc, ctx, tag):
        self.nc, self.ctx, self.tag, self.sems = nc, ctx, tag, []

    def sb(self, name, shape, dt=F32):
        return self.ctx.enter_context(self.nc.sbuf_tensor(f"{self.tag}_{name}", shape, dt))

    def ps(self, name, shape, dt=F32):
        return self.ctx.enter_context(self.nc.psum_tensor(f"{self.tag}_{name}", shape, dt))

    def sem(self, name):
        self.sems.append(self.ctx.enter_context(self.nc.semaphore(f"{self.tag}_{name}")))
        return self.sems[-1]

    def main_block(self):
        self.ctx.callback(self.clear)
        return self.ctx.enter_context(self.nc.Block())

    def clear(self):
        with self.nc.Block() as block:
            @block.sync
            def _(sp):
                for s in self.sems:
                    sp.sem_clear(s)


def product(pe, out, hi_l, lo_l, hi_r, lo_r, chunks, stop=True):
    for c in range(chunks):
        pe.matmul(out, hi_l(c), hi_r(c), start=(c == 0), stop=False)
        pe.matmul(out, hi_l(c), lo_r(c), start=False, stop=False)
        last = pe.matmul(out, lo_l(c), hi_r(c), start=False, stop=(stop and c == chunks - 1))
    return last


def self_attention(nc, consts, x, w_qkv, w_out, b_out, x1):
    with ExitStack() as ctx:
        m = Phase(nc, ctx, "sa")
        ident = m.sb("ident", [P, P])
        identb = m.sb("identb", [P, P], BF16)
        maskf = m.sb("maskf", [P, 3, 2 * P])
        mask = m.sb("mask", [P, 3, 2 * P], BF16)
        rope = m.sb("rope", [P, 4, T, D1])
        bias = m.sb("bias", [P, D])
        wh = m.sb("wh", [P, C, 3, D], F32R)
        wl = m.sb("wl", [P, C, 3, D], F32R)
        oh = m.sb("oh", [P, C, D], F32R)
        ol = m.sb("ol", [P, C, D], F32R)

        ld_x = [m.sem(f"ld_x{t}") for t in range(T)]
        st_x = [m.sem(f"st_x{t}") for t in range(T)]
        (init, s_gate, s_bst, s_mv, s_ve, s_rs, s_xn, s_xT, s_xh, s_xl, s_q, s_k, s_v, s_t, s_r, s_hi, s_lo, s_vv, s_qt, s_kt,
         s_qe, s_ke, s_mx, s_ri, s_pn, s_pv, s_oh, s_ol, s_op, s_x1, s_x1b) = [m.sem(n) for n in (
             "init gate bst mv ve rs xn xT xh xl q k v t r hi lo vv qt kt qe ke mx ri pn pv oh ol op x1 x1b").split()]
        s_sc, s_ex, s_pt, s_pe = [[m.sem(f"{name}{i}") for i in range(2)] for name in ("sc", "ex", "pt", "pe")]
        counters = [s_gate, s_bst, s_mv, s_ve, s_rs, s_xn, s_xT, s_xh, s_xl, s_q, s_k, s_v, s_t, s_r, s_hi, s_lo, s_vv,
                    s_qt, s_kt, s_qe, s_ke, s_mx, s_ri, s_pn, s_pv, s_oh, s_ol, s_op, s_x1, s_x1b]
        counters += st_x + s_sc + s_ex + s_pt + s_pe

        with ExitStack() as c2, nc.Block() as block:
            s = Phase(nc, c2, "sw")
            raw = s.sb("raw", [P, 2, 3 * D])
            s_c, s_cb = s.sem("const"), s.sem("cast")
            s_w = [s.sem(f"raw{i}") for i in range(2)]
            w_hi, w_lo = s.sem("hi"), s.sem("lo")
            c2.callback(s.clear)

            @block.sync
            def _(sp):
                for counter in counters:
                    sp.sem_inc(counter, START)
                sp.dma_start(ident[:], consts[:, K_IDENT:K_IDENT + P]).then_inc(s_c, 16)
                sp.dma_start(maskf[:].rearrange("p a b -> p (a b)"), consts[:, K_MASK:K_MASK + 768]).then_inc(s_c, 16)
                sp.dma_start(rope[:].rearrange("p a b c -> p (a b c)"),
                             consts[:, K_ROPE:K_ROPE + 4 * T * D1]).then_inc(s_c, 16)
                sp.dma_start(bias[:], b_out.rearrange("(a n) -> a n", a=1).to_broadcast([P, D])).then_inc(s_c, 16)
                for c in range(2 * C):
                    if c >= 2:
                        sp.wait_ge(w_lo, c - 1)
                    if c < C:
                        sp.dma_start(raw[:, c % 2, :], w_qkv[c * P:(c + 1) * P, :]).then_inc(s_w[c % 2], 16)
                    else:
                        sp.dma_start(raw[:, c % 2, 0:D], w_out[(c - C) * P:(c - C + 1) * P, :]).then_inc(s_w[c % 2], 16)
                sp.wait_ge(s_c, 64)

            def parts(c):
                if c < C:
                    return raw[:, c % 2, :].rearrange("p (f t) -> p t f", t=3), wh[:, c], wl[:, c]
                return raw[:, c % 2, 0:D], oh[:, c - C], ol[:, c - C]

            @block.scalar
            def _(act):
                for c in range(2 * C):
                    src, hi, lo = parts(c)
                    act.wait_ge(s_w[c % 2], 16 * (c // 2 + 1))
                    act.activation(hi, src, ACT.Copy).then_inc(w_hi, 1)

            @block.vector
            def _(dve):
                dve.wait_ge(s_c, 64)
                dve.tensor_copy(identb[:], ident[:]).then_inc(s_cb, 1)
                dve.tensor_copy(mask[:], maskf[:]).then_inc(s_cb, 1)
                for c in range(2 * C):
                    src, hi, lo = parts(c)
                    dve.wait_ge(w_hi, c + 1)
                    dve.tensor_tensor(lo, src, hi.bitcast(F32), ALU.subtract).then_inc(w_lo, 1)

        xs = m.sb("x", [P, T, D])
        st6 = m.sb("st6", [P, T, 6])
        mv = m.sb("mv", [P, T, 2])
        ve = m.sb("ve", [P, T])
        half = m.sb("half", [P, 1])
        eps = m.sb("eps", [P, 1])
        gate = m.sb("gate", [P, 1])
        rstd = m.sb("rstd", [P, T])
        xn = m.sb("xn", [P, D])
        xh = m.sb("xh", [P, C, P], F32R)
        xl = m.sb("xl", [P, C, P], F32R)
        t1 = m.sb("t1", [P, 2, D])
        t2 = m.sb("t2", [P, 2, D])
        rot = m.sb("rot", [P, 2, D])
        stack = m.sb("stack", [P, 2, 2, H1, 3 * D1], F32R)
        qT = m.sb("qT", [3 * D1, H1, P], F32R)
        kT = m.sb("kT", [3 * D1, H1, 2, P], F32R)
        v = m.sb("v", [P, T, H1, D1])
        prob = m.sb("prob", [P, H1, 2 * P])
        nmax = m.sb("nmax", [P, H1])
        rsum = m.sb("rsum", [P, H1])
        rinv = m.sb("rinv", [P, H1])
        pT = m.sb("pT", [P, 2, 4, P])
        oTh = m.sb("oTh", [P, C, P], F32R)
        oTl = m.sb("oTl", [P, C, P], F32R)

        out_ps = m.ps("out_ps", [P, C, P])
        pr_ps = [m.ps(f"pr_ps{i}", [P, D]) for i in range(2)]
        xT_ps = m.ps("xT_ps", [P, C, P])
        tn_ps = [m.ps(f"tn_ps{i}", [P, 4, P]) for i in range(2)]
        sc_ps = [m.ps(f"sc_ps{i}", [P, 2, 2 * P]) for i in range(2)]

        class Tile:

            def __init__(self, b, t):
                self.b, self.t = (b + t // T if t // T else b), t % T
                self.n = self.b * T + self.t

            def k(self, g):
                return 4 * self.n + g

            def ahead(self, i):
                return Tile(self.b, self.t + i)

            def exists(self):
                return not isinstance(self.n, int) or 0 <= self.n < NT

        def tiles(engine, tile):
            tile(Tile(0, 0))
            with engine.Fori(0, B - 1) as b:
                for i in range(1, T + 1):
                    tile(Tile(b, i))
            for i in range(1, T):
                tile(Tile(B - 1, i))


        block = m.main_block()

        @block.sync
        def _(sp):
            def load(b, t):
                sp.dma_start(xs[:, t], x[bass.ds(b * T + t, 1), :, :].rearrange("a p d -> (a p) d")).then_inc(ld_x[t], 16)

            def store(b, t):
                sp.wait_ge(s_x1b, START + b * T + t + 1)
                sp.dma_start(x1[bass.ds(b * T + t, 1), :, :].rearrange("a p d -> (a p) d"), xs[:, t]).then_inc(st_x[t], 16)

            for t in range(T):
                load(0, t)
            with sp.Fori(0, B - 1) as b:
                for t in range(T):
                    store(b, t)
                    sp.wait_ge(st_x[t], START + b * 16 + 16)
                    load(b + 1, t)
            for t in range(T):
                store(B - 1, t)
            for t in range(T):
                sp.wait_ge(st_x[t], START + 16 * B)

        @block.gpsimd
        def _(pool):
            pool.memset(half[:], -0.5).then_inc(init, 1)
            pool.memset(eps[:], LN_EPS).then_inc(init, 1)
            pool.memset(kT[:].bitcast(F32), 0.0).then_inc(init, 1)
            pool.memset(v[:], 0.0).then_inc(init, 1)
            pool.wait_ge(init, 4)

            def deviation(at):
                n, t = at.n, at.t
                pool.wait_ge(s_mv, START + n + 1)
                pool.tensor_tensor(ve[:, t:t + 1], mv[:, t, 1:2], eps[:], ALU.add).then_inc(s_ve, 1)
                pool.wait_ge(s_ve, START + n + 1)
                pool.tensor_tensor(rstd[:, t:t + 1], ve[:, t:t + 1], half[:], ALU.pow).then_inc(s_rs, 1)

            def rotate(at, i):
                n = at.n
                pool.wait_ge(s_t, START + 4 * n + 2 * i + 2)
                if not isinstance(n, int) or n > 0:
                    pool.wait_ge(s_lo, START + 2 * n + i - 1)
                pool.tensor_tensor(rot[:, i], t1[:, i], t2[:, i], ALU.add).then_inc(s_r, 1)

            def add_bias(at):
                pool.wait_ge(s_x1, START + at.n + 1)
                pool.tensor_tensor(xs[:, at.t], xs[:, at.t], bias[:], ALU.add).then_inc(s_x1b, 1)

            def tile(at):
                for g in range(4):
                    if g == 0 and at.ahead(2).exists():
                        deviation(at.ahead(2))
                    pool.wait_ge(s_ri, START + at.k(g) + 1)
                    pool.tensor_tensor(prob[:, 4 * g:4 * g + 4, :], prob[:, 4 * g:4 * g + 4, :],
                                       rinv[:, 4 * g:4 * g + 4].unsqueeze(2).to_broadcast([P, 4, 2 * P]),
                                       ALU.mult).then_inc(s_pn, 1)
                    if g in (1, 2) and at.ahead(1).exists():
                        rotate(at.ahead(1), g - 1)
                    if g == 3 and at.ahead(-1).exists():
                        add_bias(at.ahead(-1))

            deviation(Tile(0, 0))
            deviation(Tile(0, 1))
            rotate(Tile(0, 0), 0)
            rotate(Tile(0, 0), 1)
            tiles(pool, tile)
            add_bias(Tile(B - 1, T - 1))

        @block.scalar
        def _(act):
            def high_x(at):
                act.wait_ge(s_xT, START + at.n + 1)
                act.activation(xh[:], xT_ps[:], ACT.Copy).then_inc(s_xh, 1)

            def high_qk(at, i):
                n = at.n
                act.wait_ge(s_r, START + 2 * n + i + 1)
                both = stack[:, at.t % 2, i].rearrange("p h (r d) -> p h r d", r=3)
                act.activation(both[:, :, 0:2, :] if i == 0 else both[:, :, 0:3:2, :],
                               rot[:, i].rearrange("p (h d) -> p h d", h=H1).unsqueeze(2).to_broadcast([P, H1, 2, D1]),
                               ACT.Copy).then_inc(s_hi, 1)

            def take_v(at):
                act.wait_ge(s_v, START + at.n + 1)
                act.activation(v[:, at.t].rearrange("p h d -> p (h d)"), pr_ps[0][:], ACT.Copy).then_inc(s_vv, 1)

            def take_q(at, g):
                act.wait_ge(s_qt, START + at.k(g) + 1)
                act.activation(qT[:, 4 * g:4 * g + 4, :], tn_ps[0][0:3 * D1], ACT.Copy).then_inc(s_qe, 1)

            def take_prob(at, g):
                act.wait_ge(s_pt[0], START + at.k(g) + 1)
                act.activation(pT[:, 0], tn_ps[0][:], ACT.Copy).then_inc(s_pe[0], 1)

            def high_out(at):
                act.wait_ge(s_pv, START + at.k(3) + 1)
                if at.ahead(-1).exists():
                    act.wait_ge(s_op, START + at.n)
                act.activation(oTh[:], out_ps[:], ACT.Copy).then_inc(s_oh, 1)

            def tile(at):
                last, nxt = at.ahead(-1), at.ahead(1)
                for g in range(4):
                    if g == 1 and last.exists():
                        high_out(last)
                    for p in range(2):
                        act.wait_ge(s_mx, START + 2 * at.k(g) + p + 1)
                        for i in range(2):
                            h = 4 * g + 2 * p + i
                            act.activation(prob[:, h, :], sc_ps[p][:, i, :], ACT.Exp, bias=nmax[:, h:h + 1],
                                           accum_out=rsum[:, h:h + 1]).then_inc(s_ex[p], 1)
                    if g > 0:
                        take_prob(at, g - 1)
                    elif last.exists():
                        take_prob(last, 3)
                    if nxt.exists():
                        if g in (2, 3):
                            high_qk(nxt, g - 2)
                        if g == 3:
                            take_v(nxt)
                    if g == 3 and at.ahead(2).exists():
                        high_x(at.ahead(2))
                    if g < 3:
                        take_q(at, g + 1)
                    elif nxt.exists():
                        take_q(nxt, 0)

            high_x(Tile(0, 0))
            high_qk(Tile(0, 0), 0)
            high_qk(Tile(0, 0), 1)
            take_v(Tile(0, 0))
            high_x(Tile(0, 1))
            take_q(Tile(0, 0), 0)
            tiles(act, tile)
            take_prob(Tile(B - 1, T - 1), 3)
            high_out(Tile(B - 1, T - 1))

        @block.vector
        def _(dve):
            def swapped(ps):
                return ps[:].rearrange("p (h i c) -> p h i c", h=H1, c=2)[:, :, :, ::-1]

            def moments(at):
                n, t = at.n, at.t
                dve.wait_ge(ld_x[t], at.b * 16 + 16)
                dve.bn_stats(st6[:, t], xs[:, t]).then_inc(s_bst, 1)
                dve.wait_ge(s_bst, START + n + 1)
                dve.tensor_copy(gate[:], st6[:, t, 0:1]).then_inc(s_gate, 1)
                dve.bn_aggr(mv[:, t], st6[:, t]).then_inc(s_mv, 1)

            def normalise(at):
                n, t = at.n, at.t
                dve.wait_ge(s_rs, START + n + 1)
                if at.ahead(-1).exists():
                    dve.wait_ge(s_xT, START + n)
                dve.tensor_scalar(xn[:], xs[:, t], mv[:, t, 0:1], rstd[:, t:t + 1], ALU.subtract,
                                  ALU.mult).then_inc(s_xn, 1)

            def low_x(at):
                dve.wait_ge(s_xh, START + at.n + 1)
                dve.tensor_tensor(xl[:], xT_ps[:], xh[:].bitcast(F32), ALU.subtract).then_inc(s_xl, 1)

            def rotate(at, i):
                n, t = at.n, at.t
                dve.wait_ge((s_q, s_k)[i], START + n + 1)
                if at.ahead(-1).exists():
                    dve.wait_ge(s_r, START + 2 * n + i - 1)
                cos, sin = (rope[:, 2 * i + j, t] for j in range(2))
                dve.tensor_tensor(t1[:, i].rearrange("p (h d) -> p h d", h=H1),
                                  pr_ps[i][:].rearrange("p (h d) -> p h d", h=H1),
                                  cos.unsqueeze(1).to_broadcast([P, H1, D1]), ALU.mult).then_inc(s_t, 1)
                dve.tensor_tensor(t2[:, i].rearrange("p (h i c) -> p h i c", h=H1, c=2), swapped(pr_ps[i]),
                                  sin.rearrange("p (i c) -> p i c", c=2).unsqueeze(1).to_broadcast([P, H1, D1 // 2, 2]),
                                  ALU.mult).then_inc(s_t, 1)

            def low_qk(at, i):
                dve.wait_ge(s_hi, START + 2 * at.n + i + 1)
                both = stack[:, at.t % 2, i]
                dve.tensor_tensor(both[:, :, (2 - i) * D1:(3 - i) * D1], rot[:, i].rearrange("p (h d) -> p h d", h=H1),
                                  both[:, :, 0:D1].bitcast(F32), ALU.subtract).then_inc(s_lo, 1)

            def take_k(at, g):
                dve.wait_ge(s_kt, START + at.k(g) + 1)
                dve.tensor_copy(kT[:, 4 * g:4 * g + 4, at.t % 2, :], tn_ps[1][0:3 * D1]).then_inc(s_ke, 1)

            def take_prob(at, g):
                dve.wait_ge(s_pt[1], START + at.k(g) + 1)
                dve.tensor_copy(pT[:, 1], tn_ps[1][:]).then_inc(s_pe[1], 1)

            def low_out(at):
                dve.wait_ge(s_oh, START + at.n + 1)
                dve.tensor_tensor(oTl[:], out_ps[:], oTh[:].bitcast(F32), ALU.subtract).then_inc(s_ol, 1)

            def residual(at):
                dve.wait_ge(s_op, START + at.n + 1)
                dve.tensor_tensor(xs[:, at.t], pr_ps[1][:], xs[:, at.t], ALU.add).then_inc(s_x1, 1)

            def tile(at):
                last, nxt = at.ahead(-1), at.ahead(1)
                for g in range(4):
                    for p in range(2):
                        dve.wait_ge(s_sc[p], START + at.k(g) + 1)
                        h = 4 * g + 2 * p
                        dve.tensor_reduce(nmax[:, h:h + 2], sc_ps[p][:], AX.X, ALU.max, negate=True).then_inc(s_mx, 1)
                    if g == 1 and last.exists():
                        low_out(last)
                    if g > 0:
                        take_prob(at, g - 1)
                    elif last.exists():
                        take_prob(last, 3)
                    if g == 0 and at.ahead(2).exists():
                        moments(at.ahead(2))
                    if g in (1, 2) and nxt.exists():
                        rotate(nxt, g - 1)
                    for i in range(2):
                        dve.wait_ge(s_ex[i], START + 2 * at.k(g) + 2)
                    dve.reciprocal(rinv[:, 4 * g:4 * g + 4], rsum[:, 4 * g:4 * g + 4]).then_inc(s_ri, 1)
                    if g in (2, 3) and nxt.exists():
                        low_qk(nxt, g - 2)
                    if g == 2 and at.ahead(2).exists():
                        normalise(at.ahead(2))
                    if g == 3 and at.ahead(2).exists():
                        low_x(at.ahead(2))
                    if g == 3 and last.exists():
                        residual(last)
                    if g < 3:
                        take_k(at, g + 1)
                    elif nxt.exists():
                        take_k(nxt, 0)

            first, second = Tile(0, 0), Tile(0, 1)
            moments(first)
            moments(second)
            normalise(first)
            low_x(first)
            rotate(first, 0)
            rotate(first, 1)
            normalise(second)
            low_qk(first, 0)
            low_qk(first, 1)
            low_x(second)
            take_k(first, 0)
            tiles(dve, tile)
            end = Tile(B - 1, T - 1)
            take_prob(end, 3)
            low_out(end)
            residual(end)

        @block.tensor
        def _(pe):
            pe.wait_ge(init, 4)

            def turn_x(at):
                n = at.n
                pe.wait_ge(s_xn, START + n + 1)
                if at.ahead(-1).exists():
                    pe.wait_ge(s_xh, START + n)
                    pe.wait_ge(s_xl, START + n)
                for c in range(C):
                    done = pe.transpose(xT_ps[:, c, :], xn[:, c * P:(c + 1) * P], ident[:])
                done.then_inc(s_xT, 1)

            def project(at, i):
                n = at.n
                if i == 0:
                    pe.wait_ge(s_xh, START + n + 1)
                    pe.wait_ge(s_xl, START + n + 1)
                    if at.ahead(-1).exists():
                        pe.wait_ge(s_vv, START + n)
                elif i == 1:
                    if at.ahead(-2).exists():
                        pe.wait_ge(s_x1, START + n - 2)
                else:
                    pe.wait_ge(s_t, START + 4 * n + 2)
                product(pe, pr_ps[i % 2][:], lambda c: xh[:, c], lambda c: xl[:, c], lambda c: wh[:, c, i],
                        lambda c: wl[:, c, i], C).then_inc((s_q, s_k, s_v)[i], 1)

            def project_out(at):
                n = at.n
                pe.wait_ge(s_oh, START + n + 1)
                pe.wait_ge(s_ol, START + n + 1)
                k_read = 4 * (n + 3)
                if isinstance(n, int) and n + 2 >= NT:
                    k_read = 4 * NT
                    pe.wait_ge(s_x1, START + n)
                pe.wait_ge(s_t, START + k_read)
                product(pe, pr_ps[1][:], lambda c: oTh[:, c], lambda c: oTl[:, c], lambda c: oh[:, c],
                        lambda c: ol[:, c], C).then_inc(s_op, 1)

            def turn_heads(at, g):
                n, k = at.n, at.k(g)
                for i in range(2):
                    if g == 0:
                        pe.wait_ge(s_hi, START + 2 * n + i + 1)
                        pe.wait_ge(s_lo, START + 2 * n + i + 1)
                    if not isinstance(k, int) or k > 0:
                        pe.wait_ge((s_qe, s_ke)[i], START + k)
                        if not isinstance(k, int) or k > 1:
                            pe.wait_ge(s_pe[i], START + k - 1)
                    for j in range(4):
                        done = pe.transpose(tn_ps[i][0:3 * D1, j, :], stack[:, at.t % 2, i, 4 * g + j, :].bitcast(F32),
                                            ident[:])
                    done.then_inc((s_qt, s_kt)[i], 1)

            def turn_prob(at, g):
                k = at.k(g)
                pe.wait_ge(s_pn, START + k + 1)
                heads_read = k + 2
                if isinstance(k, int):
                    heads_read = min(heads_read, 4 * NT)
                for i in range(2):
                    pe.wait_ge((s_qe, s_ke)[i], START + heads_read)
                    for j in range(4):
                        done = pe.transpose(tn_ps[i][:, j, :], prob[:, 4 * g + j, i * P:(i + 1) * P], ident[:])
                    done.then_inc(s_pt[i], 1)

            def values(at, g):
                k = at.k(g)
                if g == 0:
                    pe.wait_ge(s_vv, START + at.n + 1)
                    if at.ahead(-1).exists():
                        pe.wait_ge(s_oh, START + at.n)
                        pe.wait_ge(s_ol, START + at.n)
                for i in range(2):
                    pe.wait_ge(s_pe[i], START + k + 1)
                    keys = at.t if i == at.t % 2 else (at.t - 1) % T
                    for j in range(4):
                        done = pe.matmul(out_ps[32 * j:32 * j + 32, g, :], v[:, keys, 4 * g + j, :], pT[:, i, j, :],
                                         start=(i == 0), stop=(i == 1))
                done.then_inc(s_pv, 1)

            def scores(at, g):
                k = at.k(g)
                kind = 2 if at.t == 0 else at.t % 2
                pe.wait_ge(s_qe, START + k + 1)
                pe.wait_ge(s_ke, START + k + 1)
                for p in range(2):
                    if not isinstance(k, int) or k > 0:
                        pe.wait_ge(s_ex[p], START + 2 * k)
                    pe.matmul(sc_ps[p][:], identb[:], mask[:, kind].unsqueeze(1).to_broadcast([P, 2, 2 * P]), start=True,
                              stop=False)
                    for i in range(2):
                        h = 4 * g + 2 * p + i
                        done = pe.matmul(sc_ps[p][:, i, :], qT[:, h, :], kT[:, h].rearrange("p a b -> p (a b)"),
                                         start=False, stop=(i == 1))
                    done.then_inc(s_sc[p], 1)

            def tile(at):
                last, nxt = at.ahead(-1), at.ahead(1)
                for g in range(4):
                    before = (at, g - 1) if g > 0 else (last, 3)
                    after = (at, g + 1) if g < 3 else (nxt, 0)
                    scores(at, g)
                    if before[0].exists():
                        turn_prob(*before)
                    if g == 3 and at.ahead(2).exists():
                        turn_x(at.ahead(2))
                    if g < 3 and nxt.exists():
                        project(nxt, g)
                    if g == 3 and last.exists():
                        project_out(last)
                    if after[0].exists():
                        turn_heads(*after)
                    if before[0].exists():
                        values(*before)

            first = Tile(0, 0)
            turn_x(first)
            for i in range(3):
                project(first, i)
            turn_x(first.ahead(1))
            turn_heads(first, 0)
            tiles(pe, tile)
            end = Tile(B - 1, T - 1)
            turn_prob(end, 3)
            values(end, 3)
            project_out(end)


def cross_attention(nc, consts, context, wq, wk, wv, w_router, x1, x2, xn3, logits):
    W2 = 4 * D2
    PAIRS = H2 // 2
    G = H2 // 4
    with ExitStack() as ctx:
        m = Phase(nc, ctx, "xa")
        ident = m.sb("ident", [P, P])
        wh = m.sb("wh", [P, 3, C, D], F32R)
        wl = m.sb("wl", [P, 3, C, D], F32R)
        rh = m.sb("rh", [P, C, E], F32R)
        rl = m.sb("rl", [P, C, E], F32R)
        kT = m.sb("kT", [P, PAIRS, 2, S], F32R)
        v = m.sb("v", [P, T, H2, D2 + 1])
        out_ps = m.ps("out", [P, S])
        b0 = m.ps("b0", [P, C, P])
        ring = [m.ps(f"ring{i}", [P, 2, D]) for i in range(3)]

        ld_x = [m.sem(f"ld_x{t}") for t in range(T)]
        ld_c = [m.sem(f"ld_c{t}") for t in range(T)]
        st_x = [m.sem(f"st_x{t}") for t in range(T)]
        st_n = [m.sem(f"st_n{i}") for i in range(2)]
        counters = []

        def counter(name):
            counters.append(m.sem(name))
            return counters[-1]

        s_gate, s_bst, s_mv, s_ve, s_rs, s_xn = [counter(n) for n in "gate bst mv ve rs xn".split()]
        s_xT, s_xh, s_xl, s_pr, s_sq, s_ss, s_ms, s_im, s_y0 = [counter(n) for n in "xT xh xl pr sq ss ms im y0".split()]
        s_yy, s_my, s_rr = [counter(n) for n in "yy my rr".split()]
        s_kn, s_hi, s_lo, s_vv, s_tr, s_eA, s_eD, s_lg = [counter(n) for n in "kn hi lo vv tr eA eD lg".split()]
        s_sc = [counter(f"sc{i}") for i in range(3)]
        s_ex = [counter(f"ex{i}") for i in range(3)]
        s_pv, s_ot, s_tt, s_ri, s_sm, s_x2 = [counter(n) for n in "pv ot tt ri sm x2".split()]
        counters += st_x + st_n

        with ExitStack() as c2, nc.Block() as block:
            s = Phase(nc, c2, "xw")
            raw = s.sb("raw", [P, 3, C, D])
            rr = s.sb("router", [P, C, E])
            w_c, w_r = s.sem("const"), s.sem("router")
            w_w = [s.sem(f"raw{i}") for i in range(3)]
            w_t, w_hi, w_lo, w_z, w_zo = s.sem("turned"), s.sem("hi"), s.sem("lo"), s.sem("zero"), s.sem("zero_out")
            c2.callback(s.clear)

            @block.sync
            def _(sp):
                for c in counters:
                    sp.sem_inc(c, START)
                sp.dma_start(ident[:], consts[:, K_IDENT:K_IDENT + P]).then_inc(w_c, 16)
                for i, w in enumerate((wq, wk, wv)):
                    sp.dma_start(raw[:, i], w.rearrange("(c p) d -> p c d", p=P)).then_inc(w_w[i], 16)
                sp.dma_start(rr[:], w_router.rearrange("(c p) e -> p c e", p=P)).then_inc(w_r, 16)

            @block.gpsimd
            def _(pool):
                pool.memset(kT[:].bitcast(F32), 0.0).then_inc(w_z, 1)
                pool.memset(v[:], 1.0).then_inc(w_z, 1)
                pool.wait_ge(w_z, 2)

            @block.tensor
            def _(pe):
                pe.wait_ge(w_c, 16)
                for n in range(3 * C):
                    i, c = n // C, n % C
                    if c == 0:
                        pe.wait_ge(w_w[i], 16)
                    if n >= 2:
                        pe.wait_ge(w_lo, n - 1)
                    for f in range(C):
                        last = pe.transpose(ring[n % 2][:, 0, f * P:(f + 1) * P], raw[:, i, f, c * P:(c + 1) * P], ident[:])
                    last.then_inc(w_t, 1)

            @block.scalar
            def _(act):
                for n in range(3 * C):
                    act.wait_ge(w_t, n + 1)
                    act.activation(wh[:, n // C, n % C], ring[n % 2][:, 0], ACT.Copy).then_inc(w_hi, 1)
                act.wait_ge(w_r, 16)
                act.activation(rh[:], rr[:], ACT.Copy).then_inc(w_hi, 1)

            @block.vector
            def _(dve):
                dve.memset(out_ps[:], 0.0).then_inc(w_zo, 1)
                for n in range(3 * C):
                    dve.wait_ge(w_hi, n + 1)
                    dve.tensor_tensor(wl[:, n // C, n % C], ring[n % 2][:, 0], wh[:, n // C, n % C].bitcast(F32),
                                      ALU.subtract).then_inc(w_lo, 1)
                dve.wait_ge(w_hi, 3 * C + 1)
                dve.tensor_tensor(rl[:], rr[:], rh[:].bitcast(F32), ALU.subtract).then_inc(w_lo, 1)

        xs = m.sb("x", [P, T, D])
        prob = m.sb("prob", [P, 2, 4, S])
        cx = prob[:, 1]
        st6 = m.sb("st6", [P, T, 6])
        mv = m.sb("mv", [P, T, 2])
        ve = m.sb("ve", [P, T])
        rstd = m.sb("rstd", [P, T])
        half = m.sb("half", [P, T])
        eps = m.sb("eps", [P, 1])
        gate = m.sb("gate", [P, 1])
        xn = m.sb("xn", [P, 2, D])
        xh = m.sb("xh", [P, 2, C, P], F32R)
        xl = m.sb("xl", [P, 2, C, P], F32R)
        sq = m.sb("sq", [P, H2, D2])
        ss = m.sb("ss", [P, H2])
        mh = m.sb("mh", [P, H2])
        y0 = m.sb("y0", [P, H2])
        rr = m.sb("rr", [P, H2])
        kn = sq
        stack = m.sb("stack", [P, H2, W2], F32R)
        qT = m.sb("qT", [P, PAIRS, S], F32R)
        oT = m.sb("oT", [P, S])
        rinv = m.sb("rinv", [P, T, 4])
        scaled = sq[:, 0:T * 4, :].rearrange("p (t h) d -> p t h d", t=T)
        init = m.sem("init")

        ITEMS, KQ = 3 * T, 2 * T
        turn_banks = [ring[1][:, i, :].rearrange("p (a q) -> p a q", a=4) for i in range(2)]
        UNITS = G * T * 2
        PER_SLOT = [len(range(i, UNITS, 3)) for i in range(3)]

        def reads(engine, upto):
            return sum(1 if u < 4 * T or u % 2 == engine else 0 for u in range(upto))

        READS = reads(0, 4 * KQ)

        def product_bank(j):
            if j < KQ:
                return [ring[j % 2 * 2][:, i] for i in range(2 if j < T else 1)]
            return [ring[0][:, j % 2]]

        def xT_bank(j):
            return b0[:] if j < KQ or j % 2 == 0 else ring[1][:, 0, :].rearrange("p (c q) -> p c q", c=C)

        block = m.main_block()

        @block.sync
        def _(sp):
            with sp.Fori(0, B) as b:
                for t in range(T):
                    sp.wait_ge(s_pv, START + b * G * T)
                    sp.dma_start(cx[:, t], context[bass.ds(b * T + t, 1), :, :].rearrange("a p d -> (a p) d"))\
                      .then_inc(ld_c[t], 16)
                for t in range(T):
                    sp.wait_ge(st_x[t], START + b * 16)
                    sp.dma_start(xs[:, t], x1[bass.ds(b * T + t, 1), :, :].rearrange("a p d -> (a p) d"))\
                      .then_inc(ld_x[t], 16)
                for t in range(T):
                    sp.wait_ge(s_x2, START + (b + 1) * G)
                    sp.dma_start(x2[bass.ds(b * T + t, 1), :, :].rearrange("a p d -> (a p) d"), xs[:, t])\
                      .then_inc(st_x[t], 16)
                for t in range(T):
                    sp.wait_ge(s_xn, START + b * KQ + T + t + 1)
                    sp.dma_start(xn3[bass.ds(b * T + t, 1), :, :].rearrange("a p d -> (a p) d"), xn[:, t % 2])\
                      .then_inc(st_n[t % 2], 16)
            for t in range(T):
                sp.wait_ge(st_x[t], START + 16 * B)
            for i in range(2):
                sp.wait_ge(st_n[i], START + 16 * B * T // 2)

        @block.gpsimd
        def _(pool):
            pool.memset(half[:], -0.5).then_inc(init, 1)
            pool.memset(eps[:], LN_EPS).then_inc(init, 1)
            pool.memset(stack[:].bitcast(F32), 0.0).then_inc(init, 1)
            pool.wait_ge(init, 3)

            def deviation(b, k):
                pool.wait_ge(s_mv, START + 2 * b + k + 1)
                pool.tensor_tensor(ve[:], mv[:, :, 1], eps[:].to_broadcast([P, T]), ALU.add).then_inc(s_ve, 1)
                pool.wait_ge(s_ve, START + 2 * b + k + 1)
                pool.tensor_tensor(rstd[:], ve[:], half[:], ALU.pow).then_inc(s_rs, 1)

            with pool.Fori(0, B) as b:
                deviation(b, 0)
                deviation(b, 1)

        @block.scalar
        def _(act):
            act.wait_ge(init, 3)

            def high_x(b, j):
                n = b * ITEMS + j
                act.wait_ge(s_xT, START + n + 1)
                act.wait_ge(s_pr, START + n - 1)
                act.activation(xh[:, j % 2], xT_bank(j), ACT.Copy).then_inc(s_xh, 1)

            def squares(b, j):
                n = b * KQ + j
                act.wait_ge(s_pr, START + b * ITEMS + j + 1)
                act.wait_ge(s_lo, START + n)
                for i, bank in enumerate(product_bank(j)):
                    if j < T:
                        last = act.activation(sq[:, 16 * i:16 * i + 16],
                                              bank.rearrange("p (h d c) -> p h d c", d=D2, c=2)[:, :, :, 0], ACT.Square)
                    else:
                        last = act.activation(sq[:].rearrange("p h d -> p (h d)"), bank, ACT.Square)
                last.then_inc(s_sq, 1)

            def root(b, j):
                act.wait_ge(s_im, START + b * KQ + j + 1)
                act.activation(y0[:], rr[:], ACT.Sqrt).then_inc(s_y0, 1)

            def take_values(b, j):
                for i, bank in enumerate(product_bank(j)):
                    act.activation(v[:, j, 16 * i:16 * i + 16, 0:D2],
                                   bank.rearrange("p (h d c) -> p h d c", d=D2, c=2)[:, :, :, 1], ACT.Copy).then_inc(s_vv, 1)

            def high_heads(b, j):
                n = b * KQ + j
                act.wait_ge(s_kn, START + n + 1)
                act.wait_ge(s_tr, START + 4 * n)
                places = stack[:].rearrange("p h (r d) -> p h r d", r=4)
                places = places[:, :, 0:3:2, :] if j < T else places[:, :, 0:2, :]
                act.activation(places, kn[:].unsqueeze(2).to_broadcast([P, H2, 2, D2]), ACT.Copy).then_inc(s_hi, 1)

            def turned(b, j):
                n = b * KQ + j
                for q in range(4):
                    if j < T:
                        act.wait_ge(s_tr, START + 4 * n + q + 1)
                        act.activation(kT[0:64, 4 * q:4 * q + 4, 0, j * P:(j + 1) * P], turn_banks[q % 2][0:64],
                                       ACT.Copy).then_inc(s_eA, 1)
                    elif q % 2 == 0:
                        act.wait_ge(s_tr, START + 4 * n + q + 1)
                        act.activation(qT[:, 4 * q:4 * q + 4, (j - T) * P:(j - T + 1) * P], turn_banks[0],
                                       ACT.Copy).then_inc(s_eA, 1)

            with act.Fori(0, B) as b:
                high_x(b, 0)
                high_x(b, 1)
                for j in range(KQ):
                    squares(b, j)
                    if j + 2 < KQ:
                        high_x(b, j + 2)
                    root(b, j)
                    if j < T:
                        take_values(b, j)
                    high_heads(b, j)
                    turned(b, j)
                for u in range(UNITS):
                    act.wait_ge(s_sc[u % 3], START + b * PER_SLOT[u % 3] + u // 3 + 1)
                    if u >= 4:
                        act.wait_ge(s_pv, START + b * G * T + u // 2 - 1)
                    act.activation(prob[:, u // 2 % 2, 2 * (u % 2):2 * (u % 2) + 2, :], ring[u % 3][:], ACT.Exp,
                                   scale=D2 ** -0.5).then_inc(s_ex[u % 3], 1)
                for j in range(KQ, ITEMS):
                    high_x(b, j)

        @block.vector
        def _(dve):
            dve.wait_ge(init, 3)

            def low_x(b, j):
                dve.wait_ge(s_xh, START + b * ITEMS + j + 1)
                dve.tensor_tensor(xl[:, j % 2], xT_bank(j), xh[:, j % 2].bitcast(F32), ALU.subtract).then_inc(s_xl, 1)

            def statistics(b, k):
                for t in range(T):
                    if k == 0:
                        dve.wait_ge(ld_x[t], b * 16 + 16)
                    last = dve.bn_stats(st6[:, t], xs[:, t])
                last.then_inc(s_bst, 1)
                dve.wait_ge(s_bst, START + 2 * b + k + 1)
                dve.tensor_copy(gate[:], st6[:, T - 1, 0:1]).then_inc(s_gate, 1)
                for t in range(T):
                    last = dve.bn_aggr(mv[:, t], st6[:, t])
                last.then_inc(s_mv, 1)

            def normalise(b, j):
                t, k = j % T, j // T - 1
                if t == 0:
                    dve.wait_ge(s_rs, START + 2 * b + k + 1)
                dve.wait_ge(s_xT, START + b * ITEMS + j - 1)
                dve.wait_ge(st_n[t % 2], START + 16 * (2 * b + (1 if k == 1 and t >= 2 else 0)))
                dve.tensor_scalar(xn[:, t % 2], xs[:, t], mv[:, t, 0:1], rstd[:, t:t + 1], ALU.subtract,
                                  ALU.mult).then_inc(s_xn, 1)

            def mean_squares(b, j):
                n = b * KQ + j
                dve.wait_ge(s_sq, START + n + 1)
                dve.tensor_reduce(ss[:], sq[:], AX.X, ALU.add).then_inc(s_ss, 1)
                dve.wait_ge(s_ss, START + n + 1)
                dve.tensor_scalar(mh[:], ss[:], -0.5 / D2, -0.5 * RMS_EPS, ALU.mult, ALU.add)
                dve.tensor_scalar(ss[:], ss[:], 1.0 / D2, RMS_EPS, ALU.mult, ALU.add).then_inc(s_ms, 1)
                dve.wait_ge(s_ms, START + n + 1)
                dve.reciprocal(rr[:], ss[:]).then_inc(s_im, 1)

            def heads(b, j):
                n = b * KQ + j
                dve.wait_ge(s_y0, START + n + 1)
                dve.tensor_tensor(rr[:], y0[:], y0[:], ALU.mult).then_inc(s_yy, 1)
                dve.wait_ge(s_yy, START + n + 1)
                dve.tensor_tensor(rr[:], rr[:], mh[:], ALU.mult).then_inc(s_my, 1)
                dve.wait_ge(s_my, START + n + 1)
                dve.scalar_tensor_tensor(rr[:], rr[:], 1.5, y0[:], ALU.add, ALU.mult).then_inc(s_rr, 1)
                dve.wait_ge(s_rr, START + n + 1)
                if j < T:
                    dve.wait_ge(s_vv, START + 2 * (b * T + j) + 2)
                for i, bank in enumerate(product_bank(j)):
                    if j < T:
                        src, hs = bank.rearrange("p (h d c) -> p h d c", d=D2, c=2)[:, :, :, 0], slice(16 * i, 16 * i + 16)
                    else:
                        src, hs = bank.rearrange("p (h d) -> p h d", d=D2), slice(0, H2)
                    nh = src.shape[1]
                    last = dve.tensor_tensor(kn[:, hs], src, rr[:, hs].unsqueeze(2).to_broadcast([P, nh, D2]), ALU.mult)
                last.then_inc(s_kn, 1)
                dve.wait_ge(s_hi, START + n + 1)
                at = 1 if j < T else 2
                dve.tensor_tensor(stack[:, :, at * D2:(at + 1) * D2], kn[:], stack[:, :, 0:D2].bitcast(F32),
                                  ALU.subtract).then_inc(s_lo, 1)

            def turned(b, j):
                n = b * KQ + j
                for q in range(4):
                    if j < T:
                        dve.wait_ge(s_tr, START + 4 * n + q + 1)
                        dve.tensor_copy(kT[64:128, 4 * q:4 * q + 4, 1, j * P:(j + 1) * P], turn_banks[q % 2][64:128])\
                           .then_inc(s_eD, 1)
                    elif q % 2 == 1:
                        dve.wait_ge(s_tr, START + 4 * n + q + 1)
                        dve.tensor_copy(qT[:, 4 * q:4 * q + 4, (j - T) * P:(j - T + 1) * P], turn_banks[1]).then_inc(s_eD, 1)

            def take_logits(b, j):
                dve.wait_ge(s_pr, START + b * ITEMS + j + 1)
                dve.tensor_copy(logits[:, bass.ds(b * T + (j - KQ), 1), :].rearrange("p a e -> p (a e)"),
                                product_bank(j)[0][:, 0:E]).then_inc(s_lg, 1)

            with dve.Fori(0, B) as b:
                low_x(b, 0)
                low_x(b, 1)
                for j in range(KQ):
                    mean_squares(b, j)
                    if j + 2 < KQ:
                        low_x(b, j + 2)
                    heads(b, j)
                    if j == 0:
                        statistics(b, 0)
                    if T <= j + 3 < KQ:
                        normalise(b, j + 3)
                    turned(b, j)
                for g in range(G):
                    k = b * G + g
                    dve.wait_ge(s_pv, START + k * T + T)
                    dve.wait_ge(s_tt, START + k)
                    dve.tensor_copy(oT[:], out_ps[:]).then_inc(s_ot, 1)
                    dve.wait_ge(s_tt, START + k + 1)
                    o = b0[:].rearrange("p t (h d) -> p t h d", h=4)
                    dve.reciprocal(rinv[:], o[:, :, :, D2]).then_inc(s_ri, 1)
                    dve.wait_ge(s_ri, START + k + 1)
                    dve.tensor_tensor(scaled, o[:, :, :, 0:D2], rinv[:].unsqueeze(3).to_broadcast([P, T, 4, D2]),
                                      ALU.mult).then_inc(s_sm, 1)
                    dve.wait_ge(s_sm, START + k + 1)
                    part = xs[:, :, g * 4 * D2:(g + 1) * 4 * D2]
                    dve.tensor_tensor(part, part, scaled.rearrange("p t h d -> p t (h d)"), ALU.add).then_inc(s_x2, 1)
                dve.wait_ge(s_x2, START + b * G + G)
                statistics(b, 1)
                normalise(b, KQ)
                for j in range(KQ, ITEMS):
                    if j + 1 < ITEMS:
                        normalise(b, j + 1)
                    low_x(b, j)
                    if j > KQ:
                        take_logits(b, j - 1)
                take_logits(b, ITEMS - 1)

        @block.tensor
        def _(pe):
            def turn_x(b, j):
                n = b * ITEMS + j
                if j < T:
                    pe.wait_ge(ld_c[j], b * 16 + 16)
                else:
                    pe.wait_ge(s_xn, START + b * KQ + (j - T) + 1)
                if j == 0:
                    pe.wait_ge(s_x2, START + b * G)
                pe.wait_ge(s_xl, START + (n - 1 if j > KQ else n))
                src = cx[:, j] if j < T else xn[:, j % 2]
                for c in range(C):
                    last = pe.transpose(xT_bank(j)[:, c, :], src[:, c * P:(c + 1) * P], ident[:])
                last.then_inc(s_xT, 1)

            def project(b, j):
                n = b * ITEMS + j
                pe.wait_ge(s_xh, START + n + 1)
                pe.wait_ge(s_xl, START + n + 1)
                if j == 0:
                    pe.wait_ge(s_lg, START + b * T)
                elif 2 <= j < KQ:
                    pe.wait_ge(s_kn, START + b * KQ + j - 1)
                elif j >= KQ + 2:
                    pe.wait_ge(s_lg, START + b * T + j - KQ - 1)
                i = j % 2
                for w, bank in zip((1, 2) if j < T else (0,), product_bank(j)):
                    if j < KQ:
                        last = product(pe, bank, lambda c: xh[:, i, c], lambda c: xl[:, i, c], lambda c: wh[:, w, c],
                                       lambda c: wl[:, w, c], C)
                    else:
                        last = product(pe, bank[:, 0:E], lambda c: xh[:, i, c], lambda c: xl[:, i, c], lambda c: rh[:, c],
                                       lambda c: rl[:, c], C)
                last.then_inc(s_pr, 1)

            def turn_heads(b, j):
                n = b * KQ + j
                pe.wait_ge(s_hi, START + n + 1)
                pe.wait_ge(s_lo, START + n + 1)
                for q in range(4):
                    use = max(4 * j + q - 1, 0)
                    pe.wait_ge(s_eA, START + b * READS + reads(0, use))
                    pe.wait_ge(s_eD, START + b * READS + reads(1, use))
                    for a in range(4):
                        last = pe.transpose(turn_banks[q % 2][:, a, :],
                                            stack[:, 2 * (4 * q + a):2 * (4 * q + a) + 2, :].bitcast(F32)
                                            .rearrange("p h w -> p (h w)"), ident[:])
                    last.then_inc(s_tr, 1)

            def scores(b, u):
                g, kt, pair = u // (2 * T), u // 2 % T, 2 * (u // (2 * T)) + u % 2
                if u >= 3:
                    pe.wait_ge(s_ex[u % 3], START + b * PER_SLOT[u % 3] + u // 3)
                for i in range(2):
                    last = pe.matmul(ring[u % 3][:, i, :], kT[:, pair, i, kt * P:(kt + 1) * P], qT[:, pair, :],
                                     start=True, stop=True)
                last.then_inc(s_sc[u % 3], 1)

            def values(b, w):
                g, kt = w // T, w % T
                for u in (2 * w, 2 * w + 1):
                    pe.wait_ge(s_ex[u % 3], START + b * PER_SLOT[u % 3] + u // 3 + 1)
                if kt == 0:
                    pe.wait_ge(s_ot, START + b * G + g)
                for i in range(4):
                    last = pe.matmul(out_ps[32 * i:32 * i + D2 + 1, :], v[:, kt, 4 * g + i, :], prob[:, w % 2, i, :],
                                     start=(kt == 0), stop=(kt == T - 1))
                last.then_inc(s_pv, 1)

            def turn_out(b, g):
                pe.wait_ge(s_ot, START + b * G + g + 1)
                pe.wait_ge(s_x2, START + b * G + g)
                for t in range(T):
                    last = pe.transpose(b0[:, t, :], oT[:, t * P:(t + 1) * P], ident[:])
                last.then_inc(s_tt, 1)

            with pe.Fori(0, B) as b:
                turn_x(b, 0)
                turn_x(b, 1)
                project(b, 0)
                for j in range(KQ):
                    if j + 2 < KQ:
                        turn_x(b, j + 2)
                    if j + 1 < KQ:
                        project(b, j + 1)
                    turn_heads(b, j)
                pe.wait_ge(s_eA, START + (b + 1) * READS)
                pe.wait_ge(s_eD, START + (b + 1) * READS)
                pe.wait_ge(s_vv, START + (b + 1) * 2 * T)
                WORK = G * T
                for w in range(WORK + 1):
                    if w < WORK:
                        scores(b, 2 * w)
                        scores(b, 2 * w + 1)
                    if w >= 1:
                        values(b, w - 1)
                    if w >= 3 and (w - 3) % T == 2:
                        turn_out(b, (w - 3) // T)
                turn_out(b, G - 1)
                turn_x(b, KQ)
                for j in range(KQ, ITEMS):
                    if j + 1 < ITEMS:
                        turn_x(b, j + 1)
                    project(b, j)


def route(nc, consts, logits, slot, weight, token, slots_dram, ybuf):
    NONE = E * CAP
    with ExitStack() as ctx:
        m = Phase(nc, ctx, "ro")
        k_sb = m.sb("consts", [P, K_COLS])
        tri = m.sb("tri", [P, P], BF16)
        ones = m.sb("ones", [P, P], BF16)
        ids = m.sb("ids", [P, NT], I32)
        zero_i = m.sb("zero_i", [P, P], I32)
        zero = m.sb("zero", [1, D])
        gate = m.sb("gate", [P, 5])
        now = m.sb("now", [P, 2, TOPK], I32)
        nowid = m.sb("nowid", [P, 2], I32)
        top = m.sb("top", [P, NT, TOPK])
        index = m.sb("index", [P, NT, TOPK], U32)
        indexf = m.sb("indexf", [P, NT, TOPK])
        onehot = m.sb("onehot", [P, NT, TOPK, E], BF16)
        picked = m.sb("picked", [P, NT, TOPK, E])
        mask = m.sb("mask", [P, NT, E], BF16)
        before = m.sb("before", [P, NT, E], BF16)
        base = m.sb("base", [P, E])
        over = m.sb("over", [P, NT, E])
        place = m.sb("place", [P, NT, E])
        slotf = m.sb("slotf", [P, NT, TOPK])
        diff = m.sb("diff", [P, NT, TOPK])
        total = m.sb("total", [P, NT])
        filled = m.sb("filled", [P, P], I32)
        filledf = m.sb("filledf", [P, P])
        pos = m.ps("pos", [P, 2, NT // 2, E])
        turned = m.ps("turned", [P, P])
        sc = [m.sem(f"scatter{i}") for i in range(2)]
        (s_g, ld, st_z, s_now, ld_f, s_c, s_d, s_top, s_pos, s_exp, s_slot, s_tt, s_before) = [m.sem(n) for n in (
            "g ld st_z now ld_f c d top pos exp slot tt before").split()]
        block = m.main_block()
        iota = k_sb[:, K_IOTA:K_IOTA + E]

        @block.sync
        def _(sp):
            sp.dma_start(k_sb[:], consts).then_inc(ld, 16)
            sp.wait_ge(s_c, 2)
            sp.dma_start(slots_dram.rearrange("(c p) a -> c (p a)", p=P), zero_i[:]).then_inc(st_z, 16)
            sp.dma_start(ybuf[NONE:NONE + 1, :], zero[:]).then_inc(st_z, 16)
            for c in sc:
                sp.wait_ge(c, 16 * TOPK * NT // 2)
            sp.dma_start(filled[:], slots_dram.rearrange("(c p) a -> c (p a)", p=P)).then_inc(ld_f, 16)
            sp.wait_ge(ld_f, 16)

        @block.gpsimd
        def _(pool):
            pool.memset(gate[:], 0.0).then_inc(s_g, 1)
            pool.memset(zero_i[:], 0).then_inc(s_c, 1)
            pool.memset(zero[:], 0.0).then_inc(s_c, 1)
            pool.wait_ge(st_z, 32)
            pool.wait_ge(s_slot, 1)
            pool.wait_ge(s_g, 1)
            with pool.Fori(0, NT // 2) as r:
                for i in range(2):
                    pool.tensor_copy(now[:, i], slot[:, bass.ds((2 * r + i) * TOPK, TOPK)]).then_inc(s_now, 1)
                    pool.tensor_copy(nowid[:, i:i + 1], ids[:, bass.ds(2 * r + i, 1)]).then_inc(s_now, 1)
                    pool.wait_ge(s_now, 4 * r + 2 * i + 2)
                    pool.tensor_tensor(gate[:, 1 + i:2 + i], gate[:, 0:1], gate[:, 0:1], ALU.add)
                    for k in range(TOPK):
                        pool.indirect_dma_start(
                            out=slots_dram, out_offset=bass.IndirectOffsetOnAxis(now[:, i, k:k + 1], 0),
                            in_=nowid[:, i:i + 1], in_offset=None, bounds_check=NONE - 1, oob_is_err=False).then_inc(sc[i], 16)
                for i in range(2):
                    pool.wait_ge(sc[i], 16 * TOPK * (r + 1))
                    pool.tensor_tensor(gate[:, 3 + i:4 + i], gate[:, 0:1], gate[:, 0:1], ALU.add)

        @block.scalar
        def _(act):
            act.wait_ge(s_top, 1)
            act.activation(diff[:], diff[:], ACT.Exp).then_inc(s_exp, 1)

        @block.tensor
        def _(pe):
            pe.wait_ge(s_before, 1)
            for i in range(2):
                half = slice(i * NT // 2, (i + 1) * NT // 2)
                pe.matmul(pos[:, i], tri[:], mask[:, half], start=True, stop=False)
                last = pe.matmul(pos[:, i], ones[:], before[:, half], start=False, stop=True)
            last.then_inc(s_pos, 1)
            pe.wait_ge(s_slot, 3)
            pe.transpose(turned[:], filledf[:], k_sb[:, K_IDENT:K_IDENT + P]).then_inc(s_tt, 1)

        @block.vector
        def _(dve):
            count = [0]

            def then(ins):
                count[0] += 1
                ins.then_inc(s_d, 1)
                dve.wait_ge(s_d, count[0])

            dve.wait_ge(ld, 16)
            dve.tensor_copy(tri[:], k_sb[:, K_TRI:K_TRI + P])
            dve.memset(ones[:], 1.0)
            dve.memset(before[:, 0], 0.0)
            dve.tensor_copy(ids[:], k_sb[:, K_TOK:K_TOK + NT])
            dve.tensor_scalar(base[:], iota, float(CAP), None, ALU.mult)
            for n in range(NT):
                last = dve.max(top[:, n], logits[:, n])
            then(last)
            for n in range(NT):
                last = dve.max_index(index[:, n], top[:, n], logits[:, n])
            then(last)
            dve.tensor_tensor(diff[:], top[:], top[:, :, 0:1].to_broadcast([P, NT, TOPK]), ALU.subtract).then_inc(s_top, 1)
            then(dve.tensor_copy(indexf[:], index[:]))
            then(dve.tensor_tensor(onehot[:].rearrange("p n k e -> p (n k) e"),
                                   indexf[:].rearrange("p n k -> p (n k)").unsqueeze(2).to_broadcast([P, NT * TOPK, E]),
                                   iota.unsqueeze(1).to_broadcast([P, NT * TOPK, E]), ALU.is_equal))
            with nc.allow_low_precision(reason="sums of at most 16 ones"):
                then(dve.tensor_reduce(mask[:], onehot[:].rearrange("p n k e -> p n e k"), AX.X, ALU.add))
            for n in range(1, NT):
                ins = dve.tensor_tensor(before[:, n], before[:, n - 1], mask[:, n - 1], ALU.add)
                then(ins) if n < NT - 1 else ins.then_inc(s_before, 1)
            dve.wait_ge(s_pos, 1)
            places = pos[:].rearrange("p a n e -> p (a n) e")
            dve.tensor_scalar(over[:], places, float(CAP), float(2 * NONE), ALU.is_ge, ALU.mult)
            then(dve.tensor_tensor(place[:], places, base[:].unsqueeze(1).to_broadcast([P, NT, E]), ALU.add))
            then(dve.tensor_tensor(place[:], place[:], over[:], ALU.add))
            for i in range(2):
                h = slice(i * NT // 2, (i + 1) * NT // 2)
                last = dve.tensor_tensor(picked[:, h], onehot[:, h],
                                         place[:, h].unsqueeze(2).to_broadcast([P, NT // 2, TOPK, E]), ALU.mult)
            then(last)
            then(dve.tensor_reduce(slotf[:], picked[:], AX.X, ALU.add))
            then(dve.tensor_scalar(slotf[:], slotf[:], float(NONE), None, ALU.min))
            dve.tensor_copy(slot[:], slotf[:].rearrange("p n k -> p (n k)")).then_inc(s_slot, 1)
            dve.wait_ge(s_exp, 1)
            then(dve.tensor_reduce(total[:], diff[:], AX.X, ALU.add))
            then(dve.reciprocal(total[:], total[:]))
            dve.tensor_tensor(weight[:].rearrange("p (n k) -> p n k", k=TOPK), diff[:],
                              total[:].unsqueeze(2).to_broadcast([P, NT, TOPK]), ALU.mult).then_inc(s_slot, 1)
            dve.wait_ge(ld_f, 16)
            dve.tensor_copy(filledf[:], filled[:]).then_inc(s_slot, 1)
            dve.wait_ge(s_tt, 1)
            dve.tensor_copy(token[:], turned[:]).then_inc(s_slot, 1)


def experts(nc, consts, token, xn3, w_gate, w_up, w_down, ybuf):
    R = I - P
    with ExitStack() as ctx:
        m = Phase(nc, ctx, "ex")
        ident = m.sb("ident", [P, P])
        raw = m.sb("raw", [P, 2, C, 2, I])
        rawd = m.sb("rawd", [P, 2, 2, D])
        wh = m.sb("wh", [P, 2, C, 3, P], F32R)
        wl = m.sb("wl", [P, 2, C, 3, P], F32R)
        dh = m.sb("dh", [P, 2, 2, D], F32R)
        dl = m.sb("dl", [P, 2, 2, D], F32R)
        gate = m.sb("gate", [P, 5])
        now = m.sb("now", [P, 2, CT], I32)
        xg = m.sb("xg", [P, 2, CT, D])
        xh = m.sb("xh", [P, 2, C, CAP], F32R)
        xl = m.sb("xl", [P, 2, C, CAP], F32R)
        sg = m.sb("sg", [P, 2, 2, CAP])
        h = m.sb("h", [P, 2, 2, CAP])
        hh = m.sb("hh", [P, 2, 2, CAP], F32R)
        hl = m.sb("hl", [P, 2, CAP], F32R)
        y = m.sb("y", [P, 2, CT, D])
        bx = [m.ps(f"bx{i}", [P, C, P]) for i in range(2)]
        ba = [m.ps(f"ba{i}", [P, 2, CAP]) for i in range(2)]
        bb = [m.ps(f"bb{i}", [P, CAP]) for i in range(2)]
        by = [m.ps(f"by{i}", [P, D]) for i in range(2)]

        ld_w = [m.sem(f"ld_w{i}") for i in range(2)]
        ld_d = [m.sem(f"ld_d{i}") for i in range(2)]
        ld_g = [m.sem(f"ld_g{i}") for i in range(2)]
        st_y = [[m.sem(f"st_y{i}{j}") for j in range(2)] for i in range(2)]
        w_c, w_g, s_now = m.sem("const"), m.sem("gate"), m.sem("now")
        counters = st_y[0] + st_y[1]

        def counter(name):
            counters.append(m.sem(name))
            return counters[-1]

        s_wh, s_wl, s_dh, s_dl, s_xT, s_xh, s_xl, s_gu = [counter(n) for n in "wh wl dh dl xT xh xl gu".split()]
        s_sg, s_h, s_hh, s_hl, s_dn, s_yA, s_yD = [counter(n) for n in "sg h hh hl dn yA yD".split()]

        with nc.Block() as block:
            @block.sync
            def _(sp):
                for c in counters:
                    sp.sem_inc(c, START)
                sp.dma_start(ident[:], consts[:, K_IDENT:K_IDENT + P]).then_inc(w_c, 16)
                sp.wait_ge(w_c, 16)

            @block.gpsimd
            def _(pool):
                pool.memset(gate[:], 0.0).then_inc(w_g, 1)
                pool.wait_ge(w_g, 1)

        def wait(eng, sem, count):
            if not isinstance(count, int) or count > 0:
                eng.wait_ge(sem, START + count)

        PAIRS = E // 2 - 2

        def loop(eng, first, step, last):
            first()
            step(0, 0, 0)
            with eng.Fori(0, PAIRS) as r:
                step(2 * r + 1, 1, r)
                step(2 * r + 2, 0, r + 1)
            for e in range(2 * PAIRS + 1, E):
                step(e, e % 2, e // 2)
            last()

        def nothing():
            pass

        def expert(a, e):
            return a[e:e + 1] if isinstance(e, int) else a[bass.ds(e, 1)]

        block = m.main_block()

        @block.sync
        def _(sp):
            def load(e, i, r):
                wait(sp, s_wl, 2 * e - 2)
                for n, w in enumerate((w_gate, w_up)):
                    sp.dma_start(raw[:, i, :, n, :], expert(w, e).rearrange("a (c p) f -> p (a c) f", p=P)).then_inc(ld_w[i], 16)
                wait(sp, s_dl, e - 1)
                w = expert(w_down, e)
                sp.dma_start(rawd[:, i, 0, :], w[:, 0:P, :].rearrange("a p d -> (a p) d")).then_inc(ld_d[i], 16)
                for rows in (slice(0, R), slice(R, P)):
                    sp.dma_start(rawd[rows, i, 1, :], w[:, P:I, :].rearrange("a p d -> (a p) d")).then_inc(ld_d[i], 16)

            def store(e, i):
                for j in range(CT):
                    sp.wait_ge((s_yA, s_yD)[j], START + e + 1)
                    at = CT * e + j
                    rows = ybuf[at * P:(at + 1) * P, :] if isinstance(e, int) else ybuf[bass.ds(at * P, P), :]
                    sp.dma_start(rows, y[:, i, j]).then_inc(st_y[i][j], 16)

            def step(e, i, r):
                if not isinstance(e, int) or e < E - 2:
                    load(e + 2, i, r + 1)
                if not isinstance(e, int) or e > 0:
                    store(e - 1, 1 - i)

            def last():
                store(E - 1, 1)
                for i in range(2):
                    for j in range(CT):
                        sp.wait_ge(st_y[i][j], START + 16 * E // 2)

            def first():
                load(0, 0, 0)
                load(1, 1, 0)

            loop(sp, first, step, last)

        @block.gpsimd
        def _(pool):
            def gather(e, i, r):
                wait(pool, s_xT, 2 * e - 2)
                pool.tensor_tensor(gate[:, 1 + i:2 + i], gate[:, 0:1], gate[:, 0:1], ALU.add)
                at = token[:, CT * e:CT * e + CT] if isinstance(e, int) else token[:, bass.ds(CT * e, CT)]
                pool.tensor_copy(now[:, i], at).then_inc(s_now, 1)
                pool.wait_ge(s_now, e + 1)
                pool.tensor_tensor(gate[:, 3 + i:4 + i], gate[:, 0:1], gate[:, 0:1], ALU.add)
                for j in range(CT):
                    pool.indirect_dma_start(out=xg[:, i, j, :], out_offset=None, in_=xn3,
                                            in_offset=bass.IndirectOffsetOnAxis(now[:, i, j:j + 1], 0)).then_inc(ld_g[i], 16)

            def low(e, i):
                pool.wait_ge(s_dh, START + e + 1)
                pool.tensor_tensor(dl[:, i], rawd[:, i], dh[:, i].bitcast(F32), ALU.subtract).then_inc(s_dl, 1)

            def step(e, i, r):
                if not isinstance(e, int) or e < E - 1:
                    gather(e + 1, 1 - i, r + i)
                low(e, i)

            loop(pool, lambda: gather(0, 0, 0), step, nothing)

        def weight_parts(i):
            yield raw[:, i, :, :, 0:P], wh[:, i, :, 0:2, :], wl[:, i, :, 0:2, :]
            yield raw[:, i, :, :, P:I], *(w[:, i, :, 2, :].rearrange("p c (n f) -> p c n f", n=2) for w in (wh, wl))

        @block.scalar
        def _(act):
            def weights(e, i, r):
                act.wait_ge(ld_w[i], 32 * (r + 1))
                wait(act, s_gu, e - 1)
                for src, hi, _ in weight_parts(i):
                    act.activation(hi, src, ACT.Copy).then_inc(s_wh, 1)

            def down_weights(e, i, r):
                act.wait_ge(ld_d[i], 48 * (r + 1))
                wait(act, s_dn, 2 * e - 2)
                act.activation(dh[:, i], rawd[:, i], ACT.Copy).then_inc(s_dh, 1)

            def tokens(e, i):
                for j in range(CT):
                    act.wait_ge(s_xT, START + CT * e + j + 1)
                    act.activation(xh[:, i, :, j * P:(j + 1) * P], bx[j][:], ACT.Copy).then_inc(s_xh, 1)

            def inner(e, i):
                act.wait_ge(s_gu, START + e + 1)
                act.activation(sg[:, i, 0], ba[i][:, 0], ACT.Silu).then_inc(s_sg, 1)
                act.activation(sg[0:R, i, 1], bb[i][0:R], ACT.Silu).then_inc(s_sg, 1)

            def inner_high(e, i):
                act.wait_ge(s_h, START + 2 * e + 2)
                act.activation(hh[:, i, 0], h[:, i, 0], ACT.Copy).then_inc(s_hh, 1)
                act.activation(hh[0:R, i, 1], h[0:R, i, 1], ACT.Copy).then_inc(s_hh, 1)

            def store(e, i, r):
                act.wait_ge(s_dn, START + 2 * e + 1)
                wait(act, st_y[i][0], 16 * r)
                act.activation(y[:, i, 0], by[0][:], ACT.Copy).then_inc(s_yA, 1)

            def first():
                weights(0, 0, 0)
                down_weights(0, 0, 0)
                tokens(0, 0)

            def step(e, i, r):
                ahead = not isinstance(e, int) or e < E - 1
                if ahead:
                    weights(e + 1, 1 - i, r + i)
                inner(e, i)
                if ahead:
                    tokens(e + 1, 1 - i)
                inner_high(e, i)
                if not isinstance(e, int) or e > 0:
                    store(e - 1, 1 - i, r - 1 + i)
                if ahead:
                    down_weights(e + 1, 1 - i, r + i)

            loop(act, first, step, lambda: store(E - 1, 1, E // 2 - 1))

        @block.vector
        def _(dve):
            def weights(e, i):
                dve.wait_ge(s_wh, START + 2 * e + 2)
                for src, hi, lo in weight_parts(i):
                    dve.tensor_tensor(lo, src, hi.bitcast(F32), ALU.subtract).then_inc(s_wl, 1)

            def tokens(e, i):
                for j in range(CT):
                    dve.wait_ge(s_xh, START + CT * e + j + 1)
                    at = slice(j * P, (j + 1) * P)
                    dve.tensor_tensor(xl[:, i, :, at], bx[j][:], xh[:, i, :, at].bitcast(F32), ALU.subtract).then_inc(s_xl, 1)

            def inner(e, i):
                dve.wait_ge(s_sg, START + 2 * e + 2)
                dve.tensor_tensor(h[:, i, 0], ba[i][:, 1], sg[:, i, 0], ALU.mult).then_inc(s_h, 1)
                dve.tensor_tensor(h[0:R, i, 1], bb[i][R:2 * R], sg[0:R, i, 1], ALU.mult).then_inc(s_h, 1)

            def inner_low(e, i):
                dve.wait_ge(s_hh, START + 2 * e + 2)
                dve.tensor_tensor(hl[:, i], h[:, i, 0], hh[:, i, 0].bitcast(F32), ALU.subtract).then_inc(s_hl, 1)
                dve.tensor_tensor(hh[R:2 * R, i, 1], h[0:R, i, 1], hh[0:R, i, 1].bitcast(F32), ALU.subtract).then_inc(s_hl, 1)

            def store(e, i, r):
                dve.wait_ge(s_dn, START + 2 * e + 2)
                wait(dve, st_y[i][1], 16 * r)
                dve.tensor_copy(y[:, i, 1], by[1][:]).then_inc(s_yD, 1)

            def first():
                weights(0, 0)
                tokens(0, 0)

            def step(e, i, r):
                ahead = not isinstance(e, int) or e < E - 1
                if ahead:
                    weights(e + 1, 1 - i)
                inner(e, i)
                if ahead:
                    tokens(e + 1, 1 - i)
                inner_low(e, i)
                if not isinstance(e, int) or e > 0:
                    store(e - 1, 1 - i, r - 1 + i)

            loop(dve, first, step, lambda: store(E - 1, 1, E // 2 - 1))

        @block.tensor
        def _(pe):
            def turn(e, i, r):
                pe.wait_ge(ld_g[i], 16 * CT * (r + 1))
                for j in range(CT):
                    wait(pe, s_xl, CT * e + j - 1)
                    for c in range(C):
                        last = pe.transpose(bx[j][:, c, :], xg[:, i, j, c * P:(c + 1) * P], ident[:])
                    last.then_inc(s_xT, 1)

            def up(e, i):
                pe.wait_ge(s_wl, START + 2 * e + 2)
                pe.wait_ge(s_xl, START + CT * e + CT)
                wait(pe, s_h, 2 * e - 2)
                for n, out in enumerate((ba[i][:, 0], ba[i][:, 1], bb[i][:])):
                    last = product(pe, out, lambda c: wh[:, i, c, n], lambda c: wl[:, i, c, n], lambda c: xh[:, i, c],
                                   lambda c: xl[:, i, c], C)
                last.then_inc(s_gu, 1)

            def down(e, i):
                pe.wait_ge(s_dl, START + e + 1)
                pe.wait_ge(s_hl, START + 2 * e + 2)
                for j in range(CT):
                    wait(pe, (s_yA, s_yD)[j], e)
                    at = slice(j * P, (j + 1) * P)
                    product(pe, by[j][:], lambda c: hh[:, i, 0, at], lambda c: hl[:, i, at], lambda c: dh[:, i, 0],
                            lambda c: dl[:, i, 0], 1, stop=False)
                    pe.matmul(by[j][:], hh[:, i, 1, at], dh[:, i, 1], start=False, stop=False)
                    pe.matmul(by[j][:], hh[:, i, 1, at], dl[:, i, 1], start=False, stop=True).then_inc(s_dn, 1)

            def first():
                turn(0, 0, 0)

            def step(e, i, r):
                up(e, i)
                if not isinstance(e, int) or e < E - 1:
                    turn(e + 1, 1 - i, r + i)
                if not isinstance(e, int) or e > 0:
                    down(e - 1, 1 - i)

            loop(pe, first, step, lambda: down(E - 1, 1))


def combine(nc, slot, weight, x2, ybuf, out):
    with ExitStack() as ctx:
        m = Phase(nc, ctx, "co")
        xs = m.sb("x", [P, 2, D])
        yg = m.sb("y", [P, 2, TOPK, D])
        gate = m.sb("gate", [P, 5])
        now = m.sb("now", [P, 2, TOPK], I32)
        s_g, s_now = m.sem("gate"), m.sem("now")
        ld_x = [m.sem(f"ld_x{i}") for i in range(2)]
        ld_y = [m.sem(f"ld_y{i}") for i in range(2)]
        st = [m.sem(f"st{i}") for i in range(2)]
        s_acc = [m.sem(f"acc{i}") for i in range(2)]
        counters = st + s_acc
        with nc.Block() as block:
            @block.sync
            def _(sp):
                for c in counters:
                    sp.sem_inc(c, START)

            @block.gpsimd
            def _(pool):
                pool.memset(gate[:], 0.0).then_inc(s_g, 1)
                pool.wait_ge(s_g, 1)

        block = m.main_block()

        @block.sync
        def _(sp):
            with sp.Fori(0, NT // 2) as r:
                for i in range(2):
                    sp.wait_ge(st[i], START + 16 * r)
                    sp.dma_start(xs[:, i], x2[bass.ds(2 * r + i, 1)].rearrange("a p d -> (a p) d")).then_inc(ld_x[i], 16)
                for i in range(2):
                    sp.wait_ge(s_acc[i], START + TOPK * (r + 1))
                    sp.dma_start(out[bass.ds(2 * r + i, 1)].rearrange("a p d -> (a p) d"), xs[:, i]).then_inc(st[i], 16)
            for i in range(2):
                sp.wait_ge(st[i], START + 16 * NT // 2)

        @block.gpsimd
        def _(pool):
            with pool.Fori(0, NT // 2) as r:
                for i in range(2):
                    pool.wait_ge(s_acc[i], START + TOPK * r)
                    pool.tensor_tensor(gate[:, 1 + i:2 + i], gate[:, 0:1], gate[:, 0:1], ALU.add)
                    pool.tensor_copy(now[:, i], slot[:, bass.ds((2 * r + i) * TOPK, TOPK)]).then_inc(s_now, 1)
                    pool.wait_ge(s_now, 2 * r + i + 1)
                    pool.tensor_tensor(gate[:, 3 + i:4 + i], gate[:, 0:1], gate[:, 0:1], ALU.add)
                    for k in range(TOPK):
                        pool.indirect_dma_start(
                            out=yg[:, i, k, :], out_offset=None, in_=ybuf,
                            in_offset=bass.IndirectOffsetOnAxis(now[:, i, k:k + 1], 0)).then_inc(ld_y[i], 16)

        @block.vector
        def _(dve):
            with dve.Fori(0, NT // 2) as r:
                for i in range(2):
                    dve.wait_ge(ld_x[i], 16 * (r + 1))
                    dve.wait_ge(ld_y[i], 16 * TOPK * (r + 1))
                    for k in range(TOPK):
                        if k:
                            dve.wait_ge(s_acc[i], START + TOPK * r + k)
                        dve.scalar_tensor_tensor(xs[:, i], yg[:, i, k], weight[:, bass.ds((2 * r + i) * TOPK + k, 1)],
                                                 xs[:, i], ALU.mult, ALU.add).then_inc(s_acc[i], 1)


def decoder_layer(nc, consts, x, context, w_qkv, w_out, b_out, wq, wk, wv, w_router, w_gate, w_up, w_down, out):
    def tiles(a):
        return a.rearrange("b (t p) d -> (b t) p d", p=P)

    x1 = nc.dram_tensor("x1", (NT, P, D), F32).ap()
    x2 = nc.dram_tensor("x2", (NT, P, D), F32).ap()
    xn3 = nc.dram_tensor("xn3", (NT, P, D), F32).ap()
    slots = nc.dram_tensor("slots", (E * CAP, 1), I32).ap()
    ybuf = nc.dram_tensor("ybuf", (E * CAP + 1, D), F32).ap()
    self_attention(nc, consts, tiles(x), w_qkv, w_out, b_out, x1)
    with nc.sbuf_tensor("logits", [P, NT, E], F32) as logits:
        cross_attention(nc, consts, tiles(context), wq, wk, wv, w_router, x1, x2, xn3, logits)
        with nc.sbuf_tensor("slot", [P, NT * TOPK], I32) as slot, nc.sbuf_tensor("weight", [P, NT * TOPK], F32) as weight, \
                nc.sbuf_tensor("token", [P, E * CT], I32) as token:
            route(nc, consts, logits, slot, weight, token, slots, ybuf)
            experts(nc, consts, token, xn3.rearrange("n p d -> (n p) d"), w_gate, w_up, w_down, ybuf)
            combine(nc, slot, weight, x2, ybuf, tiles(out))


def constants():
    import numpy as np

    i = np.arange(P)
    k = np.zeros((P, K_COLS), np.float32)
    k[:, K_IDENT:K_IDENT + P] = np.eye(P)
    k[:, K_TRI:K_TRI + P] = i[:, None] < i[None, :]
    own = np.where(i[None, :] <= i[:, None], 0.0, MASKED)
    past = np.where(i[None, :] >= i[:, None], 0.0, MASKED)
    none = np.full((P, P), MASKED)
    for n, pair in enumerate(((own, past), (past, own), (own, none))):
        k[:, K_MASK + n * 2 * P:K_MASK + (n + 1) * 2 * P] = np.concatenate(pair, 1)
    inv_freq = (1.0 / np.float32(10000.0) ** (np.arange(0, D1, 2, dtype=np.float32) / np.float32(D1))).astype(np.float32)
    angles = np.repeat(np.arange(S, dtype=np.float32)[:, None] * inv_freq[None, :], 2, axis=-1)
    sign = np.where(np.arange(D1) % 2 == 0, -1.0, 1.0)
    cos, sin = np.cos(angles), np.sin(angles) * sign
    scale = D1 ** -0.5
    for n, table in enumerate((cos * scale, sin * scale, cos, sin)):
        at = K_ROPE + n * T * D1
        k[:, at:at + T * D1] = table.reshape(T, P, D1).transpose(1, 0, 2).reshape(P, T * D1)
    k[:, K_IOTA:K_IOTA + E] = np.arange(E)
    k[:, K_TOK:K_TOK + NT] = i[:, None] + P * np.arange(NT)
    return k


_INS = ["x", "ctx_2048", "L0_attn_W_qkv", "L0_attn_W_out", "L0_attn_b_out", "L0_xattn_Wq", "L0_xattn_Wk", "L0_xattn_Wv",
        "L0_ffn_router_weight", "L0_ffn_gate_proj", "L0_ffn_up_proj", "L0_ffn_down_proj"]


def kernel(**inputs):
    import numpy as np
    import concourse.bacc as bacc
    from concourse.bass_utils import run_bass_kernel_spmd

    nc = bacc.Bacc("TRN2", target_bir_lowering=False, num_devices=1)
    arrays, args = {"consts_dram": constants()}, []
    for name in _INS:
        arrays[f"in_{name}_dram"] = np.ascontiguousarray(inputs[name])
    for name, a in arrays.items():
        args.append(nc.dram_tensor(name, a.shape, mybir.dt.from_np(a.dtype), kind="ExternalInput").ap())
    out = nc.dram_tensor("out_0_dram", (B, S, D), F32, kind="ExternalOutput").ap()
    decoder_layer(nc, *args, out)
    r = run_bass_kernel_spmd(nc, [arrays], core_ids=[0])
    return r.results[0]["out_0_dram"]
```

```python
from contextlib import ExitStack

import concourse.bass as bass
from concourse import mybir

F32 = mybir.dt.float32
F32R = mybir.dt.float32r
BF16 = mybir.dt.bfloat16
I32 = mybir.dt.int32
U32 = mybir.dt.uint32
ALU = mybir.AluOpType
ACT = mybir.ActivationFunctionType
AX = mybir.AxisListType

P = 128
B, S, D = 4, 512, 512
T = S // P
NT = B * T
C = D // P
H1, D1 = 16, 32
H2, D2 = 32, 16
E, I, TOPK = 64, 192, 8
CAP = 256
CT = CAP // P
LN_EPS, RMS_EPS = 1e-5, 1e-6
MASKED = -1e30

START = 2

K_IDENT, K_TRI, K_MASK, K_ROPE = 0, 128, 256, 256 + 3 * 256
K_IOTA = K_ROPE + 4 * T * D1
K_TOK = K_IOTA + P
K_COLS = K_TOK + NT


class Phase:

    def __init__(self, nc, ctx, tag):
        self.nc, self.ctx, self.tag, self.sems = nc, ctx, tag, []

    def sb(self, name, shape, dt=F32):
        return self.ctx.enter_context(self.nc.sbuf_tensor(f"{self.tag}_{name}", shape, dt))

    def ps(self, name, shape, dt=F32):
        return self.ctx.enter_context(self.nc.psum_tensor(f"{self.tag}_{name}", shape, dt))

    def sem(self, name):
        self.sems.append(self.ctx.enter_context(self.nc.semaphore(f"{self.tag}_{name}")))
        return self.sems[-1]

    def main_block(self):
        self.ctx.callback(self.clear)
        return self.ctx.enter_context(self.nc.Block())

    def clear(self):
        with self.nc.Block() as block:
            @block.sync
            def _(sp):
                for s in self.sems:
                    sp.sem_clear(s)


def product(pe, out, hi_l, lo_l, hi_r, lo_r, chunks, part=None, stop=True):
    for c in part or range(chunks):
        pe.matmul(out, hi_l(c), hi_r(c), start=(c == 0), stop=False)
        pe.matmul(out, hi_l(c), lo_r(c), start=False, stop=False)
        last = pe.matmul(out, lo_l(c), hi_r(c), start=False, stop=(stop and c == chunks - 1))
    return last


def self_attention(nc, consts, ident, prefetch, x, w_qkv, w_out, b_out, x1):
    with ExitStack() as ctx:
        m = Phase(nc, ctx, "sa")
        identb = m.sb("identb", [P, P], BF16)
        mask = m.sb("mask", [P, 3, 2 * P], BF16)
        rope = m.sb("rope", [P, 4, T, D1])
        bias = m.sb("bias", [P, D])
        wh = m.sb("wh", [P, C, 3, D], F32R)
        wl = m.sb("wl", [P, C, 3, D], F32R)
        oh = m.sb("oh", [P, C, D], F32R)
        ol = m.sb("ol", [P, C, D], F32R)
        xs = m.sb("x", [P, T, D])
        half = m.sb("half", [P, 1])
        eps = m.sb("eps", [P, 1])
        kT = m.sb("kT", [3 * D1, H1, 2, P], F32R)
        v = m.sb("v", [P, T, H1, D1])

        ld_x = [m.sem(f"ld_x{t}") for t in range(T)]
        st_x = [m.sem(f"st_x{t}") for t in range(T)]
        (s_gate, s_bst, s_mv, s_ve, s_rs, s_xn, s_xT, s_xh, s_xl, s_q, s_k, s_v, s_t, s_r, s_hi, s_lo, s_vv, s_qt, s_kt,
         s_qe, s_ke, s_mx, s_ri, s_pn, s_pv, s_oh, s_ol, s_op, s_x1, s_x1b) = [m.sem(n) for n in (
             "gate bst mv ve rs xn xT xh xl q k v t r hi lo vv qt kt qe ke mx ri pn pv oh ol op x1 x1b").split()]
        s_sc, s_ex, s_pt, s_pe = [[m.sem(f"{name}{i}") for i in range(2)] for name in ("sc", "ex", "pt", "pe")]
        counters = [s_gate, s_bst, s_mv, s_ve, s_rs, s_xn, s_xT, s_xh, s_xl, s_q, s_k, s_v, s_t, s_r, s_hi, s_lo, s_vv,
                    s_qt, s_kt, s_qe, s_ke, s_mx, s_ri, s_pn, s_pv, s_oh, s_ol, s_op, s_x1, s_x1b]
        counters += st_x + s_sc + s_ex + s_pt + s_pe

        with ExitStack() as c2, nc.Block() as block:
            s = Phase(nc, c2, "sw")
            raw = s.sb("raw", [P, C, 3 * D])
            maskf = s.sb("maskf", [P, 3, 2 * P])
            raw_out = s.sb("raw_out", [P, C, D])
            s_c, s_cb = s.sem("const"), s.sem("cast")
            s_w = [s.sem(f"raw{i}") for i in range(C + 1)]
            s_z = s.sem("zero")
            w_hi, w_lo = s.sem("hi"), s.sem("lo")
            c2.callback(s.clear)

            @block.sync
            def _(sp):
                for counter in counters:
                    sp.sem_inc(counter, START)
                for c in range(C):
                    sp.dma_start(raw[:, c, :], w_qkv[c * P:(c + 1) * P, :]).then_inc(s_w[c], 16)
                sp.dma_start(xs[:, 0], x[0]).then_inc(ld_x[0], 16)
                sp.dma_start(raw_out[:], w_out.rearrange("(c p) d -> p c d", p=P)).then_inc(s_w[C], 16)
                for t in range(1, T):
                    sp.dma_start(xs[:, t], x[t]).then_inc(ld_x[t], 16)
                prefetch(sp)
                sp.wait_ge(s_c, 64)

            @block.gpsimd
            def _(pool):
                pool.memset(half[:], -0.5).then_inc(s_z, 1)
                pool.memset(eps[:], LN_EPS).then_inc(s_z, 1)
                pool.memset(kT[:].bitcast(F32), 0.0).then_inc(s_z, 1)
                pool.memset(v[:], 0.0).then_inc(s_z, 1)
                pool.wait_ge(s_z, 4)

            def parts(c):
                if c < C:
                    return raw[:, c, :].rearrange("p (f t) -> p t f", t=3), wh[:, c], wl[:, c]
                return raw_out[:], oh[:], ol[:]

            @block.scalar
            def _(act):
                act.dma_start(ident[:], consts[:, K_IDENT:K_IDENT + P]).then_inc(s_c, 16)
                act.dma_start(maskf[:].rearrange("p a b -> p (a b)"), consts[:, K_MASK:K_MASK + 768]).then_inc(s_c, 16)
                act.dma_start(rope[:].rearrange("p a b c -> p (a b c)"),
                              consts[:, K_ROPE:K_ROPE + 4 * T * D1]).then_inc(s_c, 16)
                act.dma_start(bias[:], b_out.rearrange("(a n) -> a n", a=1).to_broadcast([P, D])).then_inc(s_c, 16)
                for c in range(C + 1):
                    src, hi, lo = parts(c)
                    act.wait_ge(s_w[c], 16)
                    act.activation(hi, src, ACT.Copy).then_inc(w_hi, 1)

            @block.vector
            def _(dve):
                dve.wait_ge(s_c, 64)
                dve.tensor_copy(identb[:], ident[:]).then_inc(s_cb, 1)
                dve.tensor_copy(mask[:], maskf[:]).then_inc(s_cb, 1)
                for c in range(C + 1):
                    src, hi, lo = parts(c)
                    dve.wait_ge(w_hi, c + 1)
                    dve.tensor_tensor(lo, src, hi.bitcast(F32), ALU.subtract).then_inc(w_lo, 1)

        st6 = m.sb("st6", [P, T, 6])
        mv = m.sb("mv", [P, T, 2])
        ve = m.sb("ve", [P, T])
        gate = m.sb("gate", [P, 1])
        rstd = m.sb("rstd", [P, T])
        xn = m.sb("xn", [P, D])
        xh = m.sb("xh", [P, C, P], F32R)
        xl = m.sb("xl", [P, C, P], F32R)
        t1 = m.sb("t1", [P, 2, D])
        t2 = m.sb("t2", [P, 2, D])
        rot = m.sb("rot", [P, 2, D])
        stack = m.sb("stack", [P, 2, 2, H1, 3 * D1], F32R)
        qT = m.sb("qT", [3 * D1, H1, P], F32R)
        prob = m.sb("prob", [P, H1, 2 * P])
        nmax = m.sb("nmax", [P, H1])
        rsum = m.sb("rsum", [P, H1])
        rinv = m.sb("rinv", [P, H1])
        pT = m.sb("pT", [P, 2, 4, P])
        oTh = m.sb("oTh", [P, C, P], F32R)
        oTl = m.sb("oTl", [P, C, P], F32R)

        out_ps = m.ps("out_ps", [P, C, P])
        pr_ps = [m.ps(f"pr_ps{i}", [P, D]) for i in range(2)]
        xT_ps = m.ps("xT_ps", [P, C, P])
        tn_ps = [m.ps(f"tn_ps{i}", [P, 4, P]) for i in range(2)]
        sc_ps = [m.ps(f"sc_ps{i}", [P, 2, 2 * P]) for i in range(2)]

        class Tile:

            def __init__(self, b, t):
                self.b, self.t = (b + t // T if t // T else b), t % T
                self.n = self.b * T + self.t

            def k(self, g):
                return 4 * self.n + g

            def ahead(self, i):
                return Tile(self.b, self.t + i)

            def exists(self):
                return not isinstance(self.n, int) or 0 <= self.n < NT

        def tiles(engine, tile):
            tile(Tile(0, 0))
            with engine.Fori(0, B - 1) as b:
                for i in range(1, T + 1):
                    tile(Tile(b, i))
            for i in range(1, T):
                tile(Tile(B - 1, i))


        block = m.main_block()

        @block.sync
        def _(sp):
            def load(b, t):
                sp.dma_start(xs[:, t], x[bass.ds(b * T + t, 1), :, :].rearrange("a p d -> (a p) d")).then_inc(ld_x[t], 16)

            def store(b, t):
                sp.wait_ge(s_x1b, START + b * T + t + 1)
                sp.dma_start(x1[bass.ds(b * T + t, 1), :, :].rearrange("a p d -> (a p) d"), xs[:, t]).then_inc(st_x[t], 16)

            with sp.Fori(0, B - 1) as b:
                for t in range(T):
                    store(b, t)
                    sp.wait_ge(st_x[t], START + b * 16 + 16)
                    load(b + 1, t)
            for t in range(T):
                store(B - 1, t)
            for t in range(T):
                sp.wait_ge(st_x[t], START + 16 * B)

        @block.gpsimd
        def _(pool):
            def deviation(at):
                n, t = at.n, at.t
                pool.wait_ge(s_mv, START + n + 1)
                pool.tensor_tensor(ve[:, t:t + 1], mv[:, t, 1:2], eps[:], ALU.add).then_inc(s_ve, 1)
                pool.wait_ge(s_ve, START + n + 1)
                pool.tensor_tensor(rstd[:, t:t + 1], ve[:, t:t + 1], half[:], ALU.pow).then_inc(s_rs, 1)

            def rotate(at, i):
                n = at.n
                pool.wait_ge(s_t, START + 4 * n + 2 * i + 2)
                if not isinstance(n, int) or n > 0:
                    pool.wait_ge(s_lo, START + 2 * n + i - 1)
                pool.tensor_tensor(rot[:, i], t1[:, i], t2[:, i], ALU.add).then_inc(s_r, 1)

            def add_bias(at):
                pool.wait_ge(s_x1, START + at.n + 1)
                pool.tensor_tensor(xs[:, at.t], xs[:, at.t], bias[:], ALU.add).then_inc(s_x1b, 1)

            def tile(at):
                for g in range(4):
                    if g == 2 and at.ahead(2).exists():
                        deviation(at.ahead(2))
                    pool.wait_ge(s_ri, START + at.k(g) + 1)
                    pool.tensor_tensor(prob[:, 4 * g:4 * g + 4, :], prob[:, 4 * g:4 * g + 4, :],
                                       rinv[:, 4 * g:4 * g + 4].unsqueeze(2).to_broadcast([P, 4, 2 * P]),
                                       ALU.mult).then_inc(s_pn, 1)
                    if g in (1, 2) and at.ahead(1).exists():
                        rotate(at.ahead(1), g - 1)
                    if g == 3 and at.ahead(-1).exists():
                        add_bias(at.ahead(-1))

            deviation(Tile(0, 0))
            deviation(Tile(0, 1))
            rotate(Tile(0, 0), 0)
            rotate(Tile(0, 0), 1)
            tiles(pool, tile)
            add_bias(Tile(B - 1, T - 1))

        @block.scalar
        def _(act):
            def high_x(at):
                act.wait_ge(s_xT, START + at.n + 1)
                act.activation(xh[:], xT_ps[:], ACT.Copy).then_inc(s_xh, 1)

            def high_qk(at, i):
                n = at.n
                act.wait_ge(s_r, START + 2 * n + i + 1)
                both = stack[:, at.t % 2, i].rearrange("p h (r d) -> p h r d", r=3)
                act.activation(both[:, :, 0:2, :] if i == 0 else both[:, :, 0:3:2, :],
                               rot[:, i].rearrange("p (h d) -> p h d", h=H1).unsqueeze(2).to_broadcast([P, H1, 2, D1]),
                               ACT.Copy).then_inc(s_hi, 1)

            def take_v(at):
                act.wait_ge(s_v, START + at.n + 1)
                act.activation(v[:, at.t].rearrange("p h d -> p (h d)"), pr_ps[0][:], ACT.Copy).then_inc(s_vv, 1)

            def take_q(at, g):
                act.wait_ge(s_qt, START + at.k(g) + 1)
                act.activation(qT[:, 4 * g:4 * g + 4, :], tn_ps[0][0:3 * D1], ACT.Copy).then_inc(s_qe, 1)

            def take_prob(at, g):
                act.wait_ge(s_pt[0], START + at.k(g) + 1)
                act.activation(pT[:, 0], tn_ps[0][:], ACT.Copy).then_inc(s_pe[0], 1)

            def high_out(at):
                act.wait_ge(s_pv, START + at.k(3) + 1)
                if at.ahead(-1).exists():
                    act.wait_ge(s_op, START + at.n)
                act.activation(oTh[:], out_ps[:], ACT.Copy).then_inc(s_oh, 1)

            def tile(at):
                last, nxt = at.ahead(-1), at.ahead(1)
                for g in range(4):
                    if g == 1 and last.exists():
                        high_out(last)
                    if g == 3 and nxt.exists():
                        high_qk(nxt, 1)
                    for p in range(2):
                        act.wait_ge(s_mx, START + 2 * at.k(g) + p + 1)
                        for i in range(2):
                            h = 4 * g + 2 * p + i
                            act.activation(prob[:, h, :], sc_ps[p][:, i, :], ACT.Exp, bias=nmax[:, h:h + 1],
                                           accum_out=rsum[:, h:h + 1]).then_inc(s_ex[p], 1)
                    if g > 0:
                        take_prob(at, g - 1)
                    elif last.exists():
                        take_prob(last, 3)
                    if g == 2 and nxt.exists():
                        high_qk(nxt, 0)
                    if g == 3 and at.ahead(2).exists():
                        high_x(at.ahead(2))
                    if g < 3:
                        take_q(at, g + 1)
                    elif nxt.exists():
                        take_q(nxt, 0)
                        take_v(nxt)

            high_x(Tile(0, 0))
            high_qk(Tile(0, 0), 0)
            high_qk(Tile(0, 0), 1)
            take_v(Tile(0, 0))
            high_x(Tile(0, 1))
            take_q(Tile(0, 0), 0)
            tiles(act, tile)
            take_prob(Tile(B - 1, T - 1), 3)
            high_out(Tile(B - 1, T - 1))

        @block.vector
        def _(dve):
            def swapped(ps):
                return ps[:].rearrange("p (h i c) -> p h i c", h=H1, c=2)[:, :, :, ::-1]

            def moments(at):
                n, t = at.n, at.t
                dve.wait_ge(ld_x[t], at.b * 16 + 16)
                dve.bn_stats(st6[:, t], xs[:, t]).then_inc(s_bst, 1)
                dve.wait_ge(s_bst, START + n + 1)
                dve.tensor_copy(gate[:], st6[:, t, 0:1]).then_inc(s_gate, 1)
                dve.bn_aggr(mv[:, t], st6[:, t]).then_inc(s_mv, 1)

            def normalise(at):
                n, t = at.n, at.t
                dve.wait_ge(s_rs, START + n + 1)
                if at.ahead(-1).exists():
                    dve.wait_ge(s_xT, START + n)
                dve.tensor_scalar(xn[:], xs[:, t], mv[:, t, 0:1], rstd[:, t:t + 1], ALU.subtract,
                                  ALU.mult).then_inc(s_xn, 1)

            def low_x(at):
                dve.wait_ge(s_xh, START + at.n + 1)
                dve.tensor_tensor(xl[:], xT_ps[:], xh[:].bitcast(F32), ALU.subtract).then_inc(s_xl, 1)

            def rotate(at, i):
                n, t = at.n, at.t
                dve.wait_ge((s_q, s_k)[i], START + n + 1)
                if at.ahead(-1).exists():
                    dve.wait_ge(s_r, START + 2 * n + i - 1)
                cos, sin = (rope[:, 2 * i + j, t] for j in range(2))
                dve.tensor_tensor(t1[:, i].rearrange("p (h d) -> p h d", h=H1),
                                  pr_ps[i][:].rearrange("p (h d) -> p h d", h=H1),
                                  cos.unsqueeze(1).to_broadcast([P, H1, D1]), ALU.mult).then_inc(s_t, 1)
                dve.tensor_tensor(t2[:, i].rearrange("p (h i c) -> p h i c", h=H1, c=2), swapped(pr_ps[i]),
                                  sin.rearrange("p (i c) -> p i c", c=2).unsqueeze(1).to_broadcast([P, H1, D1 // 2, 2]),
                                  ALU.mult).then_inc(s_t, 1)

            def low_qk(at, i):
                dve.wait_ge(s_hi, START + 2 * at.n + i + 1)
                both = stack[:, at.t % 2, i]
                dve.tensor_tensor(both[:, :, (2 - i) * D1:(3 - i) * D1], rot[:, i].rearrange("p (h d) -> p h d", h=H1),
                                  both[:, :, 0:D1].bitcast(F32), ALU.subtract).then_inc(s_lo, 1)

            def take_k(at, g):
                dve.wait_ge(s_kt, START + at.k(g) + 1)
                dve.tensor_copy(kT[:, 4 * g:4 * g + 4, at.t % 2, :], tn_ps[1][0:3 * D1]).then_inc(s_ke, 1)

            def take_prob(at, g):
                dve.wait_ge(s_pt[1], START + at.k(g) + 1)
                dve.tensor_copy(pT[:, 1], tn_ps[1][:]).then_inc(s_pe[1], 1)

            def low_out(at):
                dve.wait_ge(s_oh, START + at.n + 1)
                dve.tensor_tensor(oTl[:], out_ps[:], oTh[:].bitcast(F32), ALU.subtract).then_inc(s_ol, 1)

            def residual(at):
                dve.wait_ge(s_op, START + at.n + 1)
                dve.tensor_tensor(xs[:, at.t], pr_ps[1][:], xs[:, at.t], ALU.add).then_inc(s_x1, 1)

            def tile(at):
                last, nxt = at.ahead(-1), at.ahead(1)
                for g in range(4):
                    for p in range(2):
                        dve.wait_ge(s_sc[p], START + at.k(g) + 1)
                        h = 4 * g + 2 * p
                        dve.tensor_reduce(nmax[:, h:h + 2], sc_ps[p][:], AX.X, ALU.max, negate=True).then_inc(s_mx, 1)
                    if g == 1 and last.exists():
                        low_out(last)
                    if g > 0:
                        take_prob(at, g - 1)
                    elif last.exists():
                        take_prob(last, 3)
                    if g in (1, 2) and nxt.exists():
                        rotate(nxt, g - 1)
                    if g == 3 and nxt.exists():
                        low_qk(nxt, 1)
                    for i in range(2):
                        dve.wait_ge(s_ex[i], START + 2 * at.k(g) + 2)
                    dve.reciprocal(rinv[:, 4 * g:4 * g + 4], rsum[:, 4 * g:4 * g + 4]).then_inc(s_ri, 1)
                    if g == 2 and nxt.exists():
                        low_qk(nxt, 0)
                    if g == 1 and at.ahead(2).exists():
                        moments(at.ahead(2))
                    if g == 2 and at.ahead(2).exists():
                        normalise(at.ahead(2))
                    if g == 3 and at.ahead(2).exists():
                        low_x(at.ahead(2))
                    if g < 3:
                        take_k(at, g + 1)
                    elif nxt.exists():
                        take_k(nxt, 0)
                    if g == 3 and last.exists():
                        residual(last)

            first, second = Tile(0, 0), Tile(0, 1)
            moments(first)
            moments(second)
            normalise(first)
            low_x(first)
            rotate(first, 0)
            rotate(first, 1)
            normalise(second)
            low_qk(first, 0)
            low_qk(first, 1)
            low_x(second)
            take_k(first, 0)
            tiles(dve, tile)
            end = Tile(B - 1, T - 1)
            take_prob(end, 3)
            low_out(end)
            residual(end)

        @block.tensor
        def _(pe):
            def turn_x(at):
                n = at.n
                pe.wait_ge(s_xn, START + n + 1)
                if at.ahead(-1).exists():
                    pe.wait_ge(s_xh, START + n)
                    pe.wait_ge(s_xl, START + n)
                for c in range(C):
                    done = pe.transpose(xT_ps[:, c, :], xn[:, c * P:(c + 1) * P], ident[:])
                done.then_inc(s_xT, 1)

            def project(at, i, part=range(C)):
                n = at.n
                starts = part[0] == 0
                if starts and i == 0:
                    pe.wait_ge(s_xh, START + n + 1)
                    pe.wait_ge(s_xl, START + n + 1)
                    if at.ahead(-1).exists():
                        pe.wait_ge(s_vv, START + n)
                if starts and i == 1 and at.ahead(-2).exists():
                    pe.wait_ge(s_x1, START + n - 2)
                if starts and i == 2:
                    pe.wait_ge(s_t, START + 4 * n + 2)
                last = product(pe, pr_ps[i % 2][:], lambda c: xh[:, c], lambda c: xl[:, c], lambda c: wh[:, c, i],
                               lambda c: wl[:, c, i], C, part)
                if part[-1] == C - 1:
                    last.then_inc((s_q, s_k, s_v)[i], 1)

            def project_out(at, part=range(C)):
                n = at.n
                if part[0] == 0:
                    pe.wait_ge(s_oh, START + n + 1)
                    pe.wait_ge(s_ol, START + n + 1)
                    k_read = 4 * (n + 3)
                    if isinstance(n, int) and n + 2 >= NT:
                        k_read = 4 * NT
                        pe.wait_ge(s_x1, START + n)
                    pe.wait_ge(s_t, START + k_read)
                last = product(pe, pr_ps[1][:], lambda c: oTh[:, c], lambda c: oTl[:, c], lambda c: oh[:, c],
                               lambda c: ol[:, c], C, part)
                if part[-1] == C - 1:
                    last.then_inc(s_op, 1)

            def turn_heads(at, g):
                n, k = at.n, at.k(g)
                for i in range(2):
                    if g == 0:
                        pe.wait_ge(s_hi, START + 2 * n + i + 1)
                        pe.wait_ge(s_lo, START + 2 * n + i + 1)
                    if not isinstance(k, int) or k > 0:
                        pe.wait_ge((s_qe, s_ke)[i], START + k)
                        if not isinstance(k, int) or k > 1:
                            pe.wait_ge(s_pe[i], START + k - 1)
                    for j in range(4):
                        done = pe.transpose(tn_ps[i][0:3 * D1, j, :], stack[:, at.t % 2, i, 4 * g + j, :].bitcast(F32),
                                            ident[:])
                    done.then_inc((s_qt, s_kt)[i], 1)

            def turn_prob(at, g):
                k = at.k(g)
                pe.wait_ge(s_pn, START + k + 1)
                heads_read = k + 2
                if isinstance(k, int):
                    heads_read = min(heads_read, 4 * NT)
                for i in range(2):
                    pe.wait_ge((s_qe, s_ke)[i], START + heads_read)
                    for j in range(4):
                        done = pe.transpose(tn_ps[i][:, j, :], prob[:, 4 * g + j, i * P:(i + 1) * P], ident[:])
                    done.then_inc(s_pt[i], 1)

            def values(at, g):
                k = at.k(g)
                if g == 0:
                    pe.wait_ge(s_vv, START + at.n + 1)
                    if at.ahead(-1).exists():
                        pe.wait_ge(s_oh, START + at.n)
                        pe.wait_ge(s_ol, START + at.n)
                for i in range(2):
                    pe.wait_ge(s_pe[i], START + k + 1)
                    keys = at.t if i == at.t % 2 else (at.t - 1) % T
                    for j in range(4):
                        done = pe.matmul(out_ps[32 * j:32 * j + 32, g, :], v[:, keys, 4 * g + j, :], pT[:, i, j, :],
                                         start=(i == 0), stop=(i == 1))
                done.then_inc(s_pv, 1)

            def scores(at, g):
                k = at.k(g)
                kind = 2 if at.t == 0 else at.t % 2
                pe.wait_ge(s_qe, START + k + 1)
                pe.wait_ge(s_ke, START + k + 1)
                for p in range(2):
                    if not isinstance(k, int) or k > 0:
                        pe.wait_ge(s_ex[p], START + 2 * k)
                    pe.matmul(sc_ps[p][:], identb[:], mask[:, kind].unsqueeze(1).to_broadcast([P, 2, 2 * P]), start=True,
                              stop=False)
                    for i in range(2):
                        h = 4 * g + 2 * p + i
                        done = pe.matmul(sc_ps[p][:, i, :], qT[:, h, :], kT[:, h].rearrange("p a b -> p (a b)"),
                                         start=False, stop=(i == 1))
                    done.then_inc(s_sc[p], 1)

            def tile(at):
                last, nxt = at.ahead(-1), at.ahead(1)
                for g in range(4):
                    before = (at, g - 1) if g > 0 else (last, 3)
                    after = (at, g + 1) if g < 3 else (nxt, 0)
                    scores(at, g)
                    if before[0].exists():
                        turn_prob(*before)
                    if g == 3 and at.ahead(2).exists():
                        turn_x(at.ahead(2))
                    for part in (range(C - 1), range(C - 1, C)):
                        if g < 3 and nxt.exists():
                            project(nxt, g, part)
                        if g == 3 and last.exists():
                            project_out(last, part)
                        if part[0] == 0 and after[0].exists():
                            turn_heads(*after)
                    if before[0].exists():
                        values(*before)

            first = Tile(0, 0)
            turn_x(first)
            for i in range(3):
                project(first, i)
            turn_x(first.ahead(1))
            turn_heads(first, 0)
            tiles(pe, tile)
            end = Tile(B - 1, T - 1)
            turn_prob(end, 3)
            values(end, 3)
            project_out(end)


def cross_attention(nc, ident, stage, w_w, context, w_router, x1, x2, xn3, logits):
    W2 = 4 * D2
    PAIRS = H2 // 2
    G = H2 // 4
    with ExitStack() as ctx:
        m = Phase(nc, ctx, "xa")
        wh = m.sb("wh", [P, 3, C, D], F32R)
        wl = m.sb("wl", [P, 3, C, D], F32R)
        rh = m.sb("rh", [P, C, E], F32R)
        rl = m.sb("rl", [P, C, E], F32R)
        kT = m.sb("kT", [P, PAIRS, 2, S], F32R)
        v = m.sb("v", [P, T, H2, D2 + 1])
        out_ps = m.ps("out", [P, S])
        b0 = m.ps("b0", [P, C, P])
        ring = [m.ps(f"ring{i}", [P, 2, D]) for i in range(3)]

        ld_x = [m.sem(f"ld_x{t}") for t in range(T)]
        ld_c = [m.sem(f"ld_c{t}") for t in range(T)]
        st_x = [m.sem(f"st_x{t}") for t in range(T)]
        st_n = [m.sem(f"st_n{i}") for i in range(2)]
        counters = []

        def counter(name):
            counters.append(m.sem(name))
            return counters[-1]

        s_gate, s_bst, s_mv, s_ve, s_rs, s_xn = [counter(n) for n in "gate bst mv ve rs xn".split()]
        s_xT, s_xh, s_xl, s_pr, s_sq, s_ss, s_ms, s_im, s_y0 = [counter(n) for n in "xT xh xl pr sq ss ms im y0".split()]
        s_rT, s_rh, s_rl, s_rp = [counter(n) for n in "rT rh rl rp".split()]
        s_yy, s_my, s_rr = [counter(n) for n in "yy my rr".split()]
        s_kn, s_hi, s_lo, s_vv, s_tr, s_eA, s_eD, s_lg = [counter(n) for n in "kn hi lo vv tr eA eD lg".split()]
        s_sc = [counter(f"sc{i}") for i in range(3)]
        s_ex = [counter(f"ex{i}") for i in range(3)]
        s_pv, s_ot, s_tt, s_ri, s_sm, s_x2 = [counter(n) for n in "pv ot tt ri sm x2".split()]
        counters += st_x + st_n

        with ExitStack() as c2, nc.Block() as block:
            s = Phase(nc, c2, "xw")
            raw = stage[:].rearrange("p (i c d) -> p i c d", i=3, c=C)
            rr = s.sb("router", [P, C, E])
            w_r, w_t, w_hi, w_lo, w_zo = [s.sem(n) for n in "router turned hi lo zero_out".split()]
            banks = [ring[i // 2][:, i % 2] for i in range(4)]
            c2.callback(s.clear)

            @block.sync
            def _(sp):
                for c in counters:
                    sp.sem_inc(c, START)
                sp.dma_start(rr[:], w_router.rearrange("(c p) e -> p c e", p=P)).then_inc(w_r, 16)

            @block.tensor
            def _(pe):
                for n in range(3 * C):
                    i, c = n // C, n % C
                    if c == 0:
                        pe.wait_ge(w_w[i], 16)
                    if n >= len(banks):
                        pe.wait_ge(w_lo, n - len(banks) + 1)
                    for f in range(C):
                        last = pe.transpose(banks[n % len(banks)][:, f * P:(f + 1) * P], raw[:, i, f, c * P:(c + 1) * P], ident[:])
                    last.then_inc(w_t, 1)

            @block.scalar
            def _(act):
                for n in range(3 * C):
                    act.wait_ge(w_t, n + 1)
                    act.activation(wh[:, n // C, n % C], banks[n % len(banks)], ACT.Copy).then_inc(w_hi, 1)
                act.wait_ge(w_r, 16)
                act.activation(rh[:], rr[:], ACT.Copy).then_inc(w_hi, 1)

            @block.vector
            def _(dve):
                dve.memset(out_ps[:], 0.0).then_inc(w_zo, 1)
                for n in range(3 * C):
                    dve.wait_ge(w_hi, n + 1)
                    dve.tensor_tensor(wl[:, n // C, n % C], banks[n % len(banks)], wh[:, n // C, n % C].bitcast(F32),
                                      ALU.subtract).then_inc(w_lo, 1)
                dve.wait_ge(w_hi, 3 * C + 1)
                dve.tensor_tensor(rl[:], rr[:], rh[:].bitcast(F32), ALU.subtract).then_inc(w_lo, 1)

        prob = stage[:, 0:8 * S].rearrange("p (i h s) -> p i h s", i=2, h=4)
        xs = stage[:, 8 * S:].rearrange("p (t d) -> p t d", t=T)
        cx = prob[:, 1]
        st6 = m.sb("st6", [P, T, 6])
        mv = m.sb("mv", [P, T, 2])
        ve = m.sb("ve", [P, T])
        rstd = m.sb("rstd", [P, T])
        half = m.sb("half", [P, T])
        eps = m.sb("eps", [P, 1])
        gate = m.sb("gate", [P, 1])
        xn = m.sb("xn", [P, 2, D])
        xh = m.sb("xh", [P, 2, C, P], F32R)
        xl = m.sb("xl", [P, 2, C, P], F32R)
        sq = m.sb("sq", [P, H2, D2])
        ss = m.sb("ss", [P, H2])
        mh = m.sb("mh", [P, H2])
        y0 = m.sb("y0", [P, H2])
        rr = m.sb("rr", [P, H2])
        kn = sq
        stack = m.sb("stack", [P, H2, W2], F32R)
        qT = m.sb("qT", [P, PAIRS, S], F32R)
        oT = m.sb("oT", [P, S])
        rinv = m.sb("rinv", [P, T, 4])
        scaled = sq[:, 0:T * 4, :].rearrange("p (t h) d -> p t h d", t=T)
        init = m.sem("init")

        KQ = 2 * T
        route_h, route_l = [[qT[:, 4 * i + t, :].rearrange("p (c q) -> p c q", c=C) for t in range(T)] for i in range(2)]
        route_xT = [ring[1][:, i, :].rearrange("p (c q) -> p c q", c=C) for i in range(2)]
        route_out = ring[2][:, 1, 0:T * E].rearrange("p (t e) -> p t e", t=T)
        turn_banks = [ring[1][:, i, :].rearrange("p (a q) -> p a q", a=4) for i in range(2)]
        UNITS = G * T * 2
        PER_SLOT = [len(range(i, UNITS, 3)) for i in range(3)]

        def reads(engine, upto):
            return sum(1 if u < 4 * T or u % 2 == engine else 0 for u in range(upto))

        READS = reads(0, 4 * KQ)

        def product_bank(j):
            return [ring[j % 2 * 2][:, i] for i in range(2 if j < T else 1)]

        def batches(engine, boundary, middle):
            boundary(None, 0)
            with engine.Fori(0, B - 1) as b:
                middle(b)
                boundary(b, b + 1)
            middle(B - 1)
            boundary(B - 1, None)

        block = m.main_block()

        @block.sync
        def _(sp):
            def boundary(b, nxt):
                for t in range(T if nxt is not None else 0):
                    if b is not None:
                        sp.wait_ge(s_pv, START + nxt * G * T)
                    sp.dma_start(cx[:, t], context[bass.ds(nxt * T + t, 1), :, :].rearrange("a p d -> (a p) d"))\
                      .then_inc(ld_c[t], 16)
                for t in range(T if b is not None else 0):
                    sp.wait_ge(s_x2, START + (b + 1) * G)
                    sp.dma_start(x2[bass.ds(b * T + t, 1), :, :].rearrange("a p d -> (a p) d"), xs[:, t])\
                      .then_inc(st_x[t], 16)
                for t in range(T if b is not None else 0):
                    sp.wait_ge(s_xn, START + b * KQ + T + t + 1)
                    sp.dma_start(xn3[bass.ds(b * T + t, 1), :, :].rearrange("a p d -> (a p) d"), xn[:, t % 2])\
                      .then_inc(st_n[t % 2], 16)
                for t in range(T if nxt is not None else 0):
                    if b is not None:
                        sp.wait_ge(st_x[t], START + nxt * 16)
                    sp.dma_start(xs[:, t], x1[bass.ds(nxt * T + t, 1), :, :].rearrange("a p d -> (a p) d"))\
                      .then_inc(ld_x[t], 16)

            batches(sp, boundary, lambda b: None)
            for t in range(T):
                sp.wait_ge(st_x[t], START + 16 * B)
            for i in range(2):
                sp.wait_ge(st_n[i], START + 16 * B * T // 2)

        @block.gpsimd
        def _(pool):
            pool.memset(half[:], -0.5).then_inc(init, 1)
            pool.memset(eps[:], LN_EPS).then_inc(init, 1)
            pool.memset(stack[:].bitcast(F32), 0.0).then_inc(init, 1)
            pool.memset(v[:, :, :, D2], 1.0).then_inc(init, 1)
            pool.wait_ge(init, 4)
            pool.memset(kT[0:64, :, 1, :].bitcast(F32), 0.0).then_inc(init, 1)
            pool.wait_ge(init, 5)
            pool.memset(kT[64:128, :, 0, :].bitcast(F32), 0.0).then_inc(init, 1)
            pool.wait_ge(init, 6)

            def deviation(b, k):
                pool.wait_ge(s_mv, START + 2 * b + k + 1)
                pool.tensor_tensor(ve[:], mv[:, :, 1], eps[:].to_broadcast([P, T]), ALU.add).then_inc(s_ve, 1)
                pool.wait_ge(s_ve, START + 2 * b + k + 1)
                pool.tensor_tensor(rstd[:], ve[:], half[:], ALU.pow).then_inc(s_rs, 1)

            def boundary(b, nxt):
                if b is not None:
                    deviation(b, 1)
                if nxt is not None:
                    deviation(nxt, 0)

            batches(pool, boundary, lambda b: None)

        @block.scalar
        def _(act):
            act.wait_ge(init, 4)

            def high_x(b, j):
                n = b * KQ + j
                act.wait_ge(s_xT, START + n + 1)
                act.wait_ge(s_pr, START + n - 1)
                act.activation(xh[:, j % 2], b0[:], ACT.Copy).then_inc(s_xh, 1)

            def squares(b, j):
                n = b * KQ + j
                act.wait_ge(s_pr, START + b * KQ + j + 1)
                act.wait_ge(s_lo, START + n)
                for i, bank in enumerate(product_bank(j)):
                    if j < T:
                        last = act.activation(sq[:, 16 * i:16 * i + 16],
                                              bank.rearrange("p (h d c) -> p h d c", d=D2, c=2)[:, :, :, 0], ACT.Square)
                    else:
                        last = act.activation(sq[:].rearrange("p h d -> p (h d)"), bank, ACT.Square)
                last.then_inc(s_sq, 1)

            def root(b, j):
                act.wait_ge(s_im, START + b * KQ + j + 1)
                act.activation(y0[:], rr[:], ACT.Sqrt).then_inc(s_y0, 1)

            def take_values(b, j):
                for i, bank in enumerate(product_bank(j)):
                    act.activation(v[:, j, 16 * i:16 * i + 16, 0:D2],
                                   bank.rearrange("p (h d c) -> p h d c", d=D2, c=2)[:, :, :, 1], ACT.Copy).then_inc(s_vv, 1)

            def high_heads(b, j):
                n = b * KQ + j
                act.wait_ge(s_kn, START + n + 1)
                act.wait_ge(s_tr, START + 4 * n)
                places = stack[:].rearrange("p h (r d) -> p h r d", r=4)
                places = places[:, :, 0:3:2, :] if j < T else places[:, :, 0:2, :]
                act.activation(places, kn[:].unsqueeze(2).to_broadcast([P, H2, 2, D2]), ACT.Copy).then_inc(s_hi, 1)

            def turned(b, j, quarters):
                n = b * KQ + j
                for q in quarters:
                    if j < T:
                        act.wait_ge(s_tr, START + 4 * n + q + 1)
                        act.activation(kT[0:64, 4 * q:4 * q + 4, 0, j * P:(j + 1) * P], turn_banks[q % 2][0:64],
                                       ACT.Copy).then_inc(s_eA, 1)
                    elif q % 2 == 0:
                        act.wait_ge(s_tr, START + 4 * n + q + 1)
                        act.activation(qT[:, 4 * q:4 * q + 4, (j - T) * P:(j - T + 1) * P], turn_banks[0],
                                       ACT.Copy).then_inc(s_eA, 1)

            def route_high(b, t):
                act.wait_ge(s_rT, START + b * T + t + 1)
                act.activation(route_h[t], route_xT[t % 2], ACT.Copy).then_inc(s_rh, 1)

            def boundary(b, nxt):
                if nxt is not None:
                    high_x(nxt, 0)
                if b is not None:
                    route_high(b, 0)
                    route_high(b, 1)
                if nxt is not None:
                    high_x(nxt, 1)
                if b is not None:
                    route_high(b, 2)
                    route_high(b, 3)
                if nxt is not None:
                    squares(nxt, 0)
                    take_values(nxt, 0)
                    high_x(nxt, 2)
                    root(nxt, 0)
                    high_heads(nxt, 0)

            def middle(b):
                for j in range(KQ):
                    if j + 1 < KQ:
                        squares(b, j + 1)
                    turned(b, j, (0,))
                    if j + 1 < T:
                        take_values(b, j + 1)
                    turned(b, j, (1,))
                    if j + 1 < KQ:
                        root(b, j + 1)
                    turned(b, j, (2, 3))
                    if j + 1 < KQ:
                        high_heads(b, j + 1)
                    if j + 3 < KQ:
                        high_x(b, j + 3)
                for u in range(UNITS):
                    act.wait_ge(s_sc[u % 3], START + b * PER_SLOT[u % 3] + u // 3 + 1)
                    if u >= 4:
                        act.wait_ge(s_pv, START + b * G * T + u // 2 - 1)
                    act.activation(prob[:, u // 2 % 2, 2 * (u % 2):2 * (u % 2) + 2, :], ring[u % 3][:], ACT.Exp,
                                   scale=D2 ** -0.5).then_inc(s_ex[u % 3], 1)

            batches(act, boundary, middle)

        @block.vector
        def _(dve):
            dve.wait_ge(init, 4)

            def low_x(b, j):
                dve.wait_ge(s_xh, START + b * KQ + j + 1)
                dve.tensor_tensor(xl[:, j % 2], b0[:], xh[:, j % 2].bitcast(F32), ALU.subtract).then_inc(s_xl, 1)

            def statistics(b, k):
                for t in range(T):
                    if k == 0:
                        dve.wait_ge(ld_x[t], b * 16 + 16)
                    last = dve.bn_stats(st6[:, t], xs[:, t])
                last.then_inc(s_bst, 1)
                dve.wait_ge(s_bst, START + 2 * b + k + 1)
                dve.tensor_copy(gate[:], st6[:, T - 1, 0:1]).then_inc(s_gate, 1)
                for t in range(T):
                    last = dve.bn_aggr(mv[:, t], st6[:, t])
                last.then_inc(s_mv, 1)

            def normalise(b, t, k):
                if t == 0:
                    dve.wait_ge(s_rs, START + 2 * b + k + 1)
                if t < 2:
                    dve.wait_ge(*((s_rT, START + b * T) if k == 0 else (s_xT, START + (b + 1) * KQ)))
                else:
                    dve.wait_ge(*((s_xT, START + b * KQ + T + t - 1) if k == 0 else (s_rT, START + b * T + t - 1)))
                dve.wait_ge(st_n[t % 2], START + 16 * (2 * b + (1 if k == 1 and t >= 2 else 0)))
                dve.tensor_scalar(xn[:, t % 2], xs[:, t], mv[:, t, 0:1], rstd[:, t:t + 1], ALU.subtract,
                                  ALU.mult).then_inc(s_xn, 1)

            def mean_squares(b, j):
                n = b * KQ + j
                dve.wait_ge(s_sq, START + n + 1)
                dve.tensor_reduce(ss[:], sq[:], AX.X, ALU.add).then_inc(s_ss, 1)
                dve.wait_ge(s_ss, START + n + 1)
                dve.tensor_scalar(mh[:], ss[:], -0.5 / D2, -0.5 * RMS_EPS, ALU.mult, ALU.add)
                dve.tensor_scalar(ss[:], ss[:], 1.0 / D2, RMS_EPS, ALU.mult, ALU.add).then_inc(s_ms, 1)
                dve.wait_ge(s_ms, START + n + 1)
                dve.reciprocal(rr[:], ss[:]).then_inc(s_im, 1)

            def heads(b, j):
                n = b * KQ + j
                dve.wait_ge(s_y0, START + n + 1)
                dve.tensor_tensor(rr[:], y0[:], y0[:], ALU.mult).then_inc(s_yy, 1)
                dve.wait_ge(s_yy, START + n + 1)
                dve.tensor_tensor(rr[:], rr[:], mh[:], ALU.mult).then_inc(s_my, 1)
                dve.wait_ge(s_my, START + n + 1)
                dve.scalar_tensor_tensor(rr[:], rr[:], 1.5, y0[:], ALU.add, ALU.mult).then_inc(s_rr, 1)
                dve.wait_ge(s_rr, START + n + 1)
                if j < T:
                    dve.wait_ge(s_vv, START + 2 * (b * T + j) + 2)
                for i, bank in enumerate(product_bank(j)):
                    if j < T:
                        src, hs = bank.rearrange("p (h d c) -> p h d c", d=D2, c=2)[:, :, :, 0], slice(16 * i, 16 * i + 16)
                    else:
                        src, hs = bank.rearrange("p (h d) -> p h d", d=D2), slice(0, H2)
                    nh = src.shape[1]
                    last = dve.tensor_tensor(kn[:, hs], src, rr[:, hs].unsqueeze(2).to_broadcast([P, nh, D2]), ALU.mult)
                last.then_inc(s_kn, 1)

            def low_heads(b, j):
                n = b * KQ + j
                dve.wait_ge(s_hi, START + n + 1)
                at = 1 if j < T else 2
                dve.tensor_tensor(stack[:, :, at * D2:(at + 1) * D2], kn[:], stack[:, :, 0:D2].bitcast(F32),
                                  ALU.subtract).then_inc(s_lo, 1)

            def turned(b, j, quarters):
                n = b * KQ + j
                for q in quarters:
                    if j < T:
                        dve.wait_ge(s_tr, START + 4 * n + q + 1)
                        dve.tensor_copy(kT[64:128, 4 * q:4 * q + 4, 1, j * P:(j + 1) * P], turn_banks[q % 2][64:128])\
                           .then_inc(s_eD, 1)
                    elif q % 2 == 1:
                        dve.wait_ge(s_tr, START + 4 * n + q + 1)
                        dve.tensor_copy(qT[:, 4 * q:4 * q + 4, (j - T) * P:(j - T + 1) * P], turn_banks[1]).then_inc(s_eD, 1)

            def route_low(b, t):
                dve.wait_ge(s_rh, START + b * T + t + 1)
                dve.tensor_tensor(route_l[t], route_xT[t % 2], route_h[t].bitcast(F32), ALU.subtract).then_inc(s_rl, 1)

            def take_logits(b):
                dve.wait_ge(s_rp, START + b + 1)
                dve.tensor_copy(logits[:, bass.ds(b * T, T), :], route_out).then_inc(s_lg, 1)

            def boundary(b, nxt):
                if b is not None:
                    statistics(b, 1)
                if nxt is not None:
                    low_x(nxt, 0)
                if b is not None:
                    for t in range(2):
                        normalise(b, t, 1)
                    for t in range(2):
                        route_low(b, t)
                    for t in range(2, T):
                        normalise(b, t, 1)
                if nxt is not None:
                    low_x(nxt, 1)
                if b is not None:
                    for t in range(2, T):
                        route_low(b, t)
                    take_logits(b)
                if nxt is not None:
                    mean_squares(nxt, 0)
                    low_x(nxt, 2)
                    heads(nxt, 0)
                    low_heads(nxt, 0)

            def middle(b):
                for j in range(KQ):
                    turned(b, j, (0,))
                    if j + 1 < KQ:
                        mean_squares(b, j + 1)
                    if j == 1:
                        normalise(b, 0, 0)
                    turned(b, j, (1,))
                    if j + 1 < KQ:
                        heads(b, j + 1)
                    turned(b, j, (2, 3))
                    if j + 1 < KQ:
                        low_heads(b, j + 1)
                    if j + 3 < KQ:
                        low_x(b, j + 3)
                    if j == 0:
                        statistics(b, 0)
                    elif j + 4 < KQ:
                        normalise(b, j + 4 - T, 0)
                for g in range(G):
                    k = b * G + g
                    dve.wait_ge(s_pv, START + k * T + T)
                    dve.wait_ge(s_tt, START + k)
                    dve.tensor_copy(oT[:], out_ps[:]).then_inc(s_ot, 1)
                    dve.wait_ge(s_tt, START + k + 1)
                    o = b0[:].rearrange("p t (h d) -> p t h d", h=4)
                    dve.reciprocal(rinv[:], o[:, :, :, D2]).then_inc(s_ri, 1)
                    dve.wait_ge(s_ri, START + k + 1)
                    dve.tensor_tensor(scaled, o[:, :, :, 0:D2], rinv[:].unsqueeze(3).to_broadcast([P, T, 4, D2]),
                                      ALU.mult).then_inc(s_sm, 1)
                    dve.wait_ge(s_sm, START + k + 1)
                    part = xs[:, :, g * 4 * D2:(g + 1) * 4 * D2]
                    dve.tensor_tensor(part, part, scaled.rearrange("p t h d -> p t (h d)"), ALU.add).then_inc(s_x2, 1)
                dve.wait_ge(s_x2, START + b * G + G)

            batches(dve, boundary, middle)

        @block.tensor
        def _(pe):
            def turn_x(b, j):
                n = b * KQ + j
                if j < T:
                    pe.wait_ge(ld_c[j], b * 16 + 16)
                else:
                    pe.wait_ge(s_xn, START + b * KQ + (j - T) + 1)
                if j == 0:
                    pe.wait_ge(s_x2, START + b * G)
                pe.wait_ge(s_xl, START + n)
                src = cx[:, j] if j < T else xn[:, j % 2]
                for c in range(C):
                    last = pe.transpose(b0[:, c, :], src[:, c * P:(c + 1) * P], ident[:])
                last.then_inc(s_xT, 1)

            def project(b, j, pieces=(0, 1)):
                n = b * KQ + j
                if 0 in pieces:
                    pe.wait_ge(s_xh, START + n + 1)
                    pe.wait_ge(s_xl, START + n + 1)
                    if j == 1:
                        pe.wait_ge(s_lg, START + b)
                    elif j >= 2:
                        pe.wait_ge(s_kn, START + b * KQ + j - 1)
                i = j % 2
                for piece in pieces:
                    w, part = (1 + piece, range(C)) if j < T else (0, range(piece * C // 2, (piece + 1) * C // 2))
                    last = product(pe, product_bank(j)[piece if j < T else 0], lambda c: xh[:, i, c],
                                   lambda c: xl[:, i, c], lambda c: wh[:, w, c], lambda c: wl[:, w, c], C, part)
                if 1 in pieces:
                    last.then_inc(s_pr, 1)

            def route_turn(b, t):
                pe.wait_ge(s_xn, START + b * KQ + T + t + 1)
                if t >= 2:
                    pe.wait_ge(s_rl, START + b * T + t - 1)
                for c in range(C):
                    last = pe.transpose(route_xT[t % 2][:, c, :], xn[:, t % 2, c * P:(c + 1) * P], ident[:])
                last.then_inc(s_rT, 1)

            def route_project(b, t):
                pe.wait_ge(s_rh, START + b * T + t + 1)
                pe.wait_ge(s_rl, START + b * T + t + 1)
                last = product(pe, route_out[:, t], lambda c: route_h[t][:, c], lambda c: route_l[t][:, c],
                               lambda c: rh[:, c], lambda c: rl[:, c], C)
                if t == T - 1:
                    last.then_inc(s_rp, 1)

            def turn_heads(b, j, quarters):
                n = b * KQ + j
                pe.wait_ge(s_hi, START + n + 1)
                pe.wait_ge(s_lo, START + n + 1)
                for q in quarters:
                    use = max(4 * j + q - 1, 0)
                    pe.wait_ge(s_eA, START + b * READS + reads(0, use))
                    pe.wait_ge(s_eD, START + b * READS + reads(1, use))
                    for a in range(4):
                        last = pe.transpose(turn_banks[q % 2][:, a, :],
                                            stack[:, 2 * (4 * q + a):2 * (4 * q + a) + 2, :].bitcast(F32)
                                            .rearrange("p h w -> p (h w)"), ident[:])
                    last.then_inc(s_tr, 1)

            def scores(b, u):
                g, kt, pair = u // (2 * T), u // 2 % T, 2 * (u // (2 * T)) + u % 2
                if u >= 3:
                    pe.wait_ge(s_ex[u % 3], START + b * PER_SLOT[u % 3] + u // 3)
                for i in range(2):
                    last = pe.matmul(ring[u % 3][:, i, :], kT[:, pair, i, kt * P:(kt + 1) * P], qT[:, pair, :],
                                     start=True, stop=True)
                last.then_inc(s_sc[u % 3], 1)

            def values(b, w):
                g, kt = w // T, w % T
                for u in (2 * w, 2 * w + 1):
                    pe.wait_ge(s_ex[u % 3], START + b * PER_SLOT[u % 3] + u // 3 + 1)
                if kt == 0:
                    pe.wait_ge(s_ot, START + b * G + g)
                for i in range(4):
                    last = pe.matmul(out_ps[32 * i:32 * i + D2 + 1, :], v[:, kt, 4 * g + i, :], prob[:, w % 2, i, :],
                                     start=(kt == 0), stop=(kt == T - 1))
                last.then_inc(s_pv, 1)

            def turn_out(b, g):
                pe.wait_ge(s_ot, START + b * G + g + 1)
                pe.wait_ge(s_x2, START + b * G + g)
                for t in range(T):
                    last = pe.transpose(b0[:, t, :], oT[:, t * P:(t + 1) * P], ident[:])
                last.then_inc(s_tt, 1)

            def boundary(b, nxt):
                if nxt is not None:
                    turn_x(nxt, 0)
                if b is not None:
                    route_turn(b, 0)
                    route_turn(b, 1)
                if nxt is not None:
                    project(nxt, 0)
                    turn_x(nxt, 1)
                if b is not None:
                    route_project(b, 0)
                    route_turn(b, 2)
                    route_project(b, 1)
                    route_turn(b, 3)
                    route_project(b, 2)
                    route_project(b, 3)
                if nxt is not None:
                    turn_x(nxt, 2)
                    project(nxt, 1)

            def middle(b):
                for j in range(KQ):
                    turn_heads(b, j, (0, 1))
                    if j + 2 < KQ:
                        project(b, j + 2, (0,))
                    turn_heads(b, j, (2, 3))
                    if j + 3 < KQ:
                        turn_x(b, j + 3)
                    if j + 2 < KQ:
                        project(b, j + 2, (1,))
                pe.wait_ge(s_eA, START + (b + 1) * READS)
                pe.wait_ge(s_eD, START + (b + 1) * READS)
                pe.wait_ge(s_vv, START + (b + 1) * 2 * T)
                pe.wait_ge(init, 6)
                WORK = G * T
                for w in range(WORK + 1):
                    if w < WORK:
                        scores(b, 2 * w)
                        scores(b, 2 * w + 1)
                    if w >= 1:
                        values(b, w - 1)
                    if w >= 3 and (w - 3) % T == 2:
                        turn_out(b, (w - 3) // T)
                turn_out(b, G - 1)

            batches(pe, boundary, middle)


def route(nc, consts, logits, slot, weight, token, ybuf):
    NONE = E * CAP
    with ExitStack() as ctx:
        m = Phase(nc, ctx, "ro")
        k_sb = m.sb("consts", [P, K_COLS])
        tri = m.sb("tri", [P, P], BF16)
        ones = m.sb("ones", [P, P], BF16)
        zero = m.sb("zero", [1, D])
        top = m.sb("top", [P, NT, TOPK])
        index = m.sb("index", [P, NT, TOPK], U32)
        indexf = m.sb("indexf", [P, NT, TOPK])
        onehot = m.sb("onehot", [P, NT, TOPK, E], BF16)
        picked = m.sb("picked", [P, NT, TOPK, E])
        first = m.sb("first", [P, NT, E])
        full = m.sb("full", [P, E])
        over = m.sb("over", [P, NT, E])
        place = m.sb("place", [P, NT, E])
        slotf = m.sb("slotf", [P, NT, TOPK])
        diff = m.sb("diff", [P, NT, TOPK])
        total = m.sb("total", [P, NT])
        column = m.sb("column", [P, NT, TOPK])
        row = m.sb("row", [P, NT, TOPK])
        upper = m.sb("upper", [P, NT, TOPK])
        less = m.sb("less", [P, NT, TOPK])
        is_column = m.sb("is_column", [P, 2, TOPK, P])
        column_id = m.sb("column_id", [P, 2, TOPK, P], F32R)
        is_row = m.sb("is_row", [P, 2, TOPK, P], F32R)
        nothing = m.sb("nothing", [P, 1, P], F32R)
        pos = m.ps("pos", [P, 2, NT // 2, E])
        count = m.ps("count", [P, 2, NT // 2, E])
        table = m.ps("table", [P, P])
        (ld, st_z, s_c, s_d, s_top, s_pos, s_place, s_picked, s_exp, s_slot, s_table, s_onehot, s_count) = [m.sem(n) for n in (
            "ld st_z c d top pos place picked exp slot table onehot count").split()]
        counters = [m.sem(n) for n in "is_col col_id is_row added".split()]
        s_col, s_id, s_row, s_add = counters
        CUT = NT * 11 // 16
        with nc.Block() as block:
            @block.sync
            def _(sp):
                for c in counters:
                    sp.sem_inc(c, START)

        block = m.main_block()
        iota = k_sb[:, K_IOTA:K_IOTA + E]
        numbers = k_sb[:, K_IOTA:K_IOTA + P].unsqueeze(1).to_broadcast([P, TOPK, P])

        @block.sync
        def _(sp):
            sp.dma_start(k_sb[:], consts).then_inc(ld, 16)
            sp.wait_ge(s_c, 1)
            sp.dma_start(ybuf[NONE:NONE + 1, :], zero[:]).then_inc(st_z, 16)
            sp.wait_ge(st_z, 16)

        @block.gpsimd
        def _(pool):
            pool.memset(zero[:], 0.0).then_inc(s_c, 1)
            pool.memset(nothing[:].bitcast(F32), 0.0).then_inc(s_c, 1)
            pool.wait_ge(s_place, 1)
            pool.tensor_tensor(picked[:, CUT:], onehot[:, CUT:],
                               place[:, CUT:].unsqueeze(2).to_broadcast([P, NT - CUT, TOPK, E]), ALU.mult).then_inc(s_picked, 1)

        @block.scalar
        def _(act):
            act.wait_ge(s_top, 1)
            act.activation(diff[:], diff[:], ACT.Exp).then_inc(s_exp, 1)
            with act.Fori(0, NT // 2) as r:
                for i in range(2):
                    n = 2 * r + i
                    act.wait_ge(s_col, START + n + 1)
                    act.wait_ge(s_add, START + n - 1)
                    act.activation(column_id[:, i], is_column[:, i], ACT.Copy,
                                   scale=k_sb[:, bass.ds(n + K_TOK, 1)]).then_inc(s_id, 1)

        @block.tensor
        def _(pe):
            for out, matrix, done in ((count, ones, s_count), (pos, tri, s_pos)):
                for i in range(2):
                    pe.wait_ge(s_onehot, 1 + i)
                    for k in range(TOPK):
                        last = pe.matmul(out[:, i], matrix[:], onehot[:, i * NT // 2:(i + 1) * NT // 2, k, :],
                                         start=(k == 0), stop=(k == TOPK - 1))
                    last.then_inc(done, 1)
            pe.wait_ge(s_c, 2)
            pe.matmul(table[:], nothing[:, 0], nothing[:, 0], start=True, stop=False)
            with pe.Fori(0, NT // 2) as r:
                for i in range(2):
                    pe.wait_ge(s_id, START + 2 * r + i + 1)
                    pe.wait_ge(s_row, START + 2 * r + i + 1)
                    for k in range(TOPK):
                        last = pe.matmul(table[:], is_row[:, i, k], column_id[:, i, k], start=False, stop=False)
                    last.then_inc(s_add, 1)
            pe.matmul(table[:], nothing[:, 0], nothing[:, 0], start=False, stop=True).then_inc(s_table, 1)

        @block.vector
        def _(dve):
            steps = [0]

            def then(ins):
                steps[0] += 1
                ins.then_inc(s_d, 1)
                dve.wait_ge(s_d, steps[0])

            for n in range(NT):
                last = dve.max(top[:, n], logits[:, n])
            then(last)
            for n in range(NT):
                last = dve.max_index(index[:, n], top[:, n], logits[:, n])
            then(last)
            dve.tensor_tensor(diff[:], top[:], top[:, :, 0:1].to_broadcast([P, NT, TOPK]), ALU.subtract).then_inc(s_top, 1)
            then(dve.tensor_copy(indexf[:], index[:]))
            dve.wait_ge(ld, 16)
            dve.tensor_copy(tri[:], k_sb[:, K_TRI:K_TRI + P])
            dve.memset(ones[:], 1.0)
            dve.tensor_scalar(first[:, 0], iota, float(CAP), None, ALU.mult)
            then(dve.tensor_scalar(full[:], iota, float(CAP), float(CAP), ALU.mult, ALU.add))
            for i in range(2):
                half = slice(i * NT // 2, (i + 1) * NT // 2)
                dve.tensor_tensor(onehot[:, half].rearrange("p n k e -> p (n k) e"),
                                  indexf[:, half].rearrange("p n k -> p (n k)").unsqueeze(2)
                                  .to_broadcast([P, NT // 2 * TOPK, E]),
                                  iota.unsqueeze(1).to_broadcast([P, NT // 2 * TOPK, E]), ALU.is_equal).then_inc(s_onehot, 1)
            for n in range(1, NT):
                if (n - 1) % (NT // 2) == 0:
                    dve.wait_ge(s_count, 1 + (n - 1) // (NT // 2))
                then(dve.tensor_tensor(first[:, n], first[:, n - 1], count[:, (n - 1) // (NT // 2), (n - 1) % (NT // 2)],
                                       ALU.add))
            dve.wait_ge(s_pos, 2)
            then(dve.tensor_tensor(place[:], pos[:].rearrange("p a n e -> p (a n) e"), first[:], ALU.add))
            then(dve.tensor_tensor(over[:], place[:], full[:].unsqueeze(1).to_broadcast([P, NT, E]), ALU.is_ge))
            then(dve.tensor_scalar(over[:], over[:], float(2 * NONE), None, ALU.mult))
            dve.tensor_tensor(place[:], place[:], over[:], ALU.add).then_inc(s_place, 1)
            dve.wait_ge(s_place, 1)
            then(dve.tensor_tensor(picked[:, 0:CUT], onehot[:, 0:CUT],
                                   place[:, 0:CUT].unsqueeze(2).to_broadcast([P, CUT, TOPK, E]), ALU.mult))
            dve.wait_ge(s_picked, 1)
            then(dve.tensor_reduce(slotf[:], picked[:], AX.X, ALU.add))
            then(dve.tensor_scalar(slotf[:], slotf[:], float(NONE), None, ALU.min))
            then(dve.tensor_scalar(row[:], indexf[:], -float(CAP), None, ALU.mult))
            then(dve.tensor_tensor(row[:], row[:], slotf[:], ALU.add))
            then(dve.tensor_scalar(upper[:], row[:], float(P), None, ALU.is_ge))
            dve.tensor_scalar(column[:], indexf[:], float(CT), None, ALU.mult)
            then(dve.tensor_scalar(less[:], upper[:], -float(P), None, ALU.mult))
            dve.tensor_tensor(row[:], row[:], less[:], ALU.add)
            then(dve.tensor_tensor(column[:], column[:], upper[:], ALU.add))
            with dve.Fori(0, NT // 2) as r:
                for i in range(2):
                    n = 2 * r + i
                    dve.wait_ge(s_add, START + n - 1)
                    dve.tensor_tensor(is_column[:, i], numbers, column[:, bass.ds(n, 1)].rearrange("p a k -> p (a k)")
                                      .unsqueeze(2).to_broadcast([P, TOPK, P]), ALU.is_equal).then_inc(s_col, 1)
                    dve.tensor_tensor(is_row[:, i], numbers, row[:, bass.ds(n, 1)].rearrange("p a k -> p (a k)")
                                      .unsqueeze(2).to_broadcast([P, TOPK, P]), ALU.is_equal).then_inc(s_row, 1)
            dve.tensor_copy(slot[:], slotf[:].rearrange("p n k -> p (n k)")).then_inc(s_slot, 1)
            dve.wait_ge(s_exp, 1)
            then(dve.tensor_reduce(total[:], diff[:], AX.X, ALU.add))
            then(dve.reciprocal(total[:], total[:]))
            dve.tensor_tensor(weight[:].rearrange("p (n k) -> p n k", k=TOPK), diff[:],
                              total[:].unsqueeze(2).to_broadcast([P, NT, TOPK]), ALU.mult).then_inc(s_slot, 1)
            dve.wait_ge(s_table, 1)
            dve.tensor_copy(token[:], table[:]).then_inc(s_slot, 1)


def experts(nc, ident, token, xn3, w_gate, w_up, w_down, ybuf):
    R = I - P
    with ExitStack() as ctx:
        m = Phase(nc, ctx, "ex")
        raw = m.sb("raw", [P, 2, C, 2, I])
        rawd = m.sb("rawd", [P, 2, 2, D])
        wh = m.sb("wh", [P, 2, C, 3, P], F32R)
        wl = m.sb("wl", [P, 2, C, 3, P], F32R)
        dh = m.sb("dh", [P, 2, 2, D], F32R)
        dl = m.sb("dl", [P, 2, 2, D], F32R)
        gate = m.sb("gate", [P, 5])
        now = m.sb("now", [P, 2, CT], I32)
        xg = m.sb("xg", [P, 2, CT, D])
        xh = m.sb("xh", [P, 2, C, CAP], F32R)
        xl = m.sb("xl", [P, 2, C, CAP], F32R)
        sg = m.sb("sg", [P, 2, 2, CAP])
        h = m.sb("h", [P, 2, 2, CAP])
        hh = m.sb("hh", [P, 2, 2, CAP], F32R)
        hl = m.sb("hl", [P, 2, CAP], F32R)
        y = m.sb("y", [P, 2, CT, D])
        bx = [m.ps(f"bx{i}", [P, C, P]) for i in range(2)]
        ba = [m.ps(f"ba{i}", [P, 2, CAP]) for i in range(2)]
        bb = [m.ps(f"bb{i}", [P, CAP]) for i in range(2)]
        by = [m.ps(f"by{i}", [P, D]) for i in range(2)]

        ld_w = [m.sem(f"ld_w{i}") for i in range(2)]
        ld_d = [m.sem(f"ld_d{i}") for i in range(2)]
        ld_g = [m.sem(f"ld_g{i}") for i in range(2)]
        st_y = [[m.sem(f"st_y{i}{j}") for j in range(2)] for i in range(2)]
        w_g, s_now = m.sem("gate"), m.sem("now")
        counters = st_y[0] + st_y[1]

        def counter(name):
            counters.append(m.sem(name))
            return counters[-1]

        s_wh, s_wl, s_dh, s_dl, s_xT, s_xh, s_xl, s_gu = [counter(n) for n in "wh wl dh dl xT xh xl gu".split()]
        s_sg, s_h, s_hh, s_hl, s_dn, s_yA, s_yD = [counter(n) for n in "sg h hh hl dn yA yD".split()]

        with nc.Block() as block:
            @block.sync
            def _(sp):
                for c in counters:
                    sp.sem_inc(c, START)

            @block.gpsimd
            def _(pool):
                pool.memset(gate[:], 0.0).then_inc(w_g, 1)
                pool.wait_ge(w_g, 1)

        def wait(eng, sem, count):
            if not isinstance(count, int) or count > 0:
                eng.wait_ge(sem, START + count)

        PAIRS = E // 2 - 2

        def loop(eng, first, step, last):
            first()
            step(0, 0, 0)
            with eng.Fori(0, PAIRS) as r:
                step(2 * r + 1, 1, r)
                step(2 * r + 2, 0, r + 1)
            for e in range(2 * PAIRS + 1, E):
                step(e, e % 2, e // 2)
            last()

        def nothing():
            pass

        def expert(a, e):
            return a[e:e + 1] if isinstance(e, int) else a[bass.ds(e, 1)]

        block = m.main_block()

        @block.sync
        def _(sp):
            def load(e, i, r):
                wait(sp, s_wl, 2 * e - 2)
                for n, w in enumerate((w_gate, w_up)):
                    sp.dma_start(raw[:, i, :, n, :], expert(w, e).rearrange("a (c p) f -> p (a c) f", p=P)).then_inc(ld_w[i], 16)
                wait(sp, s_dl, e - 1)
                w = expert(w_down, e)
                sp.dma_start(rawd[:, i, 0, :], w[:, 0:P, :].rearrange("a p d -> (a p) d")).then_inc(ld_d[i], 16)
                for rows in (slice(0, R), slice(R, P)):
                    sp.dma_start(rawd[rows, i, 1, :], w[:, P:I, :].rearrange("a p d -> (a p) d")).then_inc(ld_d[i], 16)

            def store(e, i):
                for j in range(CT):
                    sp.wait_ge((s_yA, s_yD)[j], START + e + 1)
                    at = CT * e + j
                    rows = ybuf[at * P:(at + 1) * P, :] if isinstance(e, int) else ybuf[bass.ds(at * P, P), :]
                    sp.dma_start(rows, y[:, i, j]).then_inc(st_y[i][j], 16)

            def step(e, i, r):
                if not isinstance(e, int) or e < E - 2:
                    load(e + 2, i, r + 1)
                if not isinstance(e, int) or e > 0:
                    store(e - 1, 1 - i)

            def last():
                store(E - 1, 1)
                for i in range(2):
                    for j in range(CT):
                        sp.wait_ge(st_y[i][j], START + 16 * E // 2)

            def first():
                load(0, 0, 0)
                load(1, 1, 0)

            loop(sp, first, step, last)

        @block.gpsimd
        def _(pool):
            def gather(e, i, r):
                wait(pool, s_xT, 2 * e - 2)
                pool.tensor_tensor(gate[:, 1 + i:2 + i], gate[:, 0:1], gate[:, 0:1], ALU.add)
                at = token[:, CT * e:CT * e + CT] if isinstance(e, int) else token[:, bass.ds(CT * e, CT)]
                pool.tensor_copy(now[:, i], at).then_inc(s_now, 1)
                pool.wait_ge(s_now, e + 1)
                pool.tensor_tensor(gate[:, 3 + i:4 + i], gate[:, 0:1], gate[:, 0:1], ALU.add)
                for j in range(CT):
                    pool.indirect_dma_start(out=xg[:, i, j, :], out_offset=None, in_=xn3,
                                            in_offset=bass.IndirectOffsetOnAxis(now[:, i, j:j + 1], 0)).then_inc(ld_g[i], 16)

            def low(e, i):
                pool.wait_ge(s_dh, START + e + 1)
                pool.tensor_tensor(dl[:, i], rawd[:, i], dh[:, i].bitcast(F32), ALU.subtract).then_inc(s_dl, 1)

            def step(e, i, r):
                if not isinstance(e, int) or e < E - 1:
                    gather(e + 1, 1 - i, r + i)
                low(e, i)

            loop(pool, lambda: gather(0, 0, 0), step, nothing)

        def weight_parts(i):
            yield raw[:, i, :, :, 0:P], wh[:, i, :, 0:2, :], wl[:, i, :, 0:2, :]
            yield raw[:, i, :, :, P:I], *(w[:, i, :, 2, :].rearrange("p c (n f) -> p c n f", n=2) for w in (wh, wl))

        @block.scalar
        def _(act):
            def weights(e, i, r):
                act.wait_ge(ld_w[i], 32 * (r + 1))
                wait(act, s_gu, e - 1)
                for src, hi, _ in weight_parts(i):
                    act.activation(hi, src, ACT.Copy).then_inc(s_wh, 1)

            def down_weights(e, i, r):
                act.wait_ge(ld_d[i], 48 * (r + 1))
                wait(act, s_dn, 2 * e - 2)
                act.activation(dh[:, i], rawd[:, i], ACT.Copy).then_inc(s_dh, 1)

            def tokens(e, i):
                for j in range(CT):
                    act.wait_ge(s_xT, START + CT * e + j + 1)
                    act.activation(xh[:, i, :, j * P:(j + 1) * P], bx[j][:], ACT.Copy).then_inc(s_xh, 1)

            def inner(e, i):
                act.wait_ge(s_gu, START + e + 1)
                act.activation(sg[:, i, 0], ba[i][:, 0], ACT.Silu).then_inc(s_sg, 1)
                act.activation(sg[0:R, i, 1], bb[i][0:R], ACT.Silu).then_inc(s_sg, 1)

            def inner_high(e, i):
                act.wait_ge(s_h, START + 2 * e + 2)
                act.activation(hh[:, i, 0], h[:, i, 0], ACT.Copy).then_inc(s_hh, 1)
                act.activation(hh[0:R, i, 1], h[0:R, i, 1], ACT.Copy).then_inc(s_hh, 1)

            def store(e, i, r):
                act.wait_ge(s_dn, START + 2 * e + 1)
                wait(act, st_y[i][0], 16 * r)
                act.activation(y[:, i, 0], by[0][:], ACT.Copy).then_inc(s_yA, 1)

            def first():
                weights(0, 0, 0)
                down_weights(0, 0, 0)
                tokens(0, 0)

            def step(e, i, r):
                ahead = not isinstance(e, int) or e < E - 1
                if ahead:
                    weights(e + 1, 1 - i, r + i)
                inner(e, i)
                if ahead:
                    tokens(e + 1, 1 - i)
                inner_high(e, i)
                if not isinstance(e, int) or e > 0:
                    store(e - 1, 1 - i, r - 1 + i)
                if ahead:
                    down_weights(e + 1, 1 - i, r + i)

            loop(act, first, step, lambda: store(E - 1, 1, E // 2 - 1))

        @block.vector
        def _(dve):
            def weights(e, i):
                dve.wait_ge(s_wh, START + 2 * e + 2)
                for src, hi, lo in weight_parts(i):
                    dve.tensor_tensor(lo, src, hi.bitcast(F32), ALU.subtract).then_inc(s_wl, 1)

            def tokens(e, i):
                for j in range(CT):
                    dve.wait_ge(s_xh, START + CT * e + j + 1)
                    at = slice(j * P, (j + 1) * P)
                    dve.tensor_tensor(xl[:, i, :, at], bx[j][:], xh[:, i, :, at].bitcast(F32), ALU.subtract).then_inc(s_xl, 1)

            def inner(e, i):
                dve.wait_ge(s_sg, START + 2 * e + 2)
                dve.tensor_tensor(h[:, i, 0], ba[i][:, 1], sg[:, i, 0], ALU.mult).then_inc(s_h, 1)
                dve.tensor_tensor(h[0:R, i, 1], bb[i][R:2 * R], sg[0:R, i, 1], ALU.mult).then_inc(s_h, 1)

            def inner_low(e, i):
                dve.wait_ge(s_hh, START + 2 * e + 2)
                dve.tensor_tensor(hl[:, i], h[:, i, 0], hh[:, i, 0].bitcast(F32), ALU.subtract).then_inc(s_hl, 1)
                dve.tensor_tensor(hh[R:2 * R, i, 1], h[0:R, i, 1], hh[0:R, i, 1].bitcast(F32), ALU.subtract).then_inc(s_hl, 1)

            def store(e, i, r):
                dve.wait_ge(s_dn, START + 2 * e + 2)
                wait(dve, st_y[i][1], 16 * r)
                dve.tensor_copy(y[:, i, 1], by[1][:]).then_inc(s_yD, 1)

            def first():
                weights(0, 0)
                tokens(0, 0)

            def step(e, i, r):
                ahead = not isinstance(e, int) or e < E - 1
                if ahead:
                    weights(e + 1, 1 - i)
                inner(e, i)
                if ahead:
                    tokens(e + 1, 1 - i)
                inner_low(e, i)
                if not isinstance(e, int) or e > 0:
                    store(e - 1, 1 - i, r - 1 + i)

            loop(dve, first, step, lambda: store(E - 1, 1, E // 2 - 1))

        @block.tensor
        def _(pe):
            def turn(e, i, r):
                pe.wait_ge(ld_g[i], 16 * CT * (r + 1))
                for j in range(CT):
                    wait(pe, s_xl, CT * e + j - 1)
                    for c in range(C):
                        last = pe.transpose(bx[j][:, c, :], xg[:, i, j, c * P:(c + 1) * P], ident[:])
                    last.then_inc(s_xT, 1)

            def up(e, i):
                pe.wait_ge(s_wl, START + 2 * e + 2)
                pe.wait_ge(s_xl, START + CT * e + CT)
                wait(pe, s_h, 2 * e - 2)
                for n, out in enumerate((ba[i][:, 0], ba[i][:, 1], bb[i][:])):
                    last = product(pe, out, lambda c: wh[:, i, c, n], lambda c: wl[:, i, c, n], lambda c: xh[:, i, c],
                                   lambda c: xl[:, i, c], C)
                last.then_inc(s_gu, 1)

            def down(e, i):
                pe.wait_ge(s_dl, START + e + 1)
                pe.wait_ge(s_hl, START + 2 * e + 2)
                for j in range(CT):
                    wait(pe, (s_yA, s_yD)[j], e)
                    at = slice(j * P, (j + 1) * P)
                    product(pe, by[j][:], lambda c: hh[:, i, 0, at], lambda c: hl[:, i, at], lambda c: dh[:, i, 0],
                            lambda c: dl[:, i, 0], 1, stop=False)
                    pe.matmul(by[j][:], hh[:, i, 1, at], dh[:, i, 1], start=False, stop=False)
                    pe.matmul(by[j][:], hh[:, i, 1, at], dl[:, i, 1], start=False, stop=True).then_inc(s_dn, 1)

            def first():
                turn(0, 0, 0)

            def step(e, i, r):
                up(e, i)
                if not isinstance(e, int) or e < E - 1:
                    turn(e + 1, 1 - i, r + i)
                if not isinstance(e, int) or e > 0:
                    down(e - 1, 1 - i)

            loop(pe, first, step, lambda: down(E - 1, 1))


def combine(nc, slot, weight, x2, ybuf, out):
    with ExitStack() as ctx:
        m = Phase(nc, ctx, "co")
        RING = 4
        xs = m.sb("x", [P, RING, D])
        yg = m.sb("y", [P, RING, TOPK, D])
        gate = m.sb("gate", [P, 1 + 2 * RING])
        now = m.sb("now", [P, RING, TOPK], I32)
        s_g, s_now = m.sem("gate"), m.sem("now")
        ld_x = [m.sem(f"ld_x{i}") for i in range(RING)]
        ld_y = [m.sem(f"ld_y{i}") for i in range(RING)]
        st = [m.sem(f"st{i}") for i in range(RING)]
        s_acc = [m.sem(f"acc{i}") for i in range(RING)]
        counters = st + s_acc
        with nc.Block() as block:
            @block.sync
            def _(sp):
                for c in counters:
                    sp.sem_inc(c, START)

            @block.gpsimd
            def _(pool):
                pool.memset(gate[:], 0.0).then_inc(s_g, 1)
                pool.wait_ge(s_g, 1)

        block = m.main_block()

        @block.sync
        def _(sp):
            with sp.Fori(0, NT // RING) as r:
                for i in range(RING):
                    sp.wait_ge(st[i], START + 16 * r)
                    sp.dma_start(xs[:, i], x2[bass.ds(RING * r + i, 1)].rearrange("a p d -> (a p) d")).then_inc(ld_x[i], 16)
                for i in range(RING):
                    sp.wait_ge(s_acc[i], START + TOPK * (r + 1))
                    sp.dma_start(out[bass.ds(RING * r + i, 1)].rearrange("a p d -> (a p) d"), xs[:, i]).then_inc(st[i], 16)
            for i in range(RING):
                sp.wait_ge(st[i], START + 16 * NT // RING)

        @block.gpsimd
        def _(pool):
            with pool.Fori(0, NT // RING) as r:
                for i in range(RING):
                    pool.wait_ge(s_acc[i], START + TOPK * r)
                    pool.tensor_tensor(gate[:, 1 + i:2 + i], gate[:, 0:1], gate[:, 0:1], ALU.add)
                    pool.tensor_copy(now[:, i], slot[:, bass.ds((RING * r + i) * TOPK, TOPK)]).then_inc(s_now, 1)
                    pool.wait_ge(s_now, RING * r + i + 1)
                    pool.tensor_tensor(gate[:, 1 + RING + i:2 + RING + i], gate[:, 0:1], gate[:, 0:1], ALU.add)
                    for k in range(TOPK):
                        pool.indirect_dma_start(
                            out=yg[:, i, k, :], out_offset=None, in_=ybuf,
                            in_offset=bass.IndirectOffsetOnAxis(now[:, i, k:k + 1], 0)).then_inc(ld_y[i], 16)

        @block.vector
        def _(dve):
            with dve.Fori(0, NT // RING) as r:
                for i in range(RING):
                    dve.wait_ge(ld_x[i], 16 * (r + 1))
                    dve.wait_ge(ld_y[i], 16 * TOPK * (r + 1))
                    for k in range(TOPK):
                        if k:
                            dve.wait_ge(s_acc[i], START + TOPK * r + k)
                        dve.scalar_tensor_tensor(xs[:, i], yg[:, i, k], weight[:, bass.ds((RING * r + i) * TOPK + k, 1)],
                                                 xs[:, i], ALU.mult, ALU.add).then_inc(s_acc[i], 1)


def decoder_layer(nc, consts, x, context, w_qkv, w_out, b_out, wq, wk, wv, w_router, w_gate, w_up, w_down, out):
    def tiles(a):
        return a.rearrange("b (t p) d -> (b t) p d", p=P)

    x1 = nc.dram_tensor("x1", (NT, P, D), F32).ap()
    x2 = nc.dram_tensor("x2", (NT, P, D), F32).ap()
    xn3 = nc.dram_tensor("xn3", (NT, P, D), F32).ap()
    ybuf = nc.dram_tensor("ybuf", (E * CAP + 1, D), F32).ap()
    with ExitStack() as ctx:
        ident, logits = [ctx.enter_context(nc.sbuf_tensor(*a)) for a in (("ident", [P, P], F32), ("logits", [P, NT, E], F32))]
        with nc.sbuf_tensor("stage", [P, 3 * C * D], F32) as stage, nc.semaphore("ld_wq") as ld_q, \
                nc.semaphore("ld_wk") as ld_k, nc.semaphore("ld_wv") as ld_v:
            w_w = (ld_q, ld_k, ld_v)

            def prefetch(sp):
                for i, w in enumerate((wq, wk, wv)):
                    sp.dma_start(stage[:, i * C * D:(i + 1) * C * D].rearrange("p (c d) -> p c d", c=C),
                                 w.rearrange("(c p) d -> p c d", p=P)).then_inc(w_w[i], 16)

            self_attention(nc, consts, ident, prefetch, tiles(x), w_qkv, w_out, b_out, x1)
            cross_attention(nc, ident, stage, w_w, tiles(context), w_router, x1, x2, xn3, logits)
            with nc.Block() as block:
                @block.sync
                def _(sp):
                    for s in w_w:
                        sp.sem_clear(s)
        slot, weight, token = [ctx.enter_context(nc.sbuf_tensor(*a)) for a in (
            ("slot", [P, NT * TOPK], I32), ("weight", [P, NT * TOPK], F32), ("token", [P, E * CT], I32))]
        route(nc, consts, logits, slot, weight, token, ybuf)
        experts(nc, ident, token, xn3.rearrange("n p d -> (n p) d"), w_gate, w_up, w_down, ybuf)
        combine(nc, slot, weight, x2, ybuf, tiles(out))


def constants():
    import numpy as np

    i = np.arange(P)
    k = np.zeros((P, K_COLS), np.float32)
    k[:, K_IDENT:K_IDENT + P] = np.eye(P)
    k[:, K_TRI:K_TRI + P] = i[:, None] < i[None, :]
    own = np.where(i[None, :] <= i[:, None], 0.0, MASKED)
    past = np.where(i[None, :] >= i[:, None], 0.0, MASKED)
    none = np.full((P, P), MASKED)
    for n, pair in enumerate(((own, past), (past, own), (own, none))):
        k[:, K_MASK + n * 2 * P:K_MASK + (n + 1) * 2 * P] = np.concatenate(pair, 1)
    inv_freq = (1.0 / np.float32(10000.0) ** (np.arange(0, D1, 2, dtype=np.float32) / np.float32(D1))).astype(np.float32)
    angles = np.repeat(np.arange(S, dtype=np.float32)[:, None] * inv_freq[None, :], 2, axis=-1)
    sign = np.where(np.arange(D1) % 2 == 0, -1.0, 1.0)
    cos, sin = np.cos(angles), np.sin(angles) * sign
    scale = D1 ** -0.5
    for n, table in enumerate((cos * scale, sin * scale, cos, sin)):
        at = K_ROPE + n * T * D1
        k[:, at:at + T * D1] = table.reshape(T, P, D1).transpose(1, 0, 2).reshape(P, T * D1)
    k[:, K_IOTA:K_IOTA + P] = np.arange(P)
    k[:, K_TOK:K_TOK + NT] = i[:, None] + P * np.arange(NT)
    return k


_INS = ["x", "ctx_2048", "L0_attn_W_qkv", "L0_attn_W_out", "L0_attn_b_out", "L0_xattn_Wq", "L0_xattn_Wk", "L0_xattn_Wv",
        "L0_ffn_router_weight", "L0_ffn_gate_proj", "L0_ffn_up_proj", "L0_ffn_down_proj"]


def kernel(**inputs):
    import numpy as np
    import concourse.bacc as bacc
    from concourse.bass_utils import run_bass_kernel_spmd

    nc = bacc.Bacc("TRN2", target_bir_lowering=False, num_devices=1)
    arrays, args = {"consts_dram": constants()}, []
    for name in _INS:
        arrays[f"in_{name}_dram"] = np.ascontiguousarray(inputs[name])
    for name, a in arrays.items():
        args.append(nc.dram_tensor(name, a.shape, mybir.dt.from_np(a.dtype), kind="ExternalInput").ap())
    out = nc.dram_tensor("out_0_dram", (B, S, D), F32, kind="ExternalOutput").ap()
    decoder_layer(nc, *args, out)
    r = run_bass_kernel_spmd(nc, [arrays], core_ids=[0])
    return r.results[0]["out_0_dram"]
```
